# Optimizing a Trainium2 kernel written in Bass

```python
import numpy as np
import jax
import jax.numpy as jnp

def _softmax(x, axis=-1):
    return jax.nn.softmax(x, axis=axis)

def _gelu(x):
    return jax.nn.gelu(x, approximate=True)

def _silu(x):
    return jax.nn.silu(x)

def _sigmoid(x):
    return jax.nn.sigmoid(x)

def _layernorm(x, axis=-1, eps=1e-05):
    m = jnp.mean(x, axis=axis, keepdims=True)
    v = jnp.var(x, axis=axis, keepdims=True)
    return (x - m) / jnp.sqrt(v + eps)

def _scatter_add(tgt, idx, src, axis=0):
    return tgt.at[idx].add(src)

def _segment_sum(src, seg, n):
    return jax.ops.segment_sum(src, seg, n)
kernel_name = 'mk_adaln_d1_jaxref_r8_86e2e6'

def setup_inputs(seed: int=0):
    np.random.seed(seed)
    _w = jnp.asarray

    def _L0_attn_setup():
        import jax, jax.numpy as jnp
        import numpy as np
        B, T, C = (4, 512, 128)
        LN_EPS = 1e-05

        def _ln(x, g, b):
            m = x.mean(-1, keepdims=True)
            v = ((x - m) ** 2).mean(-1, keepdims=True)
            return (x - m) / jnp.sqrt(v + LN_EPS) * g + b

        def _shift(x, time_shift):
            b = x.shape[0]
            return jnp.concatenate([jnp.broadcast_to(time_shift, (b, 1, x.shape[2])), x[:, :-1]], axis=1)

        def _wkv(w, u, k, v):
            b, t, c = k.shape
            aa0 = jnp.zeros((b, c), k.dtype)
            bb0 = jnp.ones((b, c), k.dtype)
            pp0 = jnp.full((b, c), -1e+38, k.dtype)

            def step(carry, kv_t):
                aa, bb, pp = carry
                kk, vv = kv_t
                uu_kk = u + kk
                p = jnp.maximum(pp, uu_kk)
                e1 = jnp.exp(pp - p)
                e2 = jnp.exp(uu_kk - p)
                y = (e1 * aa + e2 * vv) / (e1 * bb + e2)
                ww_kk = w + kk
                pu = jnp.maximum(pp + w, ww_kk)
                e1u = jnp.exp(pp + w - pu)
                e2u = jnp.exp(ww_kk - pu)
                aa_n = e1u * aa + e2u * vv
                bb_n = e1u * bb + e2u
                pp_n = pu + jnp.log(bb_n)
                return ((aa_n, bb_n, pp_n), y)
            _, ys = jax.lax.scan(step, (aa0, bb0, pp0), (k.transpose(1, 0, 2), v.transpose(1, 0, 2)))
            return ys.transpose(1, 0, 2)
        key = jax.random.key(seed)
        ks = jax.random.split(key, 10)
        s1 = 1.0 / np.sqrt(C)
        s4 = 1.0 / np.sqrt(4 * C)
        return {'x': jax.random.normal(ks[0], (B, T, C), jnp.float32), 'time_decay': jax.random.normal(ks[1], (C,), jnp.float32), 'time_first': jax.random.normal(ks[2], (C,), jnp.float32), 'time_shift': jnp.zeros((1, 1, C), jnp.float32), 'Wk': jax.random.normal(ks[3], (C, C), jnp.float32) * s1, 'Wv': jax.random.normal(ks[4], (C, C), jnp.float32) * s1, 'Wr': jax.random.normal(ks[5], (C, C), jnp.float32) * s1, 'Wck': jax.random.normal(ks[6], (C, 4 * C), jnp.float32) * s1, 'Wcv': jax.random.normal(ks[7], (4 * C, C), jnp.float32) * s4, 'Wcr': jax.random.normal(ks[8], (C, C), jnp.float32) * s1, 'ln1_g': jnp.ones((C,), jnp.float32), 'ln1_b': jnp.zeros((C,), jnp.float32), 'ln2_g': jnp.ones((C,), jnp.float32), 'ln2_b': jnp.zeros((C,), jnp.float32)}
    _L0_attn_in = _L0_attn_setup()

    def _L0_ffn_setup():
        import jax, jax.numpy as jnp
        import numpy as np
        B, S, D = (4, 256, 128)
        E, H, TOP_K = (8, 256, 2)
        key = jax.random.key(seed)
        k_x, k_g, k_w1, k_w2, k_w3 = jax.random.split(key, 5)
        s_d = 1.0 / np.sqrt(D)
        s_h = 1.0 / np.sqrt(H)
        return {'x': jax.random.normal(k_x, (B, S, D), dtype=jnp.float32), 'w_gate': jax.random.normal(k_g, (D, E), dtype=jnp.float32) * s_d, 'w1': jax.random.normal(k_w1, (E, D, H), dtype=jnp.float32) * s_d, 'w3': jax.random.normal(k_w3, (E, D, H), dtype=jnp.float32) * s_d, 'w2': jax.random.normal(k_w2, (E, H, D), dtype=jnp.float32) * s_h}
    _L0_ffn_in = _L0_ffn_setup()
    _L0_c = _w((lambda *s: np.random.randn(*s).astype(np.float32) * 0.05)(8, 128))
    _L0_wmod = _w((lambda *s: np.random.randn(*s).astype(np.float32) * 0.05)(128, 6 * 128) * 128 ** (-0.5))
    _d = {'L0_attn_x': _L0_attn_in['x'], 'L0_attn_time_decay': _L0_attn_in['time_decay'], 'L0_attn_time_first': _L0_attn_in['time_first'], 'L0_attn_time_shift': _L0_attn_in['time_shift'], 'L0_attn_Wk': _L0_attn_in['Wk'], 'L0_attn_Wv': _L0_attn_in['Wv'], 'L0_attn_Wr': _L0_attn_in['Wr'], 'L0_attn_Wck': _L0_attn_in['Wck'], 'L0_attn_Wcv': _L0_attn_in['Wcv'], 'L0_attn_Wcr': _L0_attn_in['Wcr'], 'L0_attn_ln1_g': _L0_attn_in['ln1_g'], 'L0_attn_ln1_b': _L0_attn_in['ln1_b'], 'L0_attn_ln2_g': _L0_attn_in['ln2_g'], 'L0_attn_ln2_b': _L0_attn_in['ln2_b'], 'L0_ffn_w_gate': _L0_ffn_in['w_gate'], 'L0_ffn_w1': _L0_ffn_in['w1'], 'L0_ffn_w3': _L0_ffn_in['w3'], 'L0_ffn_w2': _L0_ffn_in['w2'], 'L0_c': _L0_c, 'L0_wmod': _L0_wmod}
    _x0 = _d['L0_attn_x']
    _d['L0_attn_x'] = jax.random.normal(jax.random.fold_in(jax.random.key(seed), 1), (8, 256, 128), dtype=_x0.dtype)
    del _x0
    return _d

def reference(L0_attn_x, L0_attn_time_decay, L0_attn_time_first, L0_attn_time_shift, L0_attn_Wk, L0_attn_Wv, L0_attn_Wr, L0_attn_Wck, L0_attn_Wcv, L0_attn_Wcr, L0_attn_ln1_g, L0_attn_ln1_b, L0_attn_ln2_g, L0_attn_ln2_b, L0_ffn_w_gate, L0_ffn_w1, L0_ffn_w3, L0_ffn_w2, L0_c, L0_wmod):

    def _L0_attn_ref(x, time_decay, time_first, time_shift, Wk, Wv, Wr, Wck, Wcv, Wcr, ln1_g, ln1_b, ln2_g, ln2_b):
        import jax, jax.numpy as jnp
        import numpy as np
        B, T, C = (4, 512, 128)
        LN_EPS = 1e-05

        def _ln(x, g, b):
            m = x.mean(-1, keepdims=True)
            v = ((x - m) ** 2).mean(-1, keepdims=True)
            return (x - m) / jnp.sqrt(v + LN_EPS) * g + b

        def _shift(x, time_shift):
            b = x.shape[0]
            return jnp.concatenate([jnp.broadcast_to(time_shift, (b, 1, x.shape[2])), x[:, :-1]], axis=1)

        def _wkv(w, u, k, v):
            b, t, c = k.shape
            aa0 = jnp.zeros((b, c), k.dtype)
            bb0 = jnp.ones((b, c), k.dtype)
            pp0 = jnp.full((b, c), -1e+38, k.dtype)

            def step(carry, kv_t):
                aa, bb, pp = carry
                kk, vv = kv_t
                uu_kk = u + kk
                p = jnp.maximum(pp, uu_kk)
                e1 = jnp.exp(pp - p)
                e2 = jnp.exp(uu_kk - p)
                y = (e1 * aa + e2 * vv) / (e1 * bb + e2)
                ww_kk = w + kk
                pu = jnp.maximum(pp + w, ww_kk)
                e1u = jnp.exp(pp + w - pu)
                e2u = jnp.exp(ww_kk - pu)
                aa_n = e1u * aa + e2u * vv
                bb_n = e1u * bb + e2u
                pp_n = pu + jnp.log(bb_n)
                return ((aa_n, bb_n, pp_n), y)
            _, ys = jax.lax.scan(step, (aa0, bb0, pp0), (k.transpose(1, 0, 2), v.transpose(1, 0, 2)))
            return ys.transpose(1, 0, 2)
        h = _ln(x, ln1_g, ln1_b)
        hs = _shift(h, time_shift)
        k = hs @ Wk
        v = hs @ Wv
        r = hs @ Wr
        y = _wkv(time_decay, time_first, k, v)
        x = x + jax.nn.sigmoid(r) * y
        h2 = _ln(x, ln2_g, ln2_b)
        h2s = _shift(h2, time_shift)
        kk = jnp.square(jax.nn.relu(h2s @ Wck))
        kv = kk @ Wcv
        rr = jax.nn.sigmoid(h2s @ Wcr)
        x = x + rr * kv
        return x

    def _L0_ffn_ref(x, w_gate, w1, w3, w2):
        import jax, jax.numpy as jnp
        import numpy as np
        B, S, D = (4, 256, 128)
        E, H, TOP_K = (8, 256, 2)
        bsz, seq_len, embed_dim = x.shape
        xt = x.reshape(-1, embed_dim)
        T = xt.shape[0]
        logits = xt @ w_gate
        top_logits, sel = jax.lax.top_k(logits, TOP_K)
        probs = jax.nn.softmax(top_logits, axis=-1).astype(x.dtype)
        h = jax.nn.silu(jnp.einsum('td,edh->eth', xt, w1)) * jnp.einsum('td,edh->eth', xt, w3)
        y = jnp.einsum('eth,ehd->etd', h, w2)
        t_idx = jnp.arange(T)
        yk = y[sel.T, t_idx[None, :], :]
        out = jnp.einsum('ktd,tk->td', yk, probs)
        return out.reshape(bsz, seq_len, embed_dim)
    x = L0_attn_x
    mod = (_silu(L0_c) @ L0_wmod).reshape(L0_c.shape[0], 6, 1, -1)
    sa, ca, ga, sb, cb, gb = (mod[:, 0], mod[:, 1], mod[:, 2], mod[:, 3], mod[:, 4], mod[:, 5])
    ga = (2 * (ga >= 0) - 1) * jnp.maximum(jnp.abs(ga), 0.25)
    gb = (2 * (gb >= 0) - 1) * jnp.maximum(jnp.abs(gb), 0.25)
    h = _layernorm(x, axis=-1) * (1 + ca) + sa
    x = x + ga * _L0_attn_ref(h, L0_attn_time_decay, L0_attn_time_first, L0_attn_time_shift, L0_attn_Wk, L0_attn_Wv, L0_attn_Wr, L0_attn_Wck, L0_attn_Wcv, L0_attn_Wcr, L0_attn_ln1_g, L0_attn_ln1_b, L0_attn_ln2_g, L0_attn_ln2_b)
    h = _layernorm(x, axis=-1) * (1 + cb) + sb
    x = x + gb * _L0_ffn_ref(h, L0_ffn_w_gate, L0_ffn_w1, L0_ffn_w3, L0_ffn_w2)
    return x

_drawn_inputs = setup_inputs


def setup_inputs(seed=0):
    import zlib

    import numpy as np

    out = dict(_drawn_inputs(seed))
    spreads = {'L0_attn_time_shift': (0.0, 0.753),
     'L0_attn_ln1_g': (1.0, 0.2),
     'L0_attn_ln1_b': (0.0, 0.449),
     'L0_attn_ln2_g': (1.0, 0.2),
     'L0_attn_ln2_b': (0.0, 0.29)}
    factors = {'L0_attn_time_first': 3.826}
    for name, (base, spread) in spreads.items():
        noise = np.random.default_rng([zlib.crc32(name.encode()), seed]).standard_normal(out[name].shape)
        drawn = base * np.exp(spread * noise) if base else spread * noise
        out[name] = jnp.asarray(drawn.astype(out[name].dtype))
    for name, factor in factors.items():
        out[name] = (out[name] * factor).astype(out[name].dtype)
    return out
```

```python
from contextlib import ExitStack

import concourse.bass as bass
from concourse import mybir

F32 = mybir.dt.float32
I32 = mybir.dt.int32
U32 = mybir.dt.uint32
ALU = mybir.AluOpType
ACT = mybir.ActivationFunctionType
AX_X = mybir.AxisListType.X
RMAX = bass.bass_isa.ReduceOp.max

P = 128
LN_EPS = 1e-5
MIN_GATE = 0.25
PP_START = -1e38
R_CAP = 2.0 ** 60
K_SAFE = 12.0
W_SAFE = 16.0


class Steps:

    def __init__(self, sem, names):
        self.sem, self.per = sem, len(names)
        self.at = {n: i + 1 for i, n in enumerate(names)}
        self.now = 0

    def value(self, group, name):
        return group * self.per + self.at[name]

    def step(self, name):
        assert self.at[name] == self.now % self.per + 1, name
        self.now += 1
        return 1


def first(g):
    return isinstance(g, int) and g == 0


def adaln_rwkv_moe(nc, x, time_decay, time_first, time_shift, Wk, Wv, Wr, Wck, Wcv, Wcr,
                   ln1_g, ln1_b, ln2_g, ln2_b, w_gate, w1, w3, w2, c, wmod, out):
    B, T, C = x.shape
    E, _, HID = w1.shape
    assert C == P and P % B == 0
    TS = P // B
    NT = T // TS
    GT = 2
    NG = NT // GT
    GS = GT * TS
    GN = GT * P
    N = B * T
    QT = 4
    NQ = NT // QT
    QN = QT * P
    FM = Wck.shape[1] // P
    HM = HID // P
    STEPS_OF_SLOT = [0, 5, 5, 5, 5, 4, 4, 4]
    assert sum(STEPS_OF_SLOT) == GS and len(STEPS_OF_SLOT) == E

    with ExitStack() as ctx:
        def sb(name, shape, dt=F32):
            return ctx.enter_context(nc.sbuf_tensor(name, shape, dt))

        def pb(name):
            return ctx.enter_context(nc.psum_tensor(name, [P, 512], F32))

        def sem(name):
            return ctx.enter_context(nc.semaphore(name))

        def steps(name, names):
            return Steps(sem(name), names)

        X = sb("X", [P, NT, C])
        H = sb("H", [P, NT, C])
        HSh = sb("HSh", [P, B + N])
        K = sb("K", [P, N])
        V = sb("V", [P, N])
        SR = sb("SR", [P, N])
        Q = sb("Q", [P, N])
        YS = sb("YS", [P, N])
        H3T = sb("H3T", [P, N])
        W1 = sb("W1", [P, E, HID])
        W3 = sb("W3", [P, E, HID])
        W2 = sb("W2", [P, E, HM, C])
        WK = sb("WK", [P, C])
        WV = sb("WV", [P, C])
        WR = sb("WR", [P, C])
        WCK = sb("WCK", [P, FM * P])
        WCV = sb("WCV", [P, FM, C])
        WCR = sb("WCR", [P, C])
        WG = sb("WG", [P, E])
        WMOD = sb("WMOD", [P, 6 * C])
        CB = sb("CB", [P, C])
        CS = sb("CS", [P, C])
        CT = sb("CT", [P, P])
        MOD = sb("MOD", [P, 6, C])
        GSG = sb("GSG", [P, 2, C])
        GAB = sb("GAB", [P, 2, C])
        VEC = sb("VEC", [P, 8])
        w_v, u_v, g1_v, b1_v, g2_v, b2_v, sh_v = (VEC[:, i:i + 1] for i in range(7))
        UE = sb("UE", [P, 2])
        ident = sb("ident", [P, P])
        zero = sb("zero", [P, P])
        NHALF = sb("NHALF", [P, QT])
        IOTA = sb("IOTA", [P, E])
        STAT = sb("STAT", [P, 2, QT, 6])
        MV = sb("MV", [P, 2, QT, 2])
        VE = sb("VE", [P, 2, QT])
        RS = sb("RS", [P, 2, QT])
        XN = sb("XN", [P, QT, C])
        HN = sb("HN", [P, QT, C])
        KM = sb("KM", [P, 6])
        KMM = sb("KMM", [P, 1])
        KMA = sb("KMA", [P, 1])
        FLAG = sb("FLAG", [P, 1], I32)
        REC = sb("REC", [P, GS + 1, 6, B])
        RQ, RG, RR_, RBB, RU, RINV = range(6)
        F1 = sb("F1", [P, GS, B])
        F2 = sb("F2", [P, GS, B])
        F2V = sb("F2V", [P, GS, B])
        E1 = sb("E1", [P, GS, B])
        E2 = sb("E2", [P, GS, B])
        EB = sb("EB", [P, GS, B])
        EAA = sb("EAA", [P, GS, B])
        E2V = sb("E2V", [P, GS, B])
        DEN = sb("DEN", [P, GS, B])
        NUM = sb("NUM", [P, GS, B])
        RDEN = sb("RDEN", [P, GS, B])
        YY = sb("YY", [P, GN])
        AA = sb("AA", [P, GS + 1, B])
        ATT = sb("ATT", [P, GN])
        X1 = sb("X1", [P, GT, C])
        X2N = sb("X2N", [P, GT, C])
        HS2 = sb("HS2", [P, B + GN])
        RRT = sb("RRT", [P, GN])
        KR = sb("KR", [P, FM * GN])
        KQ = sb("KQ", [P, FM, GN])
        T1 = sb("T1", [P, GT, C])
        XA = sb("XA", [P, GT, C])
        XG = sb("XG", [P, GT, C])
        N3 = sb("N3", [P, GT, C])
        HC = sb("HC", [P, GT, C])
        H3 = sb("H3", [P, GT, C])
        H3S = sb("H3S", [P, GN])
        LG = sb("LG", [P, GT, E])
        MX = sb("MX", [P, GT, 8])
        IX = sb("IX", [P, GT, 8], U32)
        IXF = sb("IXF", [P, GT, 2])
        DF = sb("DF", [P, GT])
        TH = sb("TH", [P, GT])
        PR = sb("PR", [P, GT, 2])
        WA = sb("WA", [P, 2, GT, E])
        WT = sb("WT", [P, GT, E])
        WE = sb("WE", [P, GT, E])
        SL = sb("SL", [P, 2, HM * GN])
        HT = sb("HT", [P, 2, HM, GN])
        YW = sb("YW", [P, 2, GT, C])
        ACC = sb("ACC", [P, GT, C])
        OG = sb("OG", [P, GT, C])
        OUT = sb("OUT", [P, GT, C])
        sPP = sb("sPP", [P, B])
        sAA = sb("sAA", [P, B])
        sBB = sb("sBB", [P, B])
        sM = sb("sM", [P, B])
        sP = sb("sP", [P, B])
        sD = sb("sD", [P, 4, B])
        sE = sb("sE", [P, 4, B])
        sT = sb("sT", [P, 9, B])
        sL = sb("sL", [P, B])

        pH1 = [pb("pH1a"), pb("pH1b")]
        pH3 = [pb("pH3a"), pb("pH3b")]
        pY = pb("pY")
        pA, pB, pC = pb("pA"), pb("pB"), pb("pC")

        x_first, x_rest = sem("x_first"), sem("x_rest")
        vec_in, c_in, wmod_in, wkvr_in = sem("vec_in"), sem("c_in"), sem("wmod_in"), sem("wkvr_in")
        mix_in, w1_in, w3_in, w2_in = sem("mix_in"), sem("w1_in"), sem("w3_in"), sem("w2_in")
        stored = sem("stored")
        pool_const = steps("pool_const", ["zero", "ident", "rest"])
        mod_act = steps("mod_act", ["silu", "ct"])
        mod_pe = steps("mod_pe", ["ct", "mod"])
        mod_dve = steps("mod_dve", ["copy0", "copy1", "ca", "cb", "sign", "abs", "size", "gate"])
        ln_dve = steps("ln_dve", [("st", n) for n in range(QT)] + [("ag", n) for n in range(QT)] + ["eps"]
                       + [("n", n) for n in range(QT)] + ["scaled", "h"]
                       + [("st2", n) for n in range(QT)] + [("ag2", n) for n in range(QT)] + ["eps2"]
                       + [("n2", n) for n in range(QT)])
        ln_pool = steps("ln_pool", ["rs", "rs2"])
        ln_pe = steps("ln_pe", ["t", "k", "v", "r"])
        ln_act = steps("ln_act", ["hs", "abs_k", "k", "v", "r"])
        shift_set = sem("shift_set")
        dk_dve = steps("dk_dve", ["dk", "clip", "km", "wu", "um", "max", "flag"])
        q_act = steps("q_act", ["u", "iu", "q"])
        kmax_all = sem("kmax_all")
        wkv = steps("wkv", ["q", "carry"] + [(n, s) for s in range(GS) for n in ("rb", "u", "inv", "g")])
        wkv_start = steps("wkv_start", ["z", "g", "bb", "inv", "aa"])
        y_dve = steps("y_dve", ["f1", "f2", "f2v"] + [("aa", b) for b in range(B)]
                      + ["e1", "e2", "eb", "ea", "carry", "num", "rden", "y", "att"])
        y_pool = steps("y_pool", ["e2v", "den"])
        a_pe = steps("a_pe", ["t_att", "t_x2", "rr", "kk0", "kk1", "kv", "t_h3", "logits"])
        a_dve = steps("a_dve", ["x1", ("st", 0), ("st", 1), ("ag", 0), ("ag", 1), "eps", ("n", 0), ("n", 1),
                                "t1", "xa", ("st3", 0), ("st3", 1), ("ag3", 0), ("ag3", 1), "eps3",
                                ("n3", 0), ("n3", 1),
                                "lg", ("mx", 0), ("mx", 1), ("ix", 0), ("ix", 1), "df", "ixf", "p1", "p2",
                                ("w", 0, 0), ("w", 0, 1), ("w", 1, 0), ("w", 1, 1), "wt"])
        a_pool = steps("a_pool", ["rs", "xg", "xr", "rs3", "hc", "h3"])
        a_act = steps("a_act", ["carry", "hs2", "rr", "re0", "sq0", "re1", "sq1", "h3s", "h3t", "th"])
        e_order = ["h0", "h1", "y0"] + [f"{n}{e + d}" for e in range(1, E - 1) for n, d in (("h", 1), ("y", 0))] \
            + [f"y{E - 1}"]
        e_pe = steps("e_pe", e_order)
        act_order = [n for o in e_order for n in ([f"s{o[1:]}"] if o[0] == "h" else [f"w{o[1:]}.{t}" for t in range(GT)])]
        e_act = steps("e_act", act_order)
        e_dve = steps("e_dve", ["we"] + [f"m{e}" for e in range(E)])
        e_pool = steps("e_pool", [f"a{e}" for e in range(1, E)] + ["og", "out"])
        passed = sem("passed")
        slow_dve, slow_act, slow_copy = sem("slow_dve"), sem("slow_act"), sem("slow_copy")

        x_tok = x.rearrange("b (j s) c -> s b j c", s=TS)
        out_tok = out.rearrange("b (j s) c -> s b j c", s=TS)

        def row(v):
            return v.rearrange("(p o) -> p o", o=1)

        def cols(g, n=GN):
            return bass.ds(g * n, n)

        def ranks(g):
            return bass.ds(g * GT, GT)

        def tile3(ap):
            return ap.rearrange("p (t b) -> p t b", b=B)

        block = ctx.enter_context(nc.Block())

        @block.sync
        def _(sp):
            for n in range(QT):
                sp.dma_start(X[:, n, :], x_tok[:, :, n, :]).then_inc(x_first, 16)
            for i, v in enumerate((row(time_decay), row(time_first), row(ln1_g), row(ln1_b), row(ln2_g), row(ln2_b),
                                   time_shift.rearrange("a b c -> c (a b)"))):
                sp.dma_start(VEC[:, i:i + 1], v).then_inc(vec_in, 16)
            for n in range(QT, NT):
                sp.dma_start(X[:, n, :], x_tok[:, :, n, :]).then_inc(x_rest, 16)
            sp.dma_start(W1[:], w1.rearrange("e d h -> d e h")).then_inc(w1_in, 16)
            sp.dma_start(W3[:], w3.rearrange("e d h -> d e h")).then_inc(w3_in, 16)
            sp.dma_start(W2[:], w2.rearrange("e (m p) d -> p e m d", p=P)).then_inc(w2_in, 16)
            with sp.Fori(0, NG) as g:
                sp.wait_ge(e_pool.sem, e_pool.value(g, "out"))
                for n in range(GT):
                    to = out_tok[:, :, bass.ds(g * GT + n, 1), :].rearrange("s b o c -> s b (o c)")
                    sp.dma_start(to, OUT[:, n, :]).then_inc(stored, 16)
            sp.wait_ge(stored, 16 * NT)

        @block.gpsimd
        def _(pool):
            pool.memset(zero[:], 0.0).then_inc(pool_const.sem, pool_const.step("zero"))
            pool.wait_ge(pool_const.sem, pool_const.value(0, "zero"))
            pool.affine_select(out=ident[:], in_=zero[:], compare_op=ALU.not_equal, fill=1.0, base=0,
                                               pattern=[[-1, P]], channel_multiplier=1).then_inc(pool_const.sem, pool_const.step("ident"))
            for e in range(E):
                pool.memset(IOTA[:, e:e + 1], float(e))
            pool.memset(Q[:, N - B:N], 1.0)
            pool.memset(NHALF[:], -0.5).then_inc(pool_const.sem, pool_const.step("rest"))
            pool.wait_ge(pool_const.sem, pool_const.value(0, "rest"))

            def first_stage(q):
                for k, (eps, rs) in enumerate((("eps", "rs"), ("eps2", "rs2"))):
                    pool.wait_ge(ln_dve.sem, ln_dve.value(q, eps))
                    pool.tensor_tensor(RS[:, k, :], VE[:, k, :], NHALF[:], ALU.pow).then_inc(ln_pool.sem, ln_pool.step(rs))

            first_stage(0)
            with pool.Fori(1, NQ) as q:
                first_stage(q)
            pool.wait_ge(dk_dve.sem, dk_dve.value(0, "max"))
            pool.partition_all_reduce(KMA[:], KMM[:], P, RMAX).then_inc(kmax_all, 1)

            def y_part(g):
                if not first(g):
                    pool.wait_ge(y_dve.sem, y_dve.value(g - 1, "rden"))
                pool.wait_ge(y_dve.sem, y_dve.value(g, "e2"))
                pool.tensor_tensor(E2V[:], E2[:], tile3(V[:, cols(g)]), ALU.mult).then_inc(y_pool.sem, y_pool.step("e2v"))
                pool.wait_ge(y_dve.sem, y_dve.value(g, "eb"))
                pool.tensor_tensor(DEN[:], EB[:], E2[:], ALU.add).then_inc(y_pool.sem, y_pool.step("den"))

            def a_ln2(g):
                pool.wait_ge(a_dve.sem, a_dve.value(g, "eps"))
                pool.tensor_tensor(RS[:, 0, 0:GT], VE[:, 0, 0:GT], NHALF[:, 0:GT], ALU.pow).then_inc(a_pool.sem, a_pool.step("rs"))

            def a_residual(g):
                pool.wait_ge(a_dve.sem, a_dve.value(g, "xa"))
                pool.tensor_tensor(XG[:], XA[:], gate_rows(0), ALU.mult).then_inc(a_pool.sem, a_pool.step("xg"))
                pool.wait_ge(a_pool.sem, a_pool.value(g, "xg"))
                pool.tensor_tensor(X[:, ranks(g), :], XG[:], X[:, ranks(g), :], ALU.add).then_inc(a_pool.sem, a_pool.step("xr"))

            def a_ln3(g):
                pool.wait_ge(a_dve.sem, a_dve.value(g, "eps3"))
                pool.tensor_tensor(RS[:, 1, 0:GT], VE[:, 1, 0:GT], NHALF[:, 0:GT], ALU.pow).then_inc(a_pool.sem, a_pool.step("rs3"))

            def a_h3(g):
                if not first(g):
                    pool.wait_ge(a_pe.sem, a_pe.value(g - 1, "t_h3"))
                pool.wait_ge(a_dve.sem, a_dve.value(g, ("n3", 1)))
                pool.tensor_tensor(HC[:], N3[:], mod_rows(4), ALU.mult).then_inc(a_pool.sem, a_pool.step("hc"))
                pool.wait_ge(a_pool.sem, a_pool.value(g, "hc"))
                pool.tensor_tensor(H3[:], HC[:], mod_rows(3), ALU.add).then_inc(a_pool.sem, a_pool.step("h3"))

            def accumulate(g, e):
                pool.wait_ge(e_act.sem, e_act.value(g, f"w{e}.{GT - 1}"))
                if e == 1:
                    if not first(g):
                        pool.wait_ge(e_pool.sem, e_pool.value(g - 1, "og"))
                    pool.tensor_tensor(ACC[:], YW[:, 0], YW[:, 1], ALU.add).then_inc(e_pool.sem, e_pool.step("a1"))
                else:
                    pool.wait_ge(e_pool.sem, e_pool.value(g, f"a{e - 1}"))
                    pool.tensor_tensor(ACC[:], ACC[:], YW[:, e % 2], ALU.add).then_inc(e_pool.sem, e_pool.step(f"a{e}"))

            def finish(g):
                pool.wait_ge(e_pool.sem, e_pool.value(g, f"a{E - 1}"))
                pool.tensor_tensor(OG[:], ACC[:], gate_rows(1), ALU.mult).then_inc(e_pool.sem, e_pool.step("og"))
                pool.wait_ge(e_pool.sem, e_pool.value(g, "og"))
                if not first(g):
                    pool.wait_ge(stored, g * (16 * GT))
                pool.tensor_tensor(OUT[:], OG[:], X[:, ranks(g), :], ALU.add).then_inc(e_pool.sem, e_pool.step("out"))

            def mod_rows(k):
                return MOD[:, k:k + 1, :].broadcast_to((P, GT, C))

            def gate_rows(k):
                return GAB[:, k:k + 1, :].broadcast_to((P, GT, C))

            def turn(ya, e_g):
                if ya is not None:
                    y_part(ya)
                for e in range(E):
                    if e_g is not None and e >= 2:
                        accumulate(e_g, e - 1)
                    if ya is not None:
                        if e == 1:
                            a_ln2(ya)
                        if e == 4:
                            a_residual(ya)
                        if e == 5:
                            a_ln3(ya)
                        if e == 6:
                            a_h3(ya)
                if e_g is not None:
                    accumulate(e_g, E - 1)
                    finish(e_g)

            turn(0, None)
            turn(1, 0)
            with pool.Fori(1, NG - 1) as g:
                turn(g + 1, g)
            turn(None, NG - 1)

        @block.scalar
        def _(act):
            act.dma_start(CB[:], c.rearrange("(o b) k -> o b k", o=1).broadcast_to((TS, B, C))).then_inc(c_in, 16)
            act.dma_start(WMOD[:], wmod).then_inc(wmod_in, 16)
            for dst, src in ((WK, Wk), (WV, Wv), (WR, Wr)):
                act.dma_start(dst[:], src).then_inc(wkvr_in, 16)
            act.dma_start(WCK[:], Wck).then_inc(mix_in, 16)
            act.dma_start(WCV[:], Wcv.rearrange("(m p) d -> p m d", p=P)).then_inc(mix_in, 16)
            act.dma_start(WCR[:], Wcr).then_inc(mix_in, 16)
            act.dma_start(WG[:], w_gate).then_inc(mix_in, 16)

            act.wait_ge(c_in, 16)
            act.activation(CS[:], CB[:], ACT.Silu).then_inc(mod_act.sem, mod_act.step("silu"))
            act.wait_ge(mod_pe.sem, mod_pe.value(0, "ct"))
            act.copy(CT[:], pB[:, 0:P]).then_inc(mod_act.sem, mod_act.step("ct"))
            act.wait_ge(vec_in, 16 * 7)
            act.wait_ge(pool_const.sem, pool_const.value(0, "zero"))
            act.activation(HSh[:, 0:B], zero[:, 0:B], ACT.Identity, bias=sh_v).then_inc(shift_set, 1)

            def first_stage(q):
                act.wait_ge(ln_pe.sem, ln_pe.value(q, "t"))
                act.activation(HSh[:, bass.ds(q * QN + B, QN)], pA[:], ACT.Identity, bias=b1_v,
                                           scale=g1_v).then_inc(ln_act.sem, ln_act.step("hs"))
                act.wait_ge(ln_pe.sem, ln_pe.value(q, "k"))
                act.activation(H3T[:, cols(q, QN)], pH1[0][:], ACT.Abs).then_inc(ln_act.sem, ln_act.step("abs_k"))
                act.copy(K[:, cols(q, QN)], pH1[0][:]).then_inc(ln_act.sem, ln_act.step("k"))
                act.wait_ge(ln_pe.sem, ln_pe.value(q, "v"))
                act.copy(V[:, cols(q, QN)], pH3[0][:]).then_inc(ln_act.sem, ln_act.step("v"))
                act.wait_ge(ln_pe.sem, ln_pe.value(q, "r"))
                act.activation(SR[:, cols(q, QN)], pH1[1][:], ACT.Tanh, scale=0.5).then_inc(ln_act.sem, ln_act.step("r"))

            first_stage(0)
            with act.Fori(1, NQ) as q:
                first_stage(q)
            act.activation(UE[:, 0:1], u_v, ACT.Exp).then_inc(q_act.sem, q_act.step("u"))
            act.activation(UE[:, 1:2], u_v, ACT.Exp, scale=-1.0).then_inc(q_act.sem, q_act.step("iu"))
            act.wait_ge(dk_dve.sem, dk_dve.value(0, "clip"))
            act.activation(Q[:, 0:N - B], YS[:, 0:N - B], ACT.Exp, bias=w_v).then_inc(q_act.sem, q_act.step("q"))

            act.wait_ge(dk_dve.sem, dk_dve.value(0, "flag"))
            outside = act.value_load(FLAG[0:1, 0:1])
            with act.If(outside > 0):
                with act.Fori(0, T) as t:
                    act.wait_ge(slow_dve, t * 17 + 7)
                    act.activation(sE[:], sD[:], ACT.Exp).then_inc(slow_act, 1)
                    act.wait_ge(slow_dve, t * 17 + 16)
                    act.activation(sL[:], sBB[:], ACT.Ln).then_inc(slow_act, 1)

            def a_hs2(g):
                if not first(g):
                    act.wait_ge(a_pe.sem, a_pe.value(g - 1, "kk1"))
                    act.copy(HS2[:, 0:B], HS2[:, GN:GN + B]).then_inc(a_act.sem, a_act.step("carry"))
                    act.wait_ge(a_act.sem, a_act.value(g, "carry"))
                else:
                    act.activation(HS2[:, 0:B], zero[:, 0:B], ACT.Identity, bias=sh_v) \
                        .then_inc(a_act.sem, a_act.step("carry"))
                act.wait_ge(a_pe.sem, a_pe.value(g, "t_x2"))
                act.activation(HS2[:, B:B + GN], pA[:, 0:GN], ACT.Identity, bias=b2_v, scale=g2_v).then_inc(a_act.sem, a_act.step("hs2"))

            def a_mix(g):
                act.wait_ge(a_pe.sem, a_pe.value(g, "rr"))
                act.activation(RRT[:], pA[:, 0:GN], ACT.Tanh, scale=0.5).then_inc(a_act.sem, a_act.step("rr"))
                half = FM * GN // 2
                for i, p in enumerate((pB, pC)):
                    act.wait_ge(a_pe.sem, a_pe.value(g, f"kk{i}"))
                    act.activation(KR[:, i * half:(i + 1) * half], p[:], ACT.Relu).then_inc(a_act.sem, a_act.step(f"re{i}"))
                    act.wait_ge(a_act.sem, a_act.value(g, f"re{i}"))
                    kq = KQ[:, i * FM // 2:(i + 1) * FM // 2, :].rearrange("p m n -> p (m n)")
                    act.activation(kq, KR[:, i * half:(i + 1) * half], ACT.Square).then_inc(a_act.sem, a_act.step(f"sq{i}"))

            def a_h3(g):
                act.wait_ge(a_pe.sem, a_pe.value(g, "t_h3"))
                act.copy(H3S[:], pB[:, 0:GN]).then_inc(a_act.sem, a_act.step("h3s"))
                act.copy(H3T[:, cols(g)], pB[:, 0:GN]).then_inc(a_act.sem, a_act.step("h3t"))

            def a_gate(g):
                act.wait_ge(a_dve.sem, a_dve.value(g, "df"))
                act.activation(TH[:], DF[:], ACT.Tanh, scale=0.5).then_inc(a_act.sem, a_act.step("th"))

            def silu(g, e):
                if e >= 2:
                    act.wait_ge(e_dve.sem, e_dve.value(g, f"m{e - 2}"))
                elif not first(g):
                    act.wait_ge(e_dve.sem, e_dve.value(g - 1, f"m{E - 2 + e}"))
                act.wait_ge(e_pe.sem, e_pe.value(g, f"h{e}"))
                act.activation(SL[:, e % 2], pH1[e % 2][:], ACT.Silu).then_inc(e_act.sem, e_act.step(f"s{e}"))

            def weigh(g, e):
                if e >= 2:
                    act.wait_ge(e_pool.sem, e_pool.value(g, f"a{max(e - 2, 1)}"))
                elif not first(g):
                    act.wait_ge(e_pool.sem, e_pool.value(g - 1, f"a{E - 2 + e}"))
                act.wait_ge(e_pe.sem, e_pe.value(g, f"y{e}"))
                if e == 0:
                    act.wait_ge(e_dve.sem, e_dve.value(g, "we"))
                for t in range(GT):
                    act.activation(YW[:, e % 2, t], pY[:, t * C:(t + 1) * C], ACT.Copy,
                                              scale=WE[:, t, e:e + 1]).then_inc(e_act.sem, e_act.step(f"w{e}.{t}"))

            def turn(ya, e_g):
                if e_g is not None:
                    silu(e_g, 0)
                for e in range(E):
                    if e_g is not None:
                        if e + 1 < E:
                            silu(e_g, e + 1)
                        weigh(e_g, e)
                    if ya is not None:
                        if e == 2:
                            a_hs2(ya)
                        if e == 3:
                            a_mix(ya)
                        if e == 6:
                            a_h3(ya)
                        if e == 7:
                            a_gate(ya)

            turn(0, None)
            turn(1, 0)
            with act.Fori(1, NG - 1) as g:
                turn(g + 1, g)
            turn(None, NG - 1)

        @block.vector
        def _(dve):
            def wait_apart(semaphore, value):
                dve.wait_ge(semaphore, value)
                if not isinstance(value, int):
                    dve.sem_inc(passed, 1)

            dve.wait_ge(mod_pe.sem, mod_pe.value(0, "mod"))
            mod2 = MOD[:].rearrange("p k c -> p (k c)")
            dve.tensor_copy(mod2[:, 0:512], pH3[1][:]).then_inc(mod_dve.sem, mod_dve.step("copy0"))
            dve.tensor_copy(mod2[:, 512:768], pY[:, 0:256]).then_inc(mod_dve.sem, mod_dve.step("copy1"))
            dve.wait_ge(mod_dve.sem, mod_dve.value(0, "copy1"))
            dve.tensor_scalar(MOD[:, 1, :], MOD[:, 1, :], 1.0, None, ALU.add).then_inc(mod_dve.sem, mod_dve.step("ca"))
            dve.tensor_scalar(MOD[:, 4, :], MOD[:, 4, :], 1.0, None, ALU.add).then_inc(mod_dve.sem, mod_dve.step("cb"))
            gates = MOD[:].rearrange("p (i k) c -> p i k c", i=2)[:, :, 2, :]
            dve.tensor_scalar(GSG[:], gates, 0.0, 2.0, ALU.is_ge, ALU.mult).then_inc(mod_dve.sem, mod_dve.step("sign"))
            dve.scalar_tensor_tensor(GAB[:], gates, -1.0, gates, ALU.mult, ALU.max).then_inc(mod_dve.sem, mod_dve.step("abs"))
            dve.wait_ge(mod_dve.sem, mod_dve.value(0, "abs"))
            dve.tensor_scalar(GAB[:], GAB[:], MIN_GATE, None, ALU.max).then_inc(mod_dve.sem, mod_dve.step("size"))
            dve.wait_ge(mod_dve.sem, mod_dve.value(0, "size"))
            dve.scalar_tensor_tensor(GAB[:], GSG[:], -1.0, GAB[:], ALU.add, ALU.mult).then_inc(mod_dve.sem, mod_dve.step("gate"))
            dve.wait_ge(pool_const.sem, pool_const.value(0, "rest"))

            def first_stage(q):
                def tiles(n=None):
                    return bass.ds(q * QT, QT) if n is None else bass.ds(q * QT + n, 1)

                def one(t, n):
                    return t[:, tiles(n), :].rearrange("p o c -> p (o c)")

                for n in range(QT):
                    dve.bn_stats(STAT[:, 0, n, :], one(X, n)).then_inc(ln_dve.sem, ln_dve.step(("st", n)))
                for n in range(QT):
                    wait_apart(ln_dve.sem, ln_dve.value(q, ("st", n)))
                    dve.bn_aggr(MV[:, 0, n, :], STAT[:, 0, n, :]).then_inc(ln_dve.sem, ln_dve.step(("ag", n)))
                dve.wait_ge(ln_dve.sem, ln_dve.value(q, ("ag", QT - 1)))
                dve.tensor_scalar(VE[:, 0, :], MV[:, 0, :, 1], LN_EPS, None, ALU.add).then_inc(ln_dve.sem, ln_dve.step("eps"))
                dve.wait_ge(ln_pool.sem, ln_pool.value(q, "rs"))
                for n in range(QT):
                    dve.tensor_scalar(XN[:, n, :], one(X, n), MV[:, 0, n, 0:1], RS[:, 0, n:n + 1],
                                                  ALU.subtract, ALU.mult).then_inc(ln_dve.sem, ln_dve.step(("n", n)))
                dve.wait_ge(ln_dve.sem, ln_dve.value(q, ("n", QT - 1)))
                dve.tensor_tensor(XN[:], XN[:], MOD[:, 1:2, :].broadcast_to((P, QT, C)), ALU.mult).then_inc(ln_dve.sem, ln_dve.step("scaled"))
                dve.wait_ge(ln_dve.sem, ln_dve.value(q, "scaled"))
                dve.tensor_tensor(H[:, tiles(), :], XN[:], MOD[:, 0:1, :].broadcast_to((P, QT, C)),
                                              ALU.add).then_inc(ln_dve.sem, ln_dve.step("h"))
                wait_apart(ln_dve.sem, ln_dve.value(q, "h"))
                for n in range(QT):
                    dve.bn_stats(STAT[:, 1, n, :], one(H, n)).then_inc(ln_dve.sem, ln_dve.step(("st2", n)))
                for n in range(QT):
                    wait_apart(ln_dve.sem, ln_dve.value(q, ("st2", n)))
                    dve.bn_aggr(MV[:, 1, n, :], STAT[:, 1, n, :]).then_inc(ln_dve.sem, ln_dve.step(("ag2", n)))
                dve.wait_ge(ln_dve.sem, ln_dve.value(q, ("ag2", QT - 1)))
                dve.tensor_scalar(VE[:, 1, :], MV[:, 1, :, 1], LN_EPS, None, ALU.add).then_inc(ln_dve.sem, ln_dve.step("eps2"))
                dve.wait_ge(ln_pool.sem, ln_pool.value(q, "rs2"))
                if not first(q):
                    dve.wait_ge(ln_pe.sem, ln_pe.value(q - 1, "t"))
                for n in range(QT):
                    dve.tensor_scalar(HN[:, n, :], one(H, n), MV[:, 1, n, 0:1], RS[:, 1, n:n + 1],
                                                  ALU.subtract, ALU.mult).then_inc(ln_dve.sem, ln_dve.step(("n2", n)))

            dve.wait_ge(x_first, 16 * QT)
            first_stage(0)
            dve.wait_ge(x_rest, 16 * (NT - QT))
            with dve.Fori(1, NQ) as q:
                first_stage(q)

            dve.wait_ge(ln_act.sem, ln_act.value(NQ - 1, "k"))
            dve.wait_ge(vec_in, 16 * 7)
            dve.tensor_tensor(YS[:, 0:N - B], K[:, 0:N - B], K[:, B:N], ALU.subtract).then_inc(dk_dve.sem, dk_dve.step("dk"))
            dve.wait_ge(dk_dve.sem, dk_dve.value(0, "dk"))
            dve.tensor_scalar(YS[:, 0:N - B], YS[:, 0:N - B], -2.0 * K_SAFE, 2.0 * K_SAFE,
                                          ALU.max, ALU.min).then_inc(dk_dve.sem, dk_dve.step("clip"))
            dve.tensor_reduce(KM[:, 0:1], H3T[:], AX_X, ALU.max).then_inc(dk_dve.sem, dk_dve.step("km"))
            dve.scalar_tensor_tensor(KM[:, 4:6], VEC[:, 0:2], -1.0, VEC[:, 0:2], ALU.mult, ALU.max).then_inc(dk_dve.sem, dk_dve.step("wu"))
            dve.wait_ge(dk_dve.sem, dk_dve.value(0, "wu"))
            dve.tensor_scalar(KM[:, 1:3], KM[:, 4:6], K_SAFE / W_SAFE, None, ALU.mult).then_inc(dk_dve.sem, dk_dve.step("um"))
            dve.wait_ge(dk_dve.sem, dk_dve.value(0, "um"))
            dve.tensor_reduce(KMM[:], KM[:, 0:3], AX_X, ALU.max).then_inc(dk_dve.sem, dk_dve.step("max"))
            dve.wait_ge(kmax_all, 1)
            dve.tensor_scalar(FLAG[:], KMA[:], K_SAFE, None, ALU.is_gt).then_inc(dk_dve.sem, dk_dve.step("flag"))

            dve.memset(REC[:, 0, :, :], 0.0).then_inc(wkv_start.sem, wkv_start.step("z"))
            dve.wait_ge(wkv_start.sem, wkv_start.value(0, "z"))
            dve.memset(REC[:, 0, RG, :], 1.0).then_inc(wkv_start.sem, wkv_start.step("g"))
            dve.memset(REC[:, 0, RBB, :], 1.0).then_inc(wkv_start.sem, wkv_start.step("bb"))
            dve.memset(REC[:, 0, RINV, :], 1e30).then_inc(wkv_start.sem, wkv_start.step("inv"))
            dve.memset(AA[:, 0, :], 0.0).then_inc(wkv_start.sem, wkv_start.step("aa"))
            dve.wait_ge(wkv_start.sem, wkv_start.value(0, "aa"))
            dve.wait_ge(q_act.sem, q_act.value(0, "q"))

            def wkv_begin(g):
                if not first(g):
                    dve.wait_ge(wkv.sem, wkv.value(g - 1, ("g", GS - 1)))
                dve.tensor_copy(REC[:, 0:GS, RQ, :], tile3(Q[:, cols(g)])).then_inc(wkv.sem, wkv.step("q"))
                if first(g):
                    dve.tensor_copy(KM[:, 3:4], KM[:, 0:1]).then_inc(wkv.sem, wkv.step("carry"))
                else:
                    dve.tensor_copy(REC[:, 0, RG:, :], REC[:, GS, RG:, :]).then_inc(wkv.sem, wkv.step("carry"))
                dve.wait_ge(wkv.sem, wkv.value(g, "carry"))

            def wkv_steps(g, s0, s1):
                for s in range(s0, s1):
                    if s > 0:
                        dve.wait_ge(wkv.sem, wkv.value(g, ("g", s - 1)))
                    u2 = REC[:, s, RU:RU + 1, :].broadcast_to((P, 2, B))
                    dve.scalar_tensor_tensor(REC[:, s + 1, RR_:RBB + 1, :], u2, 1.0,
                                                      REC[:, s, RQ:RG + 1, :], ALU.add, ALU.mult).then_inc(wkv.sem, wkv.step(("rb", s)))
                    dve.wait_ge(wkv.sem, wkv.value(g, ("rb", s)))
                    dve.scalar_tensor_tensor(REC[:, s + 1, RU, :], REC[:, s + 1, RR_, :], R_CAP,
                                                      REC[:, s + 1, RBB, :], ALU.min, ALU.mult).then_inc(wkv.sem, wkv.step(("u", s)))
                    dve.reciprocal(REC[:, s + 1, RINV, :], REC[:, s + 1, RR_, :]).then_inc(wkv.sem, wkv.step(("inv", s)))
                    dve.wait_ge(wkv.sem, wkv.value(g, ("inv", s)))
                    dve.tensor_scalar(REC[:, s + 1, RG, :], REC[:, s + 1, RINV, :], 1.0 / R_CAP, 1.0,
                                               ALU.max, ALU.min).then_inc(wkv.sem, wkv.step(("g", s)))

            def y_scan(g):
                dve.wait_ge(wkv.sem, wkv.value(g, ("g", GS - 1)))
                dve.tensor_scalar(F1[:], REC[:, 0:GS, RR_, :], 1.0, None, ALU.min).then_inc(y_dve.sem, y_dve.step("f1"))
                dve.tensor_scalar(F2[:], REC[:, 0:GS, RINV, :], 1.0, None, ALU.min).then_inc(y_dve.sem, y_dve.step("f2"))
                dve.wait_ge(y_dve.sem, y_dve.value(g, "f2"))
                if first(g):
                    dve.wait_ge(ln_act.sem, ln_act.value(NQ - 1, "r"))
                    dve.wait_ge(q_act.sem, q_act.value(0, "iu"))
                dve.tensor_tensor(F2V[:], F2[:], tile3(V[:, cols(g)]), ALU.mult).then_inc(y_dve.sem, y_dve.step("f2v"))
                dve.wait_ge(y_dve.sem, y_dve.value(g, "f2v"))
                for b in range(B):
                    dve.tensor_tensor_scan(AA[:, 1:, b], F1[:, :, b], F2V[:, :, b], AA[:, 0, b:b + 1],
                                                      ALU.mult, ALU.add).then_inc(y_dve.sem, y_dve.step(("aa", b)))
                if not first(g):
                    dve.wait_ge(y_pool.sem, y_pool.value(g - 1, "den"))
                dve.tensor_scalar(E1[:], REC[:, 0:GS, RR_, :], UE[:, 1:2], 1.0, ALU.mult, ALU.min).then_inc(y_dve.sem, y_dve.step("e1"))
                dve.tensor_scalar(E2[:], REC[:, 0:GS, RINV, :], UE[:, 0:1], 1.0, ALU.mult, ALU.min).then_inc(y_dve.sem, y_dve.step("e2"))
                dve.wait_ge(y_dve.sem, y_dve.value(g, "e1"))
                dve.tensor_tensor(EB[:], E1[:], REC[:, 0:GS, RBB, :], ALU.mult).then_inc(y_dve.sem, y_dve.step("eb"))
                dve.tensor_tensor(EAA[:], E1[:], AA[:, 0:GS, :], ALU.mult).then_inc(y_dve.sem, y_dve.step("ea"))
                dve.wait_ge(y_dve.sem, y_dve.value(g, "ea"))
                dve.tensor_copy(AA[:, 0, :], AA[:, GS, :]).then_inc(y_dve.sem, y_dve.step("carry"))

            def y_att(g):
                dve.wait_ge(y_pool.sem, y_pool.value(g, "e2v"))
                dve.wait_ge(y_dve.sem, y_dve.value(g, "carry"))
                dve.tensor_tensor(NUM[:], EAA[:], E2V[:], ALU.add).then_inc(y_dve.sem, y_dve.step("num"))
                dve.wait_ge(y_pool.sem, y_pool.value(g, "den"))
                dve.reciprocal(RDEN[:], DEN[:]).then_inc(y_dve.sem, y_dve.step("rden"))
                dve.wait_ge(y_dve.sem, y_dve.value(g, "rden"))
                dve.tensor_tensor(tile3(YY[:]), NUM[:], RDEN[:], ALU.mult).then_inc(y_dve.sem, y_dve.step("y"))
                wait_apart(y_dve.sem, y_dve.value(g, "y"))
                with dve.If(outside > 0):
                    dve.tensor_copy(YY[:], YS[:, cols(g)]).then_inc(slow_copy, 1)
                    wait_apart(slow_copy, g + 1)
                if not first(g):
                    dve.wait_ge(a_pe.sem, a_pe.value(g - 1, "t_att"))
                dve.scalar_tensor_tensor(ATT[:], SR[:, cols(g)], 1.0, YY[:], ALU.add, ALU.mult).then_inc(y_dve.sem, y_dve.step("att"))

            def norm(g, src, k, stat, aggr, eps):
                for n in range(GT):
                    dve.bn_stats(STAT[:, k, n, :], src(n)).then_inc(a_dve.sem, a_dve.step((stat, n)))
                for n in range(GT):
                    wait_apart(a_dve.sem, a_dve.value(g, (stat, n)))
                    dve.bn_aggr(MV[:, k, n, :], STAT[:, k, n, :]).then_inc(a_dve.sem, a_dve.step((aggr, n)))
                dve.wait_ge(a_dve.sem, a_dve.value(g, (aggr, GT - 1)))
                dve.tensor_scalar(VE[:, k, 0:GT], MV[:, k, 0:GT, 1], LN_EPS, None, ALU.add).then_inc(a_dve.sem, a_dve.step(eps))

            def xr(g):
                return lambda n: X[:, bass.ds(g * GT + n, 1), :].rearrange("p o c -> p (o c)")

            def a_x1(g):
                dve.wait_ge(a_pe.sem, a_pe.value(g, "t_att"))
                pa = pA[:, 0:GN].rearrange("p (n c) -> p n c", c=C)
                dve.scalar_tensor_tensor(X1[:], pa, 0.5, H[:, ranks(g), :], ALU.mult, ALU.add).then_inc(a_dve.sem, a_dve.step("x1"))
                wait_apart(a_dve.sem, a_dve.value(g, "x1"))
                norm(g, lambda n: X1[:, n, :], 0, "st", "ag", "eps")

            def a_x2(g):
                dve.wait_ge(a_pool.sem, a_pool.value(g, "rs"))
                for n in range(GT):
                    dve.tensor_scalar(X2N[:, n, :], X1[:, n, :], MV[:, 0, n, 0:1], RS[:, 0, n:n + 1],
                                                 ALU.subtract, ALU.mult).then_inc(a_dve.sem, a_dve.step(("n", n)))

            def a_mixed(g):
                dve.wait_ge(a_pe.sem, a_pe.value(g, "kv"))
                dve.wait_ge(a_act.sem, a_act.value(g, "rr"))
                kv = pA[:, 0:GN].rearrange("p (n c) -> p n c", c=C)
                dve.scalar_tensor_tensor(T1[:], RRT[:].rearrange("p (n c) -> p n c", c=C), 1.0, kv,
                                                    ALU.add, ALU.mult).then_inc(a_dve.sem, a_dve.step("t1"))
                dve.wait_ge(a_dve.sem, a_dve.value(g, "t1"))
                if not first(g):
                    dve.wait_ge(a_pool.sem, a_pool.value(g - 1, "xg"))
                dve.scalar_tensor_tensor(XA[:], T1[:], 0.5, X1[:], ALU.mult, ALU.add).then_inc(a_dve.sem, a_dve.step("xa"))

            def a_stats3(g):
                wait_apart(a_pool.sem, a_pool.value(g, "xr"))
                norm(g, xr(g), 1, "st3", "ag3", "eps3")

            def a_n3(g):
                dve.wait_ge(a_pool.sem, a_pool.value(g, "rs3"))
                if not first(g):
                    dve.wait_ge(a_pool.sem, a_pool.value(g - 1, "hc"))
                for n in range(GT):
                    dve.tensor_scalar(N3[:, n, :], xr(g)(n), MV[:, 1, n, 0:1], RS[:, 1, n:n + 1],
                                                 ALU.subtract, ALU.mult).then_inc(a_dve.sem, a_dve.step(("n3", n)))

            def a_top2(g):
                dve.wait_ge(a_pe.sem, a_pe.value(g, "logits"))
                dve.tensor_copy(LG[:], pC[:, 0:GT * E].rearrange("p (n e) -> p n e", e=E)).then_inc(a_dve.sem, a_dve.step("lg"))
                wait_apart(a_dve.sem, a_dve.value(g, "lg"))
                for n in range(GT):
                    dve.max(MX[:, n, :], LG[:, n, :]).then_inc(a_dve.sem, a_dve.step(("mx", n)))
                wait_apart(a_dve.sem, a_dve.value(g, ("mx", GT - 1)))
                for n in range(GT):
                    dve.max_index(IX[:, n, :], MX[:, n, :], LG[:, n, :]).then_inc(a_dve.sem, a_dve.step(("ix", n)))
                dve.tensor_tensor(DF[:], MX[:, :, 0], MX[:, :, 1], ALU.subtract).then_inc(a_dve.sem, a_dve.step("df"))
                dve.wait_ge(a_dve.sem, a_dve.value(g, ("ix", GT - 1)))
                dve.tensor_copy(IXF[:], IX[:, :, 0:2]).then_inc(a_dve.sem, a_dve.step("ixf"))

            def a_weights(g):
                dve.wait_ge(a_act.sem, a_act.value(g, "th"))
                dve.tensor_scalar(PR[:, :, 0], TH[:], 0.5, 0.5, ALU.mult, ALU.add).then_inc(a_dve.sem, a_dve.step("p1"))
                dve.tensor_scalar(PR[:, :, 1], TH[:], -0.5, 0.5, ALU.mult, ALU.add).then_inc(a_dve.sem, a_dve.step("p2"))
                dve.wait_ge(a_dve.sem, a_dve.value(g, "p2"))
                for n in range(GT):
                    for k in range(2):
                        dve.tensor_scalar(WA[:, k, n, :], IOTA[:], IXF[:, n, k:k + 1], PR[:, n, k:k + 1],
                                                     ALU.is_equal, ALU.mult).then_inc(a_dve.sem, a_dve.step(("w", n, k)))
                dve.wait_ge(a_dve.sem, a_dve.value(g, ("w", 1, 1)))
                dve.tensor_tensor(WT[:], WA[:, 0], WA[:, 1], ALU.add).then_inc(a_dve.sem, a_dve.step("wt"))

            def weights_in(g):
                if not first(g):
                    dve.wait_ge(e_act.sem, e_act.value(g - 1, f"w{E - 1}.{GT - 1}"))
                dve.wait_ge(a_dve.sem, a_dve.value(g, "wt"))
                dve.tensor_copy(WE[:], WT[:]).then_inc(e_dve.sem, e_dve.step("we"))

            def hidden(g, e):
                if e >= 2:
                    dve.wait_ge(e_pe.sem, e_pe.value(g, f"y{e - 2}"))
                elif not first(g):
                    dve.wait_ge(e_pe.sem, e_pe.value(g - 1, f"y{E - 2 + e}"))
                dve.wait_ge(e_act.sem, e_act.value(g, f"s{e}"))
                dve.tensor_tensor(HT[:, e % 2].rearrange("p m n -> p (m n)"), SL[:, e % 2],
                                             pH3[e % 2][:], ALU.mult).then_inc(e_dve.sem, e_dve.step(f"m{e}"))

            def turn(w_g, ya, e_g):
                if e_g is not None:
                    weights_in(e_g)
                    hidden(e_g, 0)
                if ya is not None:
                    y_scan(ya)
                if e_g is not None:
                    hidden(e_g, 1)
                if ya is not None:
                    y_att(ya)
                if w_g is not None:
                    wkv_begin(w_g)
                done = 0
                for e in range(E):
                    if e_g is not None and e >= 2:
                        hidden(e_g, e)
                    if w_g is not None:
                        wkv_steps(w_g, done, done + STEPS_OF_SLOT[e])
                        done += STEPS_OF_SLOT[e]
                    if ya is not None:
                        if e == 0:
                            a_x1(ya)
                        if e == 1:
                            a_x2(ya)
                        if e == 4:
                            a_mixed(ya)
                        if e == 5:
                            a_stats3(ya)
                            a_n3(ya)
                        if e == 7:
                            a_top2(ya)
                            a_weights(ya)

            def general_path():
                count = [0]
                per = 17
                dve.memset(sPP[:], PP_START)
                dve.memset(sAA[:], 0.0)
                dve.memset(sBB[:], 1.0).then_inc(slow_copy, 1)
                dve.wait_ge(slow_copy, 1)
                dve.sem_clear(slow_copy)
                with dve.Fori(0, T) as t:
                    kt, vt = K[:, cols(t, B)], V[:, cols(t, B)]

                    def link(ins):
                        count[0] += 1
                        ins.then_inc(slow_dve, 1)
                        if count[0] == per:
                            wait_apart(slow_dve, t * per + count[0])
                        else:
                            dve.wait_ge(slow_dve, t * per + count[0])

                    link(dve.tensor_tensor(sM[:], sPP[:], kt, ALU.max))
                    link(dve.scalar_tensor_tensor(sP[:], kt, u_v, sPP[:], ALU.add, ALU.max))
                    link(dve.tensor_tensor(sD[:, 0], sPP[:], sP[:], ALU.subtract))
                    link(dve.scalar_tensor_tensor(sD[:, 1], kt, u_v, sP[:], ALU.add, ALU.subtract))
                    link(dve.tensor_tensor(sD[:, 2], sPP[:], sM[:], ALU.subtract))
                    link(dve.tensor_tensor(sD[:, 3], kt, sM[:], ALU.subtract))
                    link(dve.tensor_scalar(sT[:, 8], sM[:], w_v, None, ALU.add))
                    dve.wait_ge(slow_act, t * 2 + 1)
                    link(dve.tensor_tensor(sT[:, 0:2], sE[:, 0:4:2], sAA[:].rearrange("p (o b) -> p o b", o=1)
                                           .broadcast_to((P, 2, B)), ALU.mult))
                    link(dve.tensor_tensor(sT[:, 2:4], sE[:, 1:4:2], vt.rearrange("p (o b) -> p o b", o=1)
                                           .broadcast_to((P, 2, B)), ALU.mult))
                    link(dve.tensor_tensor(sT[:, 4:6], sE[:, 0:4:2], sBB[:].rearrange("p (o b) -> p o b", o=1)
                                           .broadcast_to((P, 2, B)), ALU.mult))
                    link(dve.tensor_tensor(sT[:, 0], sT[:, 0], sT[:, 2], ALU.add))
                    link(dve.tensor_tensor(sAA[:], sT[:, 1], sT[:, 3], ALU.add))
                    link(dve.tensor_tensor(sT[:, 6], sT[:, 4], sE[:, 1], ALU.add))
                    link(dve.reciprocal(sT[:, 7], sT[:, 6]))
                    link(dve.tensor_tensor(YS[:, cols(t, B)], sT[:, 0], sT[:, 7], ALU.mult))
                    link(dve.tensor_tensor(sBB[:], sT[:, 5], sE[:, 3], ALU.add))
                    dve.wait_ge(slow_act, t * 2 + 2)
                    link(dve.tensor_tensor(sPP[:], sT[:, 8], sL[:], ALU.add))
                    assert count[0] == per

            wkv_begin(0)
            wkv_steps(0, 0, GS)
            dve.wait_ge(dk_dve.sem, dk_dve.value(0, "flag"))
            outside = dve.value_load(FLAG[0:1, 0:1])
            with dve.If(outside > 0):
                general_path()
            turn(1, 0, None)
            turn(2, 1, 0)
            with dve.Fori(1, NG - 2) as g:
                turn(g + 2, g + 1, g)
            turn(None, NG - 1, NG - 2)
            turn(None, None, NG - 1)

        @block.tensor
        def _(pe):
            pe.wait_ge(pool_const.sem, pool_const.value(0, "ident"))
            pe.wait_ge(mod_act.sem, mod_act.value(0, "silu"))
            pe.transpose(pB[:, 0:P], CS[:], ident[:]).then_inc(mod_pe.sem, mod_pe.step("ct"))
            pe.wait_ge(mod_act.sem, mod_act.value(0, "ct"))
            pe.wait_ge(wmod_in, 16)
            pe.matmul(pH3[1][:], CT[:], WMOD[:, 0:512], start=True, stop=True)
            pe.matmul(pY[:, 0:256], CT[:], WMOD[:, 512:768], start=True, stop=True).then_inc(mod_pe.sem, mod_pe.step("mod"))
            pe.wait_ge(wkvr_in, 48)
            pe.wait_ge(shift_set, 1)

            def first_stage(q):
                if not first(q):
                    pe.wait_ge(ln_act.sem, ln_act.value(q - 1, "r"))
                for n in range(QT):
                    pe.wait_ge(ln_dve.sem, ln_dve.value(q, ("n2", n)))
                    ins = pe.transpose(pA[:, n * P:(n + 1) * P], HN[:, n, :], ident[:])
                ins.then_inc(ln_pe.sem, ln_pe.step("t"))
                pe.wait_ge(ln_act.sem, ln_act.value(q, "hs"))
                for w, p, name in ((WK, pH1[0], "k"), (WV, pH3[0], "v"), (WR, pH1[1], "r")):
                    pe.matmul(p[:], w[:], HSh[:, cols(q, QN)], start=True, stop=True).then_inc(ln_pe.sem, ln_pe.step(name))

            first_stage(0)
            with pe.Fori(1, NQ) as q:
                first_stage(q)
            for s in (w1_in, w3_in, w2_in):
                pe.wait_ge(s, 16)
            pe.wait_ge(mix_in, 16 * 4)
            pe.wait_ge(mod_dve.sem, mod_dve.value(0, "copy1"))
            pe.wait_ge(ln_act.sem, ln_act.value(NQ - 1, "r"))

            def to_tokens(g, src, dst, name):
                for n in range(GT):
                    ins = pe.transpose(dst[:, n * P:(n + 1) * P], src(n), ident[:])
                ins.then_inc(a_pe.sem, a_pe.step(name))

            def a_att(g):
                if not first(g):
                    pe.wait_ge(a_dve.sem, a_dve.value(g - 1, "t1"))
                pe.wait_ge(y_dve.sem, y_dve.value(g, "att"))
                to_tokens(g, lambda n: ATT[:, n * P:(n + 1) * P], pA, "t_att")

            def a_x2(g):
                pe.wait_ge(a_dve.sem, a_dve.value(g, ("n", GT - 1)))
                to_tokens(g, lambda n: X2N[:, n, :], pA, "t_x2")

            def a_mix(g):
                pe.wait_ge(a_act.sem, a_act.value(g, "hs2"))
                for n in range(GT):
                    ins = pe.matmul(pA[:, n * C:(n + 1) * C], HS2[:, n * P:(n + 1) * P], WCR[:], start=True, stop=True)
                ins.then_inc(a_pe.sem, a_pe.step("rr"))
                if not first(g):
                    pe.wait_ge(a_dve.sem, a_dve.value(g - 1, "lg"))
                for i, p in enumerate((pB, pC)):
                    for m in range(FM // 2):
                        f = i * FM // 2 + m
                        ins = pe.matmul(p[:, m * GN:(m + 1) * GN], WCK[:, f * P:(f + 1) * P], HS2[:, 0:GN],
                                        start=True, stop=True)
                    ins.then_inc(a_pe.sem, a_pe.step(f"kk{i}"))

            def a_kv(g):
                pe.wait_ge(a_act.sem, a_act.value(g, "rr"))
                for n in range(GT):
                    for f in range(FM):
                        if n == 0 and f in (0, FM // 2):
                            pe.wait_ge(a_act.sem, a_act.value(g, "sq0" if f == 0 else "sq1"))
                        ins = pe.matmul(pA[:, n * C:(n + 1) * C], KQ[:, f, n * P:(n + 1) * P], WCV[:, f, :],
                                        start=(f == 0), stop=(f == FM - 1))
                ins.then_inc(a_pe.sem, a_pe.step("kv"))

            def a_h3(g):
                pe.wait_ge(a_pool.sem, a_pool.value(g, "h3"))
                to_tokens(g, lambda n: H3[:, n, :], pB, "t_h3")

            def a_logits(g):
                pe.wait_ge(a_act.sem, a_act.value(g, "h3s"))
                for n in range(GT):
                    ins = pe.matmul(pC[:, n * E:(n + 1) * E], H3S[:, n * P:(n + 1) * P], WG[:], start=True, stop=True)
                ins.then_inc(a_pe.sem, a_pe.step("logits"))

            def hidden(g, e):
                if e == 0:
                    pe.wait_ge(a_act.sem, a_act.value(g, "h3t"))
                if e >= 2:
                    pe.wait_ge(e_dve.sem, e_dve.value(g, f"m{e - 2}"))
                elif not first(g):
                    pe.wait_ge(e_dve.sem, e_dve.value(g - 1, f"m{E - 2 + e}"))
                for w, p in ((W1, pH1[e % 2]), (W3, pH3[e % 2])):
                    for m in range(HM):
                        ins = pe.matmul(p[:, m * GN:(m + 1) * GN], w[:, e, m * P:(m + 1) * P], H3T[:, cols(g)],
                                        start=True, stop=True)
                ins.then_inc(e_pe.sem, e_pe.step(f"h{e}"))

            def project(g, e):
                pe.wait_ge(e_dve.sem, e_dve.value(g, f"m{e}"))
                if e >= 1:
                    pe.wait_ge(e_act.sem, e_act.value(g, f"w{e - 1}.{GT - 1}"))
                elif not first(g):
                    pe.wait_ge(e_act.sem, e_act.value(g - 1, f"w{E - 1}.{GT - 1}"))
                for n in range(GT):
                    for m in range(HM):
                        ins = pe.matmul(pY[:, n * C:(n + 1) * C], HT[:, e % 2, m, n * P:(n + 1) * P], W2[:, e, m, :],
                                        start=(m == 0), stop=(m == HM - 1))
                ins.then_inc(e_pe.sem, e_pe.step(f"y{e}"))

            def turn(ya, e_g):
                if e_g is not None:
                    hidden(e_g, 0)
                for e in range(E):
                    if e_g is not None:
                        if e + 1 < E:
                            hidden(e_g, e + 1)
                        project(e_g, e)
                    if ya is not None:
                        if e == 1:
                            a_att(ya)
                        if e == 2:
                            a_x2(ya)
                        if e == 3:
                            a_mix(ya)
                        if e == 4:
                            a_kv(ya)
                        if e == 6:
                            a_h3(ya)
                        if e == 7:
                            a_logits(ya)

            turn(0, None)
            turn(1, 0)
            with pe.Fori(1, NG - 1) as g:
                turn(g + 1, g)
            turn(None, NG - 1)


_INS = ['L0_attn_x', 'L0_attn_time_decay', 'L0_attn_time_first', 'L0_attn_time_shift', 'L0_attn_Wk', 'L0_attn_Wv',
        'L0_attn_Wr', 'L0_attn_Wck', 'L0_attn_Wcv', 'L0_attn_Wcr', 'L0_attn_ln1_g', 'L0_attn_ln1_b', 'L0_attn_ln2_g',
        'L0_attn_ln2_b', 'L0_ffn_w_gate', 'L0_ffn_w1', 'L0_ffn_w3', 'L0_ffn_w2', 'L0_c', 'L0_wmod']
_OUTS = [((8, 256, 128), 'float32')]


def kernel(**inputs):
    import numpy as _np
    import concourse.bacc as _bacc
    from concourse import mybir as _mybir
    from concourse.bass_utils import run_bass_kernel_spmd as _run

    nc = _bacc.Bacc("TRN2", target_bir_lowering=False, num_devices=1)
    arrays, args = {}, []
    for name in _INS:
        a = _np.ascontiguousarray(inputs[name])
        arrays[f"in_{name}_dram"] = a
        args.append(nc.dram_tensor(f"in_{name}_dram", a.shape, _mybir.dt.from_np(a.dtype), kind="ExternalInput").ap())
    for i, (shape, dtype) in enumerate(_OUTS):
        dt = _mybir.dt.from_np(_np.dtype(dtype))
        args.append(nc.dram_tensor(f"out_{i}_dram", shape, dt, kind="ExternalOutput").ap())
    adaln_rwkv_moe(nc, *args)
    r = _run(nc, [arrays], core_ids=[0])
    got = tuple(r.results[0][f"out_{i}_dram"] for i in range(len(_OUTS)))
    return got[0]
```

```python
from contextlib import ExitStack
from itertools import chain

import concourse.bass as bass
from concourse import mybir

F32 = mybir.dt.float32
I32 = mybir.dt.int32
U32 = mybir.dt.uint32
ALU = mybir.AluOpType
ACT = mybir.ActivationFunctionType
AX_X = mybir.AxisListType.X
RMAX = bass.bass_isa.ReduceOp.max

P = 128
LN_EPS = 1e-5
MIN_GATE = 0.25
PP_START = -1e38
R_CAP = 2.0 ** 60
K_SAFE = 12.0
W_SAFE = 16.0


class Steps:

    def __init__(self, sem, names):
        self.sem, self.per = sem, len(names)
        self.at = {n: i + 1 for i, n in enumerate(names)}
        self.now = 0

    def value(self, group, name):
        return group * self.per + self.at[name]

    def step(self, name):
        assert self.at[name] == self.now % self.per + 1, name
        self.now += 1
        return 1


def first(g):
    return isinstance(g, int) and g == 0


def adaln_rwkv_moe(nc, x, time_decay, time_first, time_shift, Wk, Wv, Wr, Wck, Wcv, Wcr,
                   ln1_g, ln1_b, ln2_g, ln2_b, w_gate, w1, w3, w2, c, wmod, out):
    B, T, C = x.shape
    E, _, HID = w1.shape
    assert C == P and P % B == 0
    TS = P // B
    NT = T // TS
    GT = 2
    NG = NT // GT
    GS = GT * TS
    GN = GT * P
    N = B * T
    QT = 4
    NQ = NT // QT
    QN = QT * P
    FM = Wck.shape[1] // P
    HM = HID // P
    SLOTS = 2 * E
    LATE = 3
    FIRST_FULL = 4
    TURNS = NG + 3
    RP = 4

    with ExitStack() as ctx:
        def sb(name, shape, dt=F32):
            return ctx.enter_context(nc.sbuf_tensor(name, shape, dt))

        def pb(name):
            return ctx.enter_context(nc.psum_tensor(name, [P, 512], F32))

        def sem(name):
            return ctx.enter_context(nc.semaphore(name))

        def steps(name, names):
            return Steps(sem(name), names)

        X = sb("X", [P, NT, C])
        H = sb("H", [P, NT, C])
        HSh = sb("HSh", [P, B + N])
        K = sb("K", [P, N])
        V = sb("V", [P, N])
        SR = sb("SR", [P, N])
        Q = sb("Q", [P, N])
        YS = sb("YS", [P, N])
        H3T = sb("H3T", [P, N])
        W1 = sb("W1", [P, E, HID])
        W3 = sb("W3", [P, E, HID])
        W2 = sb("W2", [P, E, HM, C])
        WK = sb("WK", [P, C])
        WV = sb("WV", [P, C])
        WR = sb("WR", [P, C])
        WCK = sb("WCK", [P, FM * P])
        WCV = sb("WCV", [P, FM, C])
        WCR = sb("WCR", [P, C])
        WG = sb("WG", [P, E])
        WMOD = sb("WMOD", [P, 6 * C])
        CB = sb("CB", [B, C])
        CSW = sb("CSW", [B, 1])
        CS = sb("CS", [B, C])
        CT = sb("CT", [P, P])
        MOD = sb("MOD", [P, 6, C])
        GSG = sb("GSG", [P, 2, C])
        GAB = sb("GAB", [P, 2, C])
        VEC = sb("VEC", [P, 8])
        w_v, u_v, g1_v, b1_v, g2_v, b2_v, sh_v = (VEC[:, i:i + 1] for i in range(7))
        UE = sb("UE", [P, 2])
        ident = sb("ident", [P, P])
        zero = sb("zero", [P, P])
        NHALF = sb("NHALF", [P, QT])
        IOTA = sb("IOTA", [P, E])
        STAT = sb("STAT", [P, 2, QT, 6])
        MV = sb("MV", [P, 2, QT, 2])
        VE = sb("VE", [P, 2, QT])
        RS = sb("RS", [P, 2, QT])
        XN = sb("XN", [P, QT, C])
        HN = sb("HN", [P, QT, C])
        KM = sb("KM", [P, NQ + 2])
        VA = sb("VA", [P, 2])
        KMM = sb("KMM", [P, 1])
        KMA = sb("KMA", [P, 1])
        FLAG = sb("FLAG", [P, 1], I32)
        REC = sb("REC", [P, GS + 1, 6, B])
        RQ, RG, RR_, RBB, RU, RINV = range(6)
        F1 = sb("F1", [P, GS, B])
        F2 = sb("F2", [P, GS, B])
        F2V = sb("F2V", [P, GS, B])
        E1 = sb("E1", [P, GS, B])
        E2 = sb("E2", [P, GS, B])
        EB = sb("EB", [P, GS, B])
        EAA = sb("EAA", [P, GS, B])
        E2V = sb("E2V", [P, GS, B])
        DEN = sb("DEN", [P, GS, B])
        NUM = sb("NUM", [P, GS, B])
        RDEN = sb("RDEN", [P, GS, B])
        YY = sb("YY", [P, GN])
        AA = sb("AA", [P, GS + 1, B])
        ATT = sb("ATT", [P, GN])
        X1 = sb("X1", [P, GT, C])
        X2N = sb("X2N", [P, GT, C])
        HS2 = sb("HS2", [P, B + GN])
        RRT = sb("RRT", [P, GN])
        KR = sb("KR", [P, FM * GN])
        KQ = sb("KQ", [P, FM, GN])
        T1 = sb("T1", [P, GT, C])
        XA = sb("XA", [P, GT, C])
        XG = sb("XG", [P, GT, C])
        N3 = sb("N3", [P, GT, C])
        H3 = sb("H3", [P, GT, C])
        H3S = sb("H3S", [P, GN])
        LG = sb("LG", [P, GT, E])
        MX = sb("MX", [P, GT, 8])
        IX = sb("IX", [P, GT, 8], U32)
        IXF = sb("IXF", [P, GT, 2])
        DF = sb("DF", [P, GT])
        TH = sb("TH", [P, GT])
        PR = sb("PR", [P, GT, 2])
        WA = sb("WA", [P, 2, GT, E])
        WT = sb("WT", [P, GT, E])
        WE = sb("WE", [P, GT, E])
        SL = sb("SL", [P, 2, HM * GN])
        HT = sb("HT", [P, 2, HM, GN])
        YW = sb("YW", [P, 2, GT, C])
        ACC = sb("ACC", [P, GT, C])
        OG = sb("OG", [P, GT, C])
        OUT = sb("OUT", [P, GT, C])
        sPP = sb("sPP", [P, B])
        sAA = sb("sAA", [P, B])
        sBB = sb("sBB", [P, B])
        sM = sb("sM", [P, B])
        sP = sb("sP", [P, B])
        sD = sb("sD", [P, 4, B])
        sE = sb("sE", [P, 4, B])
        sT = sb("sT", [P, 9, B])
        sL = sb("sL", [P, B])

        pH1 = [pb("pH1a"), pb("pH1b")]
        pH3 = [pb("pH3a"), pb("pH3b")]
        pY = pb("pY")
        pA, pB, pC = pb("pA"), pb("pB"), pb("pC")

        x_first, x_rest = sem("x_first"), sem("x_rest")
        vec_in, c_in, wkvr_in = sem("vec_in"), sem("c_in"), sem("wkvr_in")
        wmod_first, wmod_rest, warm = sem("wmod_first"), sem("wmod_rest"), sem("warm")
        mix_in, w1_in, w3_in, w2_in = sem("mix_in"), sem("w1_in"), sem("w3_in"), sem("w2_in")
        stored = sem("stored")
        pool_const = steps("pool_const", ["zero", "ident", "rest"])
        mod_act = steps("mod_act", ["silu", "ct"])
        mod_pe = steps("mod_pe", ["ct", "first", "rest"])
        mod_dve = steps("mod_dve", ["sa", "ca", "rest", "cb", "sign", "abs", "size", "gate"])
        ln_dve = steps("ln_dve", [(n, i) for n in ("st", "ag") for i in range(QT)] + ["eps"]
                       + [(n, i) for n in ("scaled", "h") for i in range(QT)])
        ln2_dve = steps("ln2_dve", [(n, i) for n in ("st", "ag") for i in range(QT)] + ["eps"]
                        + [("n", i) for i in range(QT)])
        ln_pool, ln2_pool = steps("ln_pool", ["rs"]), steps("ln2_pool", ["rs"])
        ln_pe = steps("ln_pe", ["t", "k", "v", "r"])
        ln_act = steps("ln_act", ["hs", "k", "abs_k", "v", "r"])
        shift_set = sem("shift_set")
        dk_dve = steps("dk_dve", ["dk", "clip"])
        dk_pool = steps("dk_pool", ["dk", "clip"])
        kmax_dve = steps("kmax_dve", [("km", q) for q in range(NQ)] + ["wu", "um", "max", "flag"])
        u_act = steps("u_act", ["u", "iu"])
        q_act = steps("q_act", ["first"] + [("q", q) for q in range(NQ)])
        kmax_all = sem("kmax_all")
        wkv = steps("wkv", ["q", "carry"] + [(n, s) for s in range(GS) for n in ("rb", "u", "inv", "g")])
        wkv_start = steps("wkv_start", ["z", "g", "bb", "inv"])
        y_dve = steps("y_dve", ["f1", "f2", "e1", "e2", "eb", "f2v"] + [("aa", b) for b in range(B)]
                      + ["ea", "carry", "num"] + [("rden", i) for i in range(RP)] + ["y", "att"])
        y_pool = steps("y_pool", ["e2v", "den"])
        a_pe = steps("a_pe", ["t_att", "t_x2", "rr", "kk0", "kk1", "kv"])
        g_pe = steps("g_pe", ["t_h3", "logits"])
        a_dve = steps("a_dve", ["x1", ("st", 0), ("st", 1), ("ag", 0), ("ag", 1), "eps", ("n", 0), ("n", 1)])
        g_dve = steps("g_dve", ["t1", "xa", ("st3", 0), ("st3", 1), ("ag3", 0), ("ag3", 1), "eps3",
                                ("n3", 0), ("n3", 1), ("h3", 0), ("h3", 1),
                                "lg", ("mx", 0), ("mx", 1), ("ix", 0), ("ix", 1), "df", "ixf", "p1", "p2",
                                ("w", 0, 0), ("w", 0, 1), ("w", 1, 0), ("w", 1, 1), "wt"])
        a_pool = steps("a_pool", ["rs"])
        g_pool = steps("g_pool", ["xg", "xr", "rs3"])
        a_act = steps("a_act", ["carry", "hs2", "rr", "re0", "sq0", "re1", "sq1"])
        g_act = steps("g_act", ["h3s", "h3t", "th"])
        h_pe = steps("h_pe", list(range(E)))
        p_pe = steps("p_pe", list(range(E)))
        s_act = steps("s_act", list(range(E)))
        w_act = steps("w_act", [(e, n) for e in range(E) for n in range(GT)])
        e_dve = steps("e_dve", [f"m{e}.{m}" for e in range(E) for m in range(HM)])
        we_dve = steps("we_dve", ["we"])
        e_pool = steps("e_pool", [f"a{e}" for e in range(1, E)] + ["og", "out"])
        passed = sem("passed")
        slow_dve, slow_act, slow_copy = sem("slow_dve"), sem("slow_act"), sem("slow_copy")

        x_tok = x.rearrange("b (j s) c -> s b j c", s=TS)
        out_tok = out.rearrange("b (j s) c -> s b j c", s=TS)

        def row(v):
            return v.rearrange("(p o) -> p o", o=1)

        def difference_cols(q):
            return max(GN, q * QN - B), (q + 1) * QN - B

        def cols(g, n=GN):
            return bass.ds(g * n, n)

        def ranks(g):
            return bass.ds(g * GT, GT)

        def groups(t):
            def group(g):
                return g if not isinstance(g, int) or 0 <= g < NG else None
            return group(t), group(t - 1), group(t - 2), group(t - 3)

        def expert(t, j):
            _, _, gate, late = groups(t)
            return (late, E - LATE + j) if j < LATE else (gate, j - LATE)

        def ahead(t, j):
            _, _, gate, _ = groups(t)
            return expert(t, j + 1) if j + 1 < E else (gate, E - LATE)

        def tile3(ap):
            return ap.rearrange("p (t b) -> p t b", b=B)

        block = ctx.enter_context(nc.Block())

        @block.sync
        def _(sp):
            for n in range(QT):
                sp.dma_start(X[:, n, :], x_tok[:, :, n, :]).then_inc(x_first, 16)
            for i, v in enumerate((row(time_decay), row(time_first), row(ln1_g), row(ln1_b), row(ln2_g), row(ln2_b),
                                   time_shift.rearrange("a b c -> c (a b)"))):
                sp.dma_start(VEC[:, i:i + 1], v).then_inc(vec_in, 16)
            for n in range(QT, NT):
                sp.dma_start(X[:, n, :], x_tok[:, :, n, :]).then_inc(x_rest, 16)
            sp.dma_start(W1[:], w1.rearrange("e d h -> d e h")).then_inc(w1_in, 16)
            sp.dma_start(W3[:], w3.rearrange("e d h -> d e h")).then_inc(w3_in, 16)
            sp.dma_start(W2[:], w2.rearrange("e (m p) d -> p e m d", p=P)).then_inc(w2_in, 16)
            with sp.Fori(0, NG) as g:
                sp.wait_ge(e_pool.sem, e_pool.value(g, "out"))
                for n in range(GT):
                    to = out_tok[:, :, bass.ds(g * GT + n, 1), :].rearrange("s b o c -> s b (o c)")
                    sp.dma_start(to, OUT[:, n, :]).then_inc(stored, 16)
            sp.wait_ge(stored, 16 * NT)

        @block.gpsimd
        def _(pool):
            pool.memset(zero[:], 0.0).then_inc(pool_const.sem, pool_const.step("zero"))
            pool.wait_ge(pool_const.sem, pool_const.value(0, "zero"))
            pool.affine_select(out=ident[:], in_=zero[:], compare_op=ALU.not_equal, fill=1.0, base=0,
                                               pattern=[[-1, P]], channel_multiplier=1).then_inc(pool_const.sem, pool_const.step("ident"))
            for e in range(E):
                pool.memset(IOTA[:, e:e + 1], float(e))
            pool.memset(Q[:, N - B:N], 1.0)
            pool.memset(NHALF[:], -0.5).then_inc(pool_const.sem, pool_const.step("rest"))
            pool.wait_ge(pool_const.sem, pool_const.value(0, "rest"))

            def deviations(q):
                pool.wait_ge(ln_dve.sem, ln_dve.value(q, "eps"))
                pool.tensor_tensor(RS[:, 0, :], VE[:, 0, :], NHALF[:], ALU.pow) \
                    .then_inc(ln_pool.sem, ln_pool.step("rs"))

            def deviations2(q):
                pool.wait_ge(ln2_dve.sem, ln2_dve.value(q, "eps"))
                pool.tensor_tensor(RS[:, 1, :], VE[:, 1, :], NHALF[:], ALU.pow) \
                    .then_inc(ln2_pool.sem, ln2_pool.step("rs"))

            def differences(q):
                c0, c1 = difference_cols(q)
                pool.wait_ge(ln_act.sem, ln_act.value(q, "k"))
                pool.tensor_tensor(YS[:, c0:c1], K[:, c0:c1], K[:, c0 + B:c1 + B], ALU.subtract) \
                    .then_inc(dk_pool.sem, dk_pool.step("dk"))
                pool.wait_ge(dk_pool.sem, dk_pool.value(q, "dk"))
                pool.tensor_scalar(YS[:, c0:c1], YS[:, c0:c1], -2.0 * K_SAFE, 2.0 * K_SAFE, ALU.max, ALU.min) \
                    .then_inc(dk_pool.sem, dk_pool.step("clip"))

            deviations(0)
            for q in range(NQ):
                deviations2(q)
                if q + 1 < NQ:
                    deviations(q + 1)
                if q > 0:
                    differences(q - 1)
            pool.wait_ge(kmax_dve.sem, kmax_dve.value(0, "max"))
            pool.partition_all_reduce(KMA[:], KMM[:], P, RMAX).then_inc(kmax_all, 1)
            differences(NQ - 1)

            def y_part(g):
                if not first(g):
                    pool.wait_ge(y_dve.sem, y_dve.value(g - 1, ("rden", RP - 1)))
                pool.wait_ge(y_dve.sem, y_dve.value(g, "e2"))
                pool.tensor_tensor(E2V[:], E2[:], tile3(V[:, cols(g)]), ALU.mult).then_inc(y_pool.sem, y_pool.step("e2v"))
                pool.wait_ge(y_dve.sem, y_dve.value(g, "eb"))
                pool.tensor_tensor(DEN[:], EB[:], E2[:], ALU.add).then_inc(y_pool.sem, y_pool.step("den"))

            def a_ln2(g):
                pool.wait_ge(a_dve.sem, a_dve.value(g, "eps"))
                pool.tensor_tensor(RS[:, 0, 0:GT], VE[:, 0, 0:GT], NHALF[:, 0:GT], ALU.pow).then_inc(a_pool.sem, a_pool.step("rs"))

            def a_residual(g):
                pool.wait_ge(g_dve.sem, g_dve.value(g, "xa"))
                pool.tensor_tensor(XG[:], XA[:], gate_rows(0), ALU.mult).then_inc(g_pool.sem, g_pool.step("xg"))
                pool.wait_ge(g_pool.sem, g_pool.value(g, "xg"))
                pool.tensor_tensor(X[:, ranks(g), :], XG[:], X[:, ranks(g), :], ALU.add).then_inc(g_pool.sem, g_pool.step("xr"))

            def a_ln3(g):
                pool.wait_ge(g_dve.sem, g_dve.value(g, "eps3"))
                pool.tensor_tensor(RS[:, 1, 0:GT], VE[:, 1, 0:GT], NHALF[:, 0:GT], ALU.pow).then_inc(g_pool.sem, g_pool.step("rs3"))

            def accumulate(g, e):
                pool.wait_ge(w_act.sem, w_act.value(g, (e, GT - 1)))
                if e == 1:
                    if not first(g):
                        pool.wait_ge(e_pool.sem, e_pool.value(g - 1, "og"))
                    pool.tensor_tensor(ACC[:], YW[:, 0], YW[:, 1], ALU.add).then_inc(e_pool.sem, e_pool.step("a1"))
                else:
                    pool.wait_ge(e_pool.sem, e_pool.value(g, f"a{e - 1}"))
                    pool.tensor_tensor(ACC[:], ACC[:], YW[:, e % 2], ALU.add).then_inc(e_pool.sem, e_pool.step(f"a{e}"))

            def finish(g):
                pool.wait_ge(e_pool.sem, e_pool.value(g, f"a{E - 1}"))
                pool.tensor_tensor(OG[:], ACC[:], gate_rows(1), ALU.mult).then_inc(e_pool.sem, e_pool.step("og"))
                pool.wait_ge(e_pool.sem, e_pool.value(g, "og"))
                if not first(g):
                    pool.wait_ge(stored, g * (16 * GT))
                pool.tensor_tensor(OUT[:], OG[:], X[:, ranks(g), :], ALU.add).then_inc(e_pool.sem, e_pool.step("out"))

            def gate_rows(k):
                return GAB[:, k:k + 1, :].broadcast_to((P, GT, C))

            def turn(t):
                _, att, gate, late = groups(t)
                for slot in range(SLOTS):
                    g, e = expert(t, slot // 2)
                    if slot == 0 and att is not None:
                        y_part(att)
                    if slot == 5 and att is not None:
                        a_ln2(att)
                    if slot == 13 and att is not None:
                        a_residual(att)
                    if slot == 15 and att is not None:
                        a_ln3(att)
                    if slot % 2 == 1 and g is not None and e > 0:
                        accumulate(g, e)
                    if slot == 2 * LATE and late is not None:
                        finish(late)

            for t in range(1, FIRST_FULL):
                turn(t)
            with pool.Fori(FIRST_FULL, NG) as t:
                turn(t)
            for t in range(NG, TURNS):
                turn(t)

        @block.scalar
        def _(act):
            act.dma_start(CB[:], c).then_inc(c_in, 16)
            act.dma_start(WMOD[:, 0:2 * C], wmod[:, 0:2 * C]).then_inc(wmod_first, 16)
            act.dma_start(WMOD[:, 2 * C:], wmod[:, 2 * C:]).then_inc(wmod_rest, 16)
            for dst, src in ((WK, Wk), (WV, Wv), (WR, Wr)):
                act.dma_start(dst[:], src).then_inc(wkvr_in, 16)
            act.dma_start(WCK[:], Wck).then_inc(mix_in, 16)
            act.dma_start(WCV[:], Wcv.rearrange("(m p) d -> p m d", p=P)).then_inc(mix_in, 16)
            act.dma_start(WCR[:], Wcr).then_inc(mix_in, 16)
            act.dma_start(WG[:], w_gate).then_inc(mix_in, 16)

            act.wait_ge(pool_const.sem, pool_const.value(0, "zero"))
            act.activation(CSW[:], zero[0:B, 0:1], ACT.Silu).then_inc(warm, 1)
            act.wait_ge(c_in, 16)
            act.activation(CS[:], CB[:], ACT.Silu).then_inc(mod_act.sem, mod_act.step("silu"))
            act.wait_ge(mod_pe.sem, mod_pe.value(0, "ct"))
            ct = pB[:, 0:B].rearrange("p (o b) -> p o b", o=1).broadcast_to((P, TS, B))
            act.copy(tile3(CT[:]), ct).then_inc(mod_act.sem, mod_act.step("ct"))
            act.wait_ge(vec_in, 16 * 7)
            act.activation(HSh[:, 0:B], zero[:, 0:B], ACT.Identity, bias=sh_v).then_inc(shift_set, 1)
            act.activation(UE[:, 0:1], u_v, ACT.Exp).then_inc(u_act.sem, u_act.step("u"))
            act.activation(UE[:, 1:2], u_v, ACT.Exp, scale=-1.0).then_inc(u_act.sem, u_act.step("iu"))

            def first_stage(q):
                act.wait_ge(ln_pe.sem, ln_pe.value(q, "t"))
                act.activation(HSh[:, bass.ds(q * QN + B, QN)], pA[:], ACT.Identity, bias=b1_v,
                                           scale=g1_v).then_inc(ln_act.sem, ln_act.step("hs"))
                act.wait_ge(ln_pe.sem, ln_pe.value(q, "k"))
                act.copy(K[:, cols(q, QN)], pH1[0][:]).then_inc(ln_act.sem, ln_act.step("k"))
                if q == 0:
                    act.wait_ge(dk_dve.sem, dk_dve.value(0, "clip"))
                    act.activation(Q[:, 0:GN], YS[:, 0:GN], ACT.Exp, bias=w_v).then_inc(q_act.sem, q_act.step("first"))
                act.activation(H3T[:, cols(q, QN)], pH1[0][:], ACT.Abs).then_inc(ln_act.sem, ln_act.step("abs_k"))
                act.wait_ge(ln_pe.sem, ln_pe.value(q, "v"))
                act.copy(V[:, cols(q, QN)], pH3[0][:]).then_inc(ln_act.sem, ln_act.step("v"))
                act.wait_ge(ln_pe.sem, ln_pe.value(q, "r"))
                act.activation(SR[:, cols(q, QN)], pH1[1][:], ACT.Tanh, scale=0.5).then_inc(ln_act.sem, ln_act.step("r"))

            def exponentials(q):
                c0, c1 = difference_cols(q)
                act.wait_ge(dk_pool.sem, dk_pool.value(q, "clip"))
                act.activation(Q[:, c0:c1], YS[:, c0:c1], ACT.Exp, bias=w_v).then_inc(q_act.sem, q_act.step(("q", q)))

            for q in range(NQ):
                first_stage(q)
                if q > 0:
                    exponentials(q - 1)
            exponentials(NQ - 1)

            act.wait_ge(kmax_dve.sem, kmax_dve.value(0, "flag"))
            outside = act.value_load(FLAG[0:1, 0:1])
            with act.If(outside > 0):
                with act.Fori(0, T) as t:
                    act.wait_ge(slow_dve, t * 17 + 7)
                    act.activation(sE[:], sD[:], ACT.Exp).then_inc(slow_act, 1)
                    act.wait_ge(slow_dve, t * 17 + 16)
                    act.activation(sL[:], sBB[:], ACT.Ln).then_inc(slow_act, 1)

            def a_hs2(g):
                if not first(g):
                    act.wait_ge(a_pe.sem, a_pe.value(g - 1, "kk1"))
                    act.copy(HS2[:, 0:B], HS2[:, GN:GN + B]).then_inc(a_act.sem, a_act.step("carry"))
                    act.wait_ge(a_act.sem, a_act.value(g, "carry"))
                else:
                    act.activation(HS2[:, 0:B], zero[:, 0:B], ACT.Identity, bias=sh_v) \
                        .then_inc(a_act.sem, a_act.step("carry"))
                act.wait_ge(a_pe.sem, a_pe.value(g, "t_x2"))
                act.activation(HS2[:, B:B + GN], pA[:, 0:GN], ACT.Identity, bias=b2_v, scale=g2_v).then_inc(a_act.sem, a_act.step("hs2"))

            def a_mix(g, i):
                if i == 0:
                    if not first(g):
                        act.wait_ge(g_dve.sem, g_dve.value(g - 1, "t1"))
                    act.wait_ge(a_pe.sem, a_pe.value(g, "rr"))
                    act.activation(RRT[:], pA[:, 0:GN], ACT.Tanh, scale=0.5).then_inc(a_act.sem, a_act.step("rr"))
                half = slice(i * FM * GN // 2, (i + 1) * FM * GN // 2)
                act.wait_ge(a_pe.sem, a_pe.value(g, f"kk{i}"))
                act.activation(KR[:, half], (pB, pC)[i][:], ACT.Relu).then_inc(a_act.sem, a_act.step(f"re{i}"))
                act.wait_ge(a_act.sem, a_act.value(g, f"re{i}"))
                kq = KQ[:, i * FM // 2:(i + 1) * FM // 2, :].rearrange("p m n -> p (m n)")
                act.activation(kq, KR[:, half], ACT.Square).then_inc(a_act.sem, a_act.step(f"sq{i}"))

            def a_h3(g):
                act.wait_ge(g_pe.sem, g_pe.value(g, "t_h3"))
                act.copy(H3S[:], pB[:, 0:GN]).then_inc(g_act.sem, g_act.step("h3s"))
                act.copy(H3T[:, cols(g)], pB[:, 0:GN]).then_inc(g_act.sem, g_act.step("h3t"))

            def a_gate(g):
                act.wait_ge(g_dve.sem, g_dve.value(g, "df"))
                act.activation(TH[:], DF[:], ACT.Tanh, scale=0.5).then_inc(g_act.sem, g_act.step("th"))

            def silu(g, e):
                if e >= 2:
                    act.wait_ge(e_dve.sem, e_dve.value(g, f"m{e - 2}.{HM - 1}"))
                elif not first(g):
                    act.wait_ge(e_dve.sem, e_dve.value(g - 1, f"m{E - 2 + e}.{HM - 1}"))
                act.wait_ge(h_pe.sem, h_pe.value(g, e))
                act.activation(SL[:, e % 2], pH1[e % 2][:], ACT.Silu).then_inc(s_act.sem, s_act.step(e))

            def weigh(g, e):
                if e >= 2:
                    act.wait_ge(e_pool.sem, e_pool.value(g, f"a{max(e - 2, 1)}"))
                elif not first(g):
                    act.wait_ge(e_pool.sem, e_pool.value(g - 1, f"a{E - 2 + e}"))
                act.wait_ge(p_pe.sem, p_pe.value(g, e))
                if e == 0:
                    act.wait_ge(we_dve.sem, we_dve.value(g, "we"))
                for n in range(GT):
                    act.activation(YW[:, e % 2, n], pY[:, n * C:(n + 1) * C], ACT.Copy, scale=WE[:, n, e:e + 1]) \
                        .then_inc(w_act.sem, w_act.step((e, n)))

            def turn(t):
                _, att, gate, late = groups(t)
                for slot in range(SLOTS):
                    if slot == 3 and gate is not None:
                        a_h3(gate)
                    if slot == 6 and gate is not None:
                        a_gate(gate)
                    if slot == 7 and att is not None:
                        a_hs2(att)
                    if slot == 8 and att is not None:
                        a_mix(att, 0)
                    if slot == 9 and att is not None:
                        a_mix(att, 1)
                    g, e = expert(t, slot // 2) if slot % 2 else ahead(t, slot // 2)
                    if g is not None:
                        if slot % 2:
                            weigh(g, e)
                        else:
                            silu(g, e)

            for t in range(1, FIRST_FULL):
                turn(t)
            with act.Fori(FIRST_FULL, NG) as t:
                turn(t)
            for t in range(NG, TURNS):
                turn(t)

        @block.vector
        def _(dve):
            def wait_apart(semaphore, value):
                dve.wait_ge(semaphore, value)
                if not isinstance(value, int):
                    dve.sem_inc(passed, 1)

            def modulation():
                dve.wait_ge(mod_pe.sem, mod_pe.value(0, "first"))
                dve.tensor_scalar(MOD[:, 1, :], pH3[1][:, C:2 * C], 1.0, None, ALU.add) \
                    .then_inc(mod_dve.sem, mod_dve.step("sa"))
                dve.tensor_copy(MOD[:, 0, :], pH3[1][:, 0:C]).then_inc(mod_dve.sem, mod_dve.step("ca"))
                dve.wait_ge(mod_dve.sem, mod_dve.value(0, "ca"))

            def rest_of_modulation():
                dve.wait_ge(mod_pe.sem, mod_pe.value(0, "rest"))
                dve.tensor_copy(MOD[:].rearrange("p k c -> p (k c)")[:, 2 * C:], pY[:]) \
                    .then_inc(mod_dve.sem, mod_dve.step("rest"))
                dve.wait_ge(mod_dve.sem, mod_dve.value(0, "rest"))
                dve.tensor_scalar(MOD[:, 4, :], MOD[:, 4, :], 1.0, None, ALU.add).then_inc(mod_dve.sem, mod_dve.step("cb"))
                gates = MOD[:].rearrange("p (i k) c -> p i k c", i=2)[:, :, 2, :]
                dve.tensor_scalar(GSG[:], gates, 0.0, 2.0, ALU.is_ge, ALU.mult).then_inc(mod_dve.sem, mod_dve.step("sign"))
                dve.scalar_tensor_tensor(GAB[:], gates, -1.0, gates, ALU.mult, ALU.max).then_inc(mod_dve.sem, mod_dve.step("abs"))
                dve.wait_ge(mod_dve.sem, mod_dve.value(0, "abs"))
                dve.tensor_scalar(GAB[:], GAB[:], MIN_GATE, None, ALU.max).then_inc(mod_dve.sem, mod_dve.step("size"))
                dve.wait_ge(mod_dve.sem, mod_dve.value(0, "size"))
                dve.scalar_tensor_tensor(GAB[:], GSG[:], -1.0, GAB[:], ALU.add, ALU.mult).then_inc(mod_dve.sem, mod_dve.step("gate"))

            def part_stats(q, k, src, counter):
                for n in range(QT):
                    if k == 1:
                        dve.wait_ge(ln_dve.sem, ln_dve.value(q, ("h", n)))
                    dve.bn_stats(STAT[:, k, n, :], src(n)).then_inc(counter.sem, counter.step(("st", n)))
                    yield
                for n in range(QT):
                    dve.wait_ge(counter.sem, counter.value(q, ("st", n)))
                    dve.bn_aggr(MV[:, k, n, :], STAT[:, k, n, :]).then_inc(counter.sem, counter.step(("ag", n)))
                    yield
                dve.wait_ge(counter.sem, counter.value(q, ("ag", QT - 1)))
                dve.tensor_scalar(VE[:, k, :], MV[:, k, :, 1], LN_EPS, None, ALU.add) \
                    .then_inc(counter.sem, counter.step("eps"))
                yield

            def stats(q):
                yield from part_stats(q, 0, lambda n: X[:, q * QT + n, :], ln_dve)

            def modulated(q):
                dve.wait_ge(ln_dve.sem, ln_dve.value(q, "eps"))
                for n in range(QT):
                    dve.scalar_tensor_tensor(XN[:, n, :], X[:, q * QT + n, :], MV[:, 0, n, 0:1], MOD[:, 1, :],
                                             ALU.subtract, ALU.mult).then_inc(ln_dve.sem, ln_dve.step(("scaled", n)))
                    yield
                dve.wait_ge(ln_pool.sem, ln_pool.value(q, "rs"))
                for n in range(QT):
                    dve.wait_ge(ln_dve.sem, ln_dve.value(q, ("scaled", n)))
                    dve.scalar_tensor_tensor(H[:, q * QT + n, :], XN[:, n, :], RS[:, 0, n:n + 1], MOD[:, 0, :],
                                             ALU.mult, ALU.add).then_inc(ln_dve.sem, ln_dve.step(("h", n)))
                    yield
                yield from part_stats(q, 1, lambda n: H[:, q * QT + n, :], ln2_dve)

            def normed(q):
                dve.wait_ge(ln2_pool.sem, ln2_pool.value(q, "rs"))
                if not first(q):
                    dve.wait_ge(ln_pe.sem, ln_pe.value(q - 1, "t"))
                for n in range(QT):
                    dve.tensor_scalar(HN[:, n, :], H[:, q * QT + n, :], MV[:, 1, n, 0:1], RS[:, 1, n:n + 1],
                                      ALU.subtract, ALU.mult).then_inc(ln2_dve.sem, ln2_dve.step(("n", n)))
                    yield

            def first_difference():
                dve.wait_ge(ln_act.sem, ln_act.value(0, "k"))
                dve.tensor_tensor(YS[:, 0:GN], K[:, 0:GN], K[:, B:GN + B], ALU.subtract) \
                    .then_inc(dk_dve.sem, dk_dve.step("dk"))
                dve.wait_ge(dk_dve.sem, dk_dve.value(0, "dk"))
                dve.tensor_scalar(YS[:, 0:GN], YS[:, 0:GN], -2.0 * K_SAFE, 2.0 * K_SAFE, ALU.max, ALU.min) \
                    .then_inc(dk_dve.sem, dk_dve.step("clip"))

            def largest_k(q):
                dve.wait_ge(ln_act.sem, ln_act.value(q, "abs_k"))
                dve.tensor_reduce(KM[:, q:q + 1], H3T[:, q * QN:(q + 1) * QN], AX_X, ALU.max) \
                    .then_inc(kmax_dve.sem, kmax_dve.step(("km", q)))
                yield

            def range_check():
                dve.scalar_tensor_tensor(VA[:], VEC[:, 0:2], -1.0, VEC[:, 0:2], ALU.mult, ALU.max) \
                    .then_inc(kmax_dve.sem, kmax_dve.step("wu"))
                yield
                dve.wait_ge(kmax_dve.sem, kmax_dve.value(0, "wu"))
                dve.tensor_scalar(KM[:, NQ:NQ + 2], VA[:], K_SAFE / W_SAFE, None, ALU.mult) \
                    .then_inc(kmax_dve.sem, kmax_dve.step("um"))
                yield
                dve.wait_ge(kmax_dve.sem, kmax_dve.value(0, "um"))
                dve.tensor_reduce(KMM[:], KM[:], AX_X, ALU.max).then_inc(kmax_dve.sem, kmax_dve.step("max"))
                yield

            def rest_of_first_stage():
                dve.wait_ge(x_rest, 16 * (NT - QT))
                yield from stats(1)
                for q in range(1, NQ):
                    yield from modulated(q)
                    if q + 1 < NQ:
                        yield from stats(q + 1)
                    yield from largest_k(q - 1)
                    yield from normed(q)

            dve.memset(REC[:, 0, :, :], 0.0).then_inc(wkv_start.sem, wkv_start.step("z"))
            dve.wait_ge(wkv_start.sem, wkv_start.value(0, "z"))
            dve.memset(REC[:, 0, RG, :], 1.0).then_inc(wkv_start.sem, wkv_start.step("g"))
            dve.memset(REC[:, 0, RBB, :], 1.0).then_inc(wkv_start.sem, wkv_start.step("bb"))
            dve.memset(REC[:, 0, RINV, :], 1e30).then_inc(wkv_start.sem, wkv_start.step("inv"))
            dve.wait_ge(wkv_start.sem, wkv_start.value(0, "inv"))

            def wkv_begin(g):
                if not first(g):
                    dve.wait_ge(y_dve.sem, y_dve.value(g - 1, "eb"))
                dve.tensor_copy(REC[:, 0:GS, RQ, :], tile3(Q[:, cols(g)])).then_inc(wkv.sem, wkv.step("q"))
                if first(g):
                    dve.memset(AA[:, 0, :], 0.0).then_inc(wkv.sem, wkv.step("carry"))
                else:
                    dve.tensor_copy(REC[:, 0, RG:, :], REC[:, GS, RG:, :]).then_inc(wkv.sem, wkv.step("carry"))
                dve.wait_ge(wkv.sem, wkv.value(g, "carry"))

            def wkv_steps(g, s0, s1, side):
                for s in range(s0, s1):
                    if s > 0:
                        dve.wait_ge(wkv.sem, wkv.value(g, ("g", s - 1)))
                    u2 = REC[:, s, RU:RU + 1, :].broadcast_to((P, 2, B))
                    dve.scalar_tensor_tensor(REC[:, s + 1, RR_:RBB + 1, :], u2, 1.0,
                                                      REC[:, s, RQ:RG + 1, :], ALU.add, ALU.mult).then_inc(wkv.sem, wkv.step(("rb", s)))
                    next(side, None)
                    dve.wait_ge(wkv.sem, wkv.value(g, ("rb", s)))
                    dve.scalar_tensor_tensor(REC[:, s + 1, RU, :], REC[:, s + 1, RR_, :], R_CAP,
                                                      REC[:, s + 1, RBB, :], ALU.min, ALU.mult).then_inc(wkv.sem, wkv.step(("u", s)))
                    dve.reciprocal(REC[:, s + 1, RINV, :], REC[:, s + 1, RR_, :]).then_inc(wkv.sem, wkv.step(("inv", s)))
                    next(side, None)
                    dve.wait_ge(wkv.sem, wkv.value(g, ("inv", s)))
                    dve.tensor_scalar(REC[:, s + 1, RG, :], REC[:, s + 1, RINV, :], 1.0 / R_CAP, 1.0,
                                               ALU.max, ALU.min).then_inc(wkv.sem, wkv.step(("g", s)))
                    next(side, None)

            def y_records(g):
                if first(g):
                    dve.wait_ge(u_act.sem, u_act.value(0, "iu"))
                    dve.wait_ge(ln_act.sem, ln_act.value(NQ - 1, "r"))
                else:
                    dve.wait_ge(y_dve.sem, y_dve.value(g - 1, "att"))
                    dve.wait_ge(y_pool.sem, y_pool.value(g - 1, "den"))
                dve.wait_ge(wkv.sem, wkv.value(g, ("g", GS - 1)))
                dve.tensor_scalar(F1[:], REC[:, 0:GS, RR_, :], 1.0, None, ALU.min) \
                    .then_inc(y_dve.sem, y_dve.step("f1"))
                dve.tensor_scalar(F2[:], REC[:, 0:GS, RINV, :], 1.0, None, ALU.min) \
                    .then_inc(y_dve.sem, y_dve.step("f2"))
                dve.tensor_scalar(E1[:], REC[:, 0:GS, RR_, :], UE[:, 1:2], 1.0, ALU.mult, ALU.min) \
                    .then_inc(y_dve.sem, y_dve.step("e1"))
                dve.tensor_scalar(E2[:], REC[:, 0:GS, RINV, :], UE[:, 0:1], 1.0, ALU.mult, ALU.min) \
                    .then_inc(y_dve.sem, y_dve.step("e2"))
                dve.wait_ge(y_dve.sem, y_dve.value(g, "e1"))
                dve.tensor_tensor(EB[:], E1[:], REC[:, 0:GS, RBB, :], ALU.mult).then_inc(y_dve.sem, y_dve.step("eb"))

            def y_scan(g):
                dve.wait_ge(y_dve.sem, y_dve.value(g, "f2"))
                dve.tensor_tensor(F2V[:], F2[:], tile3(V[:, cols(g)]), ALU.mult).then_inc(y_dve.sem, y_dve.step("f2v"))
                yield
                dve.wait_ge(y_dve.sem, y_dve.value(g, "f2v"))
                for b in range(B):
                    dve.tensor_tensor_scan(AA[:, 1:, b], F1[:, :, b], F2V[:, :, b], AA[:, 0, b:b + 1],
                                           ALU.mult, ALU.add).then_inc(y_dve.sem, y_dve.step(("aa", b)))
                    if b % 2:
                        yield
                dve.wait_ge(y_dve.sem, y_dve.value(g, ("aa", B - 1)))
                dve.tensor_tensor(EAA[:], E1[:], AA[:, 0:GS, :], ALU.mult).then_inc(y_dve.sem, y_dve.step("ea"))
                yield

            def y_att(g):
                dve.wait_ge(y_dve.sem, y_dve.value(g, "ea"))
                dve.tensor_copy(AA[:, 0, :], AA[:, GS, :]).then_inc(y_dve.sem, y_dve.step("carry"))
                dve.wait_ge(y_pool.sem, y_pool.value(g, "e2v"))
                dve.tensor_tensor(NUM[:], EAA[:], E2V[:], ALU.add).then_inc(y_dve.sem, y_dve.step("num"))
                yield
                dve.wait_ge(y_pool.sem, y_pool.value(g, "den"))
                piece = GS // RP
                for i in range(RP):
                    dve.reciprocal(RDEN[:, i * piece:(i + 1) * piece, :], DEN[:, i * piece:(i + 1) * piece, :]) \
                        .then_inc(y_dve.sem, y_dve.step(("rden", i)))
                    yield
                dve.wait_ge(y_dve.sem, y_dve.value(g, ("rden", RP - 1)))
                dve.tensor_tensor(tile3(YY[:]), NUM[:], RDEN[:], ALU.mult).then_inc(y_dve.sem, y_dve.step("y"))
                yield
                wait_apart(y_dve.sem, y_dve.value(g, "y"))
                with dve.If(outside > 0):
                    dve.tensor_copy(YY[:], YS[:, cols(g)]).then_inc(slow_copy, 1)
                    wait_apart(slow_copy, g + 1)
                if not first(g):
                    dve.wait_ge(a_pe.sem, a_pe.value(g - 1, "t_att"))
                dve.scalar_tensor_tensor(ATT[:], SR[:, cols(g)], 1.0, YY[:], ALU.add, ALU.mult) \
                    .then_inc(y_dve.sem, y_dve.step("att"))
                yield

            def norm(g, src, k, dve_steps, stat, aggr, eps):
                for n in range(GT):
                    dve.bn_stats(STAT[:, k, n, :], src(n)).then_inc(dve_steps.sem, dve_steps.step((stat, n)))
                    yield
                for n in range(GT):
                    wait_apart(dve_steps.sem, dve_steps.value(g, (stat, n)))
                    dve.bn_aggr(MV[:, k, n, :], STAT[:, k, n, :]).then_inc(dve_steps.sem, dve_steps.step((aggr, n)))
                    yield
                dve.wait_ge(dve_steps.sem, dve_steps.value(g, (aggr, GT - 1)))
                dve.tensor_scalar(VE[:, k, 0:GT], MV[:, k, 0:GT, 1], LN_EPS, None, ALU.add).then_inc(dve_steps.sem, dve_steps.step(eps))
                yield

            def xr(g):
                return lambda n: X[:, bass.ds(g * GT + n, 1), :].rearrange("p o c -> p (o c)")

            def a_x1(g):
                if not first(g):
                    dve.wait_ge(g_dve.sem, g_dve.value(g - 1, "xa"))
                dve.wait_ge(a_pe.sem, a_pe.value(g, "t_att"))
                pa = pA[:, 0:GN].rearrange("p (n c) -> p n c", c=C)
                dve.scalar_tensor_tensor(X1[:], pa, 0.5, H[:, ranks(g), :], ALU.mult, ALU.add).then_inc(a_dve.sem, a_dve.step("x1"))
                yield
                wait_apart(a_dve.sem, a_dve.value(g, "x1"))
                yield from norm(g, lambda n: X1[:, n, :], 0, a_dve, "st", "ag", "eps")

            def a_x2(g):
                dve.wait_ge(a_pool.sem, a_pool.value(g, "rs"))
                for n in range(GT):
                    dve.tensor_scalar(X2N[:, n, :], X1[:, n, :], MV[:, 0, n, 0:1], RS[:, 0, n:n + 1],
                                                 ALU.subtract, ALU.mult).then_inc(a_dve.sem, a_dve.step(("n", n)))
                    yield

            def a_mixed(g):
                dve.wait_ge(a_pe.sem, a_pe.value(g, "kv"))
                dve.wait_ge(a_act.sem, a_act.value(g, "rr"))
                kv = pA[:, 0:GN].rearrange("p (n c) -> p n c", c=C)
                dve.scalar_tensor_tensor(T1[:], RRT[:].rearrange("p (n c) -> p n c", c=C), 1.0, kv,
                                                    ALU.add, ALU.mult).then_inc(g_dve.sem, g_dve.step("t1"))
                yield
                dve.wait_ge(g_dve.sem, g_dve.value(g, "t1"))
                if not first(g):
                    dve.wait_ge(g_pool.sem, g_pool.value(g - 1, "xg"))
                dve.scalar_tensor_tensor(XA[:], T1[:], 0.5, X1[:], ALU.mult, ALU.add).then_inc(g_dve.sem, g_dve.step("xa"))
                yield

            def a_stats3(g):
                wait_apart(g_pool.sem, g_pool.value(g, "xr"))
                yield from norm(g, xr(g), 1, g_dve, "st3", "ag3", "eps3")

            def a_n3(g):
                dve.wait_ge(g_dve.sem, g_dve.value(g, "eps3"))
                for n in range(GT):
                    dve.scalar_tensor_tensor(N3[:, n, :], xr(g)(n), MV[:, 1, n, 0:1], MOD[:, 4, :],
                                             ALU.subtract, ALU.mult).then_inc(g_dve.sem, g_dve.step(("n3", n)))
                    yield

            def a_h3(g):
                dve.wait_ge(g_pool.sem, g_pool.value(g, "rs3"))
                dve.wait_ge(g_dve.sem, g_dve.value(g, ("n3", GT - 1)))
                if not first(g):
                    dve.wait_ge(g_pe.sem, g_pe.value(g - 1, "t_h3"))
                for n in range(GT):
                    dve.scalar_tensor_tensor(H3[:, n, :], N3[:, n, :], RS[:, 1, n:n + 1], MOD[:, 3, :],
                                             ALU.mult, ALU.add).then_inc(g_dve.sem, g_dve.step(("h3", n)))
                    yield

            def a_top2(g):
                dve.wait_ge(g_pe.sem, g_pe.value(g, "logits"))
                dve.tensor_copy(LG[:], pC[:, 0:GT * E].rearrange("p (n e) -> p n e", e=E)).then_inc(g_dve.sem, g_dve.step("lg"))
                yield
                wait_apart(g_dve.sem, g_dve.value(g, "lg"))
                for n in range(GT):
                    dve.max(MX[:, n, :], LG[:, n, :]).then_inc(g_dve.sem, g_dve.step(("mx", n)))
                    yield
                wait_apart(g_dve.sem, g_dve.value(g, ("mx", GT - 1)))
                for n in range(GT):
                    dve.max_index(IX[:, n, :], MX[:, n, :], LG[:, n, :]).then_inc(g_dve.sem, g_dve.step(("ix", n)))
                    yield
                dve.tensor_tensor(DF[:], MX[:, :, 0], MX[:, :, 1], ALU.subtract).then_inc(g_dve.sem, g_dve.step("df"))
                yield
                dve.wait_ge(g_dve.sem, g_dve.value(g, ("ix", GT - 1)))
                dve.tensor_copy(IXF[:], IX[:, :, 0:2]).then_inc(g_dve.sem, g_dve.step("ixf"))
                yield

            def a_weights(g):
                dve.wait_ge(g_act.sem, g_act.value(g, "th"))
                dve.tensor_scalar(PR[:, :, 0], TH[:], 0.5, 0.5, ALU.mult, ALU.add).then_inc(g_dve.sem, g_dve.step("p1"))
                yield
                dve.tensor_scalar(PR[:, :, 1], TH[:], -0.5, 0.5, ALU.mult, ALU.add).then_inc(g_dve.sem, g_dve.step("p2"))
                yield
                dve.wait_ge(g_dve.sem, g_dve.value(g, "p2"))
                for n in range(GT):
                    for k in range(2):
                        dve.tensor_scalar(WA[:, k, n, :], IOTA[:], IXF[:, n, k:k + 1], PR[:, n, k:k + 1],
                                                     ALU.is_equal, ALU.mult).then_inc(g_dve.sem, g_dve.step(("w", n, k)))
                        yield
                dve.wait_ge(g_dve.sem, g_dve.value(g, ("w", 1, 1)))
                dve.tensor_tensor(WT[:], WA[:, 0], WA[:, 1], ALU.add).then_inc(g_dve.sem, g_dve.step("wt"))
                yield

            def weights_in(g):
                if not first(g):
                    dve.wait_ge(w_act.sem, w_act.value(g - 1, (E - 1, GT - 1)))
                dve.wait_ge(g_dve.sem, g_dve.value(g, "wt"))
                dve.tensor_copy(WE[:], WT[:]).then_inc(we_dve.sem, we_dve.step("we"))
                yield

            def hidden(g, e):
                if e >= 2:
                    dve.wait_ge(p_pe.sem, p_pe.value(g, e - 2))
                elif not first(g):
                    dve.wait_ge(p_pe.sem, p_pe.value(g - 1, E - 2 + e))
                dve.wait_ge(s_act.sem, s_act.value(g, e))
                for m in range(HM):
                    part = slice(m * GN, (m + 1) * GN)
                    dve.tensor_tensor(HT[:, e % 2, m, :], SL[:, e % 2, part], pH3[e % 2][:, part], ALU.mult) \
                        .then_inc(e_dve.sem, e_dve.step(f"m{e}.{m}"))
                    yield

            def side_work(t, slot):
                _, att, gate, _ = groups(t)
                g, e = expert(t, slot // 2)
                if slot % 2 == 0 and g is not None:
                    yield from hidden(g, e)
                if att is not None:
                    if slot == 0:
                        yield from y_scan(att)
                    if slot == 1:
                        yield from y_att(att)
                    if slot == 4:
                        yield from a_x1(att)
                    if slot == 6:
                        yield from a_x2(att)
                    if slot == 12:
                        yield from a_mixed(att)
                    if slot == 14:
                        yield from a_stats3(att)
                        yield from a_n3(att)
                if gate is not None:
                    if slot == 1:
                        yield from a_h3(gate)
                    if slot == 5:
                        yield from a_top2(gate)
                    if slot == 7:
                        yield from a_weights(gate)
                        yield from weights_in(gate)

            def turn(t):
                rec, att, _, _ = groups(t)
                if att is not None:
                    y_records(att)
                if rec is not None:
                    wkv_begin(rec)
                side = iter(())
                for slot in range(SLOTS):
                    side = chain(side, side_work(t, slot))
                    if rec is not None:
                        wkv_steps(rec, slot * GS // SLOTS, (slot + 1) * GS // SLOTS, side)
                    else:
                        for _ in side:
                            pass
                for _ in side:
                    pass

            def general_path():
                count = [0]
                per = 17
                dve.memset(sPP[:], PP_START)
                dve.memset(sAA[:], 0.0)
                dve.memset(sBB[:], 1.0).then_inc(slow_copy, 1)
                dve.wait_ge(slow_copy, 1)
                dve.sem_clear(slow_copy)
                with dve.Fori(0, T) as t:
                    kt, vt = K[:, cols(t, B)], V[:, cols(t, B)]

                    def link(ins):
                        count[0] += 1
                        ins.then_inc(slow_dve, 1)
                        if count[0] == per:
                            wait_apart(slow_dve, t * per + count[0])
                        else:
                            dve.wait_ge(slow_dve, t * per + count[0])

                    link(dve.tensor_tensor(sM[:], sPP[:], kt, ALU.max))
                    link(dve.scalar_tensor_tensor(sP[:], kt, u_v, sPP[:], ALU.add, ALU.max))
                    link(dve.tensor_tensor(sD[:, 0], sPP[:], sP[:], ALU.subtract))
                    link(dve.scalar_tensor_tensor(sD[:, 1], kt, u_v, sP[:], ALU.add, ALU.subtract))
                    link(dve.tensor_tensor(sD[:, 2], sPP[:], sM[:], ALU.subtract))
                    link(dve.tensor_tensor(sD[:, 3], kt, sM[:], ALU.subtract))
                    link(dve.tensor_scalar(sT[:, 8], sM[:], w_v, None, ALU.add))
                    dve.wait_ge(slow_act, t * 2 + 1)
                    link(dve.tensor_tensor(sT[:, 0:2], sE[:, 0:4:2], sAA[:].rearrange("p (o b) -> p o b", o=1)
                                           .broadcast_to((P, 2, B)), ALU.mult))
                    link(dve.tensor_tensor(sT[:, 2:4], sE[:, 1:4:2], vt.rearrange("p (o b) -> p o b", o=1)
                                           .broadcast_to((P, 2, B)), ALU.mult))
                    link(dve.tensor_tensor(sT[:, 4:6], sE[:, 0:4:2], sBB[:].rearrange("p (o b) -> p o b", o=1)
                                           .broadcast_to((P, 2, B)), ALU.mult))
                    link(dve.tensor_tensor(sT[:, 0], sT[:, 0], sT[:, 2], ALU.add))
                    link(dve.tensor_tensor(sAA[:], sT[:, 1], sT[:, 3], ALU.add))
                    link(dve.tensor_tensor(sT[:, 6], sT[:, 4], sE[:, 1], ALU.add))
                    link(dve.reciprocal(sT[:, 7], sT[:, 6]))
                    link(dve.tensor_tensor(YS[:, cols(t, B)], sT[:, 0], sT[:, 7], ALU.mult))
                    link(dve.tensor_tensor(sBB[:], sT[:, 5], sE[:, 3], ALU.add))
                    dve.wait_ge(slow_act, t * 2 + 2)
                    link(dve.tensor_tensor(sPP[:], sT[:, 8], sL[:], ALU.add))
                    assert count[0] == per

            dve.wait_ge(pool_const.sem, pool_const.value(0, "rest"))
            dve.wait_ge(x_first, 16 * QT)
            for _ in stats(0):
                pass
            modulation()
            for _ in chain(modulated(0), normed(0)):
                pass
            rest_of_modulation()
            first_difference()
            dve.wait_ge(q_act.sem, q_act.value(0, "first"))
            wkv_begin(0)
            side = rest_of_first_stage()
            wkv_steps(0, 0, GS, side)
            for _ in chain(side, largest_k(NQ - 1), range_check()):
                pass
            dve.wait_ge(kmax_all, 1)
            dve.tensor_scalar(FLAG[:], KMA[:], K_SAFE, None, ALU.is_gt).then_inc(kmax_dve.sem, kmax_dve.step("flag"))
            dve.wait_ge(q_act.sem, q_act.value(0, ("q", NQ - 1)))
            dve.wait_ge(kmax_dve.sem, kmax_dve.value(0, "flag"))
            outside = dve.value_load(FLAG[0:1, 0:1])
            with dve.If(outside > 0):
                general_path()
            for t in range(1, FIRST_FULL):
                turn(t)
            with dve.Fori(FIRST_FULL, NG) as t:
                turn(t)
            for t in range(NG, TURNS):
                turn(t)

        @block.tensor
        def _(pe):
            pe.wait_ge(pool_const.sem, pool_const.value(0, "ident"))
            pe.wait_ge(mod_act.sem, mod_act.value(0, "silu"))
            pe.transpose(pB[:, 0:B], CS[:], ident[0:B, 0:B]).then_inc(mod_pe.sem, mod_pe.step("ct"))
            pe.wait_ge(mod_act.sem, mod_act.value(0, "ct"))
            pe.wait_ge(wmod_first, 16)
            pe.matmul(pH3[1][:, 0:2 * C], CT[:], WMOD[:, 0:2 * C], start=True, stop=True) \
                .then_inc(mod_pe.sem, mod_pe.step("first"))
            pe.wait_ge(wmod_rest, 16)
            pe.matmul(pY[:], CT[:], WMOD[:, 2 * C:], start=True, stop=True).then_inc(mod_pe.sem, mod_pe.step("rest"))
            pe.wait_ge(wkvr_in, 48)
            pe.wait_ge(shift_set, 1)

            def first_stage(q):
                if not first(q):
                    pe.wait_ge(ln_act.sem, ln_act.value(q - 1, "r"))
                for n in range(QT):
                    pe.wait_ge(ln2_dve.sem, ln2_dve.value(q, ("n", n)))
                    ins = pe.transpose(pA[:, n * P:(n + 1) * P], HN[:, n, :], ident[:])
                ins.then_inc(ln_pe.sem, ln_pe.step("t"))
                pe.wait_ge(ln_act.sem, ln_act.value(q, "hs"))
                for w, p, name in ((WK, pH1[0], "k"), (WV, pH3[0], "v"), (WR, pH1[1], "r")):
                    pe.matmul(p[:], w[:], HSh[:, cols(q, QN)], start=True, stop=True).then_inc(ln_pe.sem, ln_pe.step(name))

            first_stage(0)
            with pe.Fori(1, NQ) as q:
                first_stage(q)
            for s in (w1_in, w3_in, w2_in):
                pe.wait_ge(s, 16)
            pe.wait_ge(mix_in, 16 * 4)
            pe.wait_ge(mod_dve.sem, mod_dve.value(0, "rest"))
            pe.wait_ge(ln_act.sem, ln_act.value(NQ - 1, "r"))

            def to_tokens(src, dst):
                for n in range(GT):
                    ins = pe.transpose(dst[:, n * P:(n + 1) * P], src(n), ident[:])
                return ins

            def a_att(g):
                if not first(g):
                    pe.wait_ge(g_dve.sem, g_dve.value(g - 1, "t1"))
                pe.wait_ge(y_dve.sem, y_dve.value(g, "att"))
                to_tokens(lambda n: ATT[:, n * P:(n + 1) * P], pA).then_inc(a_pe.sem, a_pe.step("t_att"))

            def a_x2(g):
                pe.wait_ge(a_dve.sem, a_dve.value(g, ("n", GT - 1)))
                to_tokens(lambda n: X2N[:, n, :], pA).then_inc(a_pe.sem, a_pe.step("t_x2"))

            def a_mix(g):
                pe.wait_ge(a_act.sem, a_act.value(g, "hs2"))
                for n in range(GT):
                    ins = pe.matmul(pA[:, n * C:(n + 1) * C], HS2[:, n * P:(n + 1) * P], WCR[:], start=True, stop=True)
                ins.then_inc(a_pe.sem, a_pe.step("rr"))
                if not first(g):
                    pe.wait_ge(g_dve.sem, g_dve.value(g - 1, "lg"))
                for i, p in enumerate((pB, pC)):
                    for m in range(FM // 2):
                        f = i * FM // 2 + m
                        ins = pe.matmul(p[:, m * GN:(m + 1) * GN], WCK[:, f * P:(f + 1) * P], HS2[:, 0:GN],
                                        start=True, stop=True)
                    ins.then_inc(a_pe.sem, a_pe.step(f"kk{i}"))

            def a_kv(g):
                pe.wait_ge(a_act.sem, a_act.value(g, "rr"))
                for n in range(GT):
                    for f in range(FM):
                        if n == 0 and f in (0, FM // 2):
                            pe.wait_ge(a_act.sem, a_act.value(g, "sq0" if f == 0 else "sq1"))
                        ins = pe.matmul(pA[:, n * C:(n + 1) * C], KQ[:, f, n * P:(n + 1) * P], WCV[:, f, :],
                                        start=(f == 0), stop=(f == FM - 1))
                ins.then_inc(a_pe.sem, a_pe.step("kv"))

            def a_h3(g):
                pe.wait_ge(g_dve.sem, g_dve.value(g, ("h3", GT - 1)))
                to_tokens(lambda n: H3[:, n, :], pB).then_inc(g_pe.sem, g_pe.step("t_h3"))

            def a_logits(g):
                pe.wait_ge(g_act.sem, g_act.value(g, "h3s"))
                for n in range(GT):
                    ins = pe.matmul(pC[:, n * E:(n + 1) * E], H3S[:, n * P:(n + 1) * P], WG[:], start=True, stop=True)
                ins.then_inc(g_pe.sem, g_pe.step("logits"))

            def hidden(g, e):
                if e == 0:
                    pe.wait_ge(g_act.sem, g_act.value(g, "h3t"))
                if e >= 2:
                    pe.wait_ge(e_dve.sem, e_dve.value(g, f"m{e - 2}.{HM - 1}"))
                elif not first(g):
                    pe.wait_ge(e_dve.sem, e_dve.value(g - 1, f"m{E - 2 + e}.{HM - 1}"))
                for w, p in ((W1, pH1[e % 2]), (W3, pH3[e % 2])):
                    for m in range(HM):
                        ins = pe.matmul(p[:, m * GN:(m + 1) * GN], w[:, e, m * P:(m + 1) * P], H3T[:, cols(g)],
                                        start=True, stop=True)
                ins.then_inc(h_pe.sem, h_pe.step(e))

            def project(g, e):
                pe.wait_ge(e_dve.sem, e_dve.value(g, f"m{e}.{HM - 1}"))
                if e >= 1:
                    pe.wait_ge(w_act.sem, w_act.value(g, (e - 1, GT - 1)))
                elif not first(g):
                    pe.wait_ge(w_act.sem, w_act.value(g - 1, (E - 1, GT - 1)))
                for n in range(GT):
                    for m in range(HM):
                        ins = pe.matmul(pY[:, n * C:(n + 1) * C], HT[:, e % 2, m, n * P:(n + 1) * P], W2[:, e, m, :],
                                        start=(m == 0), stop=(m == HM - 1))
                ins.then_inc(p_pe.sem, p_pe.step(e))

            def turn(t):
                _, att, gate, _ = groups(t)
                for slot in range(SLOTS):
                    if slot == 4 and gate is not None:
                        a_logits(gate)
                    if slot == 8 and att is not None:
                        a_mix(att)
                    g, e = expert(t, slot // 2) if slot % 2 else ahead(t, slot // 2)
                    if g is not None:
                        if slot % 2:
                            project(g, e)
                        else:
                            hidden(g, e)
                    if slot == 2 and gate is not None:
                        a_h3(gate)
                    if slot == 3 and att is not None:
                        a_att(att)
                    if slot == 6 and att is not None:
                        a_x2(att)
                    if slot == 10 and att is not None:
                        a_kv(att)

            for t in range(1, FIRST_FULL):
                turn(t)
            with pe.Fori(FIRST_FULL, NG) as t:
                turn(t)
            for t in range(NG, TURNS):
                turn(t)


_INS = ['L0_attn_x', 'L0_attn_time_decay', 'L0_attn_time_first', 'L0_attn_time_shift', 'L0_attn_Wk', 'L0_attn_Wv',
        'L0_attn_Wr', 'L0_attn_Wck', 'L0_attn_Wcv', 'L0_attn_Wcr', 'L0_attn_ln1_g', 'L0_attn_ln1_b', 'L0_attn_ln2_g',
        'L0_attn_ln2_b', 'L0_ffn_w_gate', 'L0_ffn_w1', 'L0_ffn_w3', 'L0_ffn_w2', 'L0_c', 'L0_wmod']
_OUTS = [((8, 256, 128), 'float32')]


def kernel(**inputs):
    import numpy as _np
    import concourse.bacc as _bacc
    from concourse import mybir as _mybir
    from concourse.bass_utils import run_bass_kernel_spmd as _run

    nc = _bacc.Bacc("TRN2", target_bir_lowering=False, num_devices=1)
    arrays, args = {}, []
    for name in _INS:
        a = _np.ascontiguousarray(inputs[name])
        arrays[f"in_{name}_dram"] = a
        args.append(nc.dram_tensor(f"in_{name}_dram", a.shape, _mybir.dt.from_np(a.dtype), kind="ExternalInput").ap())
    for i, (shape, dtype) in enumerate(_OUTS):
        dt = _mybir.dt.from_np(_np.dtype(dtype))
        args.append(nc.dram_tensor(f"out_{i}_dram", shape, dt, kind="ExternalOutput").ap())
    adaln_rwkv_moe(nc, *args)
    r = _run(nc, [arrays], core_ids=[0])
    got = tuple(r.results[0][f"out_{i}_dram"] for i in range(len(_OUTS)))
    return got[0]
```

```python
from contextlib import ExitStack
from itertools import chain

import concourse.bass as bass
from concourse import mybir

F32 = mybir.dt.float32
I32 = mybir.dt.int32
U32 = mybir.dt.uint32
ALU = mybir.AluOpType
ACT = mybir.ActivationFunctionType
AX_X = mybir.AxisListType.X
RMAX = bass.bass_isa.ReduceOp.max

P = 128
LN_EPS = 1e-5
MIN_GATE = 0.25
PP_START = -1e38
R_CAP = 2.0 ** 60
NOTHING = 1e-30
K_SAFE = 12.0
W_SAFE = 16.0


class Steps:

    def __init__(self, sem, names):
        self.sem, self.per = sem, len(names)
        self.at = {n: i + 1 for i, n in enumerate(names)}
        self.now = 0

    def value(self, group, name):
        return group * self.per + self.at[name]

    def step(self, name):
        assert self.at[name] == self.now % self.per + 1, name
        self.now += 1
        return 1


def first(g):
    return isinstance(g, int) and g == 0


def adaln_rwkv_moe(nc, x, time_decay, time_first, time_shift, Wk, Wv, Wr, Wck, Wcv, Wcr,
                   ln1_g, ln1_b, ln2_g, ln2_b, w_gate, w1, w3, w2, c, wmod, out):
    B, T, C = x.shape
    E, _, HID = w1.shape
    assert C == P and P % B == 0
    TS = P // B
    NT = T // TS
    GT = 2
    NG = NT // GT
    GS = GT * TS
    GN = GT * P
    N = B * T
    QT = 4
    NQ = NT // QT
    QN = QT * P
    FM = Wck.shape[1] // P
    HM = HID // P
    SLOTS = 2 * E
    LATE = 3
    FIRST_FULL = 4
    TURNS = NG + 3
    HS = GS // 2
    HALF_N = GN // 2
    RP = 2

    with ExitStack() as ctx:
        def sb(name, shape, dt=F32):
            return ctx.enter_context(nc.sbuf_tensor(name, shape, dt))

        def pb(name):
            return ctx.enter_context(nc.psum_tensor(name, [P, 512], F32))

        def sem(name):
            return ctx.enter_context(nc.semaphore(name))

        def steps(name, names):
            return Steps(sem(name), names)

        X = sb("X", [P, NT, C])
        H = sb("H", [P, NT, C])
        HSh = sb("HSh", [P, B + N])
        K = sb("K", [P, N])
        V = sb("V", [P, N])
        SR = sb("SR", [P, N])
        Q = sb("Q", [P, N + B])
        YS = sb("YS", [P, N])
        H3T = sb("H3T", [P, N])
        W1 = sb("W1", [P, E, HID])
        W3 = sb("W3", [P, E, HID])
        W2 = sb("W2", [P, E, HM, C])
        WK = sb("WK", [P, C])
        WV = sb("WV", [P, C])
        WR = sb("WR", [P, C])
        WCK = sb("WCK", [P, FM * P])
        WCV = sb("WCV", [P, FM, C])
        WCR = sb("WCR", [P, C])
        WG = sb("WG", [P, E])
        WMOD = sb("WMOD", [P, 6 * C])
        CB = sb("CB", [B, C])
        CSW = sb("CSW", [B, 1])
        CS = sb("CS", [B, C])
        CT = sb("CT", [P, P])
        MOD = sb("MOD", [P, 6, C])
        GSG = sb("GSG", [P, 2, C])
        GAB = sb("GAB", [P, 2, C])
        VEC = sb("VEC", [P, 8])
        w_v, u_v, g1_v, b1_v, g2_v, b2_v, sh_v = (VEC[:, i:i + 1] for i in range(7))
        UE = sb("UE", [P, 2])
        ident = sb("ident", [P, P])
        zero = sb("zero", [P, P])
        NHALF = sb("NHALF", [P, QT])
        IOTA = sb("IOTA", [P, E])
        STAT = sb("STAT", [P, 2, QT, 6])
        MV = sb("MV", [P, 2, QT, 2])
        VE = sb("VE", [P, 2, QT])
        RS = sb("RS", [P, 2, QT])
        XN = sb("XN", [P, QT, C])
        HN = sb("HN", [P, QT, C])
        KM = sb("KM", [P, NQ + 2])
        VA = sb("VA", [P, 2])
        KMM = sb("KMM", [P, 1])
        KMA = sb("KMA", [P, 1])
        FLAG = sb("FLAG", [P, 1], I32)
        REC = sb("REC", [P, 2, GS + 1, 6, B])
        RQ, RG, RR_, RBB, RU, RINV = range(6)
        F1 = sb("F1", [P, 2, HS, B])
        F2 = sb("F2", [P, 2, HS, B])
        F2V = sb("F2V", [P, 2, HS, B])
        E1 = sb("E1", [P, 2, HS, B])
        E2 = sb("E2", [P, 2, HS, B])
        EB = sb("EB", [P, 2, HS, B])
        EAA = sb("EAA", [P, 2, HS, B])
        E2V = sb("E2V", [P, 2, HS, B])
        DEN = sb("DEN", [P, 2, HS, B])
        NUM = sb("NUM", [P, 2, HS, B])
        RDEN = sb("RDEN", [P, 2, HS, B])
        YY = sb("YY", [P, GN])
        AA = sb("AA", [P, 2, HS + 1, B])
        ATT = sb("ATT", [P, GN])
        X1 = sb("X1", [P, GT, C])
        X2N = sb("X2N", [P, GT, C])
        HS2 = sb("HS2", [P, B + GN])
        RRT = sb("RRT", [P, GN])
        KR = sb("KR", [P, FM * GN])
        KQ = sb("KQ", [P, FM, GN])
        T1 = sb("T1", [P, GT, C])
        XA = sb("XA", [P, GT, C])
        XG = sb("XG", [P, GT, C])
        N3 = sb("N3", [P, GT, C])
        H3 = sb("H3", [P, GT, C])
        H3S = sb("H3S", [P, GN])
        LG = sb("LG", [P, GT, E])
        MX = sb("MX", [P, GT, 8])
        IX = sb("IX", [P, GT, 8], U32)
        IXF = sb("IXF", [P, GT, 2])
        DF = sb("DF", [P, GT])
        TH = sb("TH", [P, GT])
        PR = sb("PR", [P, GT, 2])
        WA = sb("WA", [P, 2, GT, E])
        WT = sb("WT", [P, GT, E])
        WE = sb("WE", [P, GT, E])
        SL = sb("SL", [P, 2, HM * GN])
        H3V = sb("H3V", [P, 2, GN])
        HT = sb("HT", [P, 2, HM, GN])
        YW = sb("YW", [P, 2, GT, C])
        ACC = sb("ACC", [P, GT, C])
        OG = sb("OG", [P, GT, C])
        OUT = sb("OUT", [P, GT, C])
        sPP = sb("sPP", [P, B])
        sAA = sb("sAA", [P, B])
        sBB = sb("sBB", [P, B])
        sM = sb("sM", [P, B])
        sP = sb("sP", [P, B])
        sD = sb("sD", [P, 4, B])
        sE = sb("sE", [P, 4, B])
        sT = sb("sT", [P, 9, B])
        sL = sb("sL", [P, B])

        pH1 = [pb("pH1a"), pb("pH1b")]
        pH3 = [pb("pH3a"), pb("pH3b")]
        pY = pb("pY")
        pA, pB, pC = pb("pA"), pb("pB"), pb("pC")

        x_first, x_rest = sem("x_first"), sem("x_rest")
        vec_in, c_in, wkvr_in = sem("vec_in"), sem("c_in"), sem("wkvr_in")
        wmod_first, wmod_rest, warm = sem("wmod_first"), sem("wmod_rest"), sem("warm")
        mix_in, w1_in, w3_in, w2_in = sem("mix_in"), sem("w1_in"), sem("w3_in"), sem("w2_in")
        stored = sem("stored")
        pool_const = steps("pool_const", ["zero", "ident", "rest"])
        mod_act = steps("mod_act", ["silu", "ct"])
        mod_pe = steps("mod_pe", ["ct", "first", "rest"])
        mod_dve = steps("mod_dve", ["sa", "ca", "rest", "cb", "sign", "abs", "size", "gate"])
        ln_dve = steps("ln_dve", [(n, i) for n in ("st", "ag") for i in range(QT)] + ["eps"]
                       + [(n, i) for n in ("scaled", "h") for i in range(QT)])
        ln2_dve = steps("ln2_dve", [(n, i) for n in ("st", "ag") for i in range(QT)] + ["eps"]
                        + [("n", i) for i in range(QT)])
        ln_pool, ln2_pool = steps("ln_pool", ["rs"]), steps("ln2_pool", ["rs"])
        ln_pe = steps("ln_pe", ["t", "k", "v", "r"])
        ln_act = steps("ln_act", ["hs", "k", "abs_k", "v", "r"])
        shift_set = sem("shift_set")
        dk_dve = steps("dk_dve", ["dk", "clip"])
        dk_pool = steps("dk_pool", ["dk", "clip"])
        kmax_dve = steps("kmax_dve", [("km", q) for q in range(NQ)] + ["wu", "um", "max", "flag"])
        u_act = steps("u_act", ["u", "iu"])
        q_act = steps("q_act", ["first"] + [("q", q) for q in range(NQ)])
        kmax_all = sem("kmax_all")
        wkv = steps("wkv", [("rb", 0), "q", ("inv", 0), ("u", 0), "carry", ("g", 0)]
                    + [(n, s) for s in range(1, GS) for n in ("rb", "inv", "u", "g")])
        wkv_start = steps("wkv_start", ["z", "aa", "g", "bb", "inv", "q"])
        y_dve = steps("y_dve", ["f1", "f2", "e1", "e2", "eb", "carry"] + [("aa", b) for b in range(B)]
                      + [("rden", i) for i in range(RP)] + ["y", "att"])
        y_pool = steps("y_pool", ["f2v", "e2v", "den", "ea", "num"])
        a_pe = steps("a_pe", ["t_att", "t_x2", "rr", "kk0", "kk1", "kv"])
        g_pe = steps("g_pe", ["t_h3", "logits"])
        a_dve = steps("a_dve", ["x1", ("st", 0), ("st", 1), ("ag", 0), ("ag", 1), "eps", ("n", 0), ("n", 1)])
        g_dve = steps("g_dve", ["t1", "xa", ("st3", 0), ("st3", 1), ("ag3", 0), ("ag3", 1), "eps3",
                                ("n3", 0), ("n3", 1), ("h3", 0), ("h3", 1),
                                "lg", ("mx", 0), ("mx", 1), ("ix", 0), ("ix", 1), "df", "ixf", "p1", "p2",
                                ("w", 0, 0), ("w", 0, 1), ("w", 1, 0), ("w", 1, 1), "wt"])
        a_pool = steps("a_pool", ["rs"])
        g_pool = steps("g_pool", ["xg", "xr", "rs3"])
        a_act = steps("a_act", ["carry", "hs2", "rr", "re0", "sq0", "re1", "sq1"])
        g_act = steps("g_act", ["h3s", "h3t", "th"])
        h_pe = steps("h_pe", list(range(E)))
        p_pe = steps("p_pe", list(range(E)))
        s_act = steps("s_act", [(n, e) for e in range(E) for n in ("h3", "silu")])
        w_act = steps("w_act", [(e, n) for e in range(E) for n in range(GT)])
        m_first = steps("m_first", list(range(E)))
        m_second = steps("m_second", list(range(E)))
        m_last = sem("m_last")
        we_dve = steps("we_dve", ["we"])
        e_pool = steps("e_pool", [f"a{e}" for e in range(1, E)] + ["og", "out"])
        passed = sem("passed")
        slow_dve, slow_act, slow_copy = sem("slow_dve"), sem("slow_act"), sem("slow_copy")

        x_tok = x.rearrange("b (j s) c -> s b j c", s=TS)
        out_tok = out.rearrange("b (j s) c -> s b j c", s=TS)

        def row(v):
            return v.rearrange("(p o) -> p o", o=1)

        def difference_cols(q):
            return max(GN + B, q * QN - B), (q + 1) * QN - B

        def last_part(g):
            return min(NQ - 1, -(-((g + 1) * GN + 2 * B) // QN) - 1) if isinstance(g, int) else NQ - 1

        def cols(g, n=GN):
            return bass.ds(g * n, n)

        def ranks(g):
            return bass.ds(g * GT, GT)

        def groups(t):
            def group(g):
                return g if not isinstance(g, int) or 0 <= g < NG else None
            return group(t), group(t - 1), group(t - 2), group(t - 3)

        def expert(t, j):
            _, _, gate, late = groups(t)
            return (late, E - LATE + j) if j < LATE else (gate, j - LATE)

        def ahead(t, j):
            _, _, gate, _ = groups(t)
            return expert(t, j + 1) if j + 1 < E else (gate, E - LATE)

        def second_half(g, e):
            last = (g - NG + 3) * E + e - (E - LATE) if isinstance(g, int) else -1
            return (m_last, last + 1) if last >= 0 else (m_second.sem, m_second.value(g, e))

        def tile3(ap):
            return ap.rearrange("p (t b) -> p t b", b=B)

        block = ctx.enter_context(nc.Block())

        @block.sync
        def _(sp):
            for n in range(QT):
                sp.dma_start(X[:, n, :], x_tok[:, :, n, :]).then_inc(x_first, 16)
            for i, v in enumerate((row(time_decay), row(time_first), row(ln1_g), row(ln1_b), row(ln2_g), row(ln2_b),
                                   time_shift.rearrange("a b c -> c (a b)"))):
                sp.dma_start(VEC[:, i:i + 1], v).then_inc(vec_in, 16)
            for dst, src in ((WK, Wk), (WV, Wv), (WR, Wr)):
                sp.dma_start(dst[:], src).then_inc(wkvr_in, 16)
            sp.dma_start(WMOD[:, 2 * C:], wmod[:, 2 * C:]).then_inc(wmod_rest, 16)
            for n in range(QT, NT):
                sp.dma_start(X[:, n, :], x_tok[:, :, n, :]).then_inc(x_rest, 16)
            sp.dma_start(WCK[:], Wck).then_inc(mix_in, 16)
            sp.dma_start(WCV[:], Wcv.rearrange("(m p) d -> p m d", p=P)).then_inc(mix_in, 16)
            sp.dma_start(WCR[:], Wcr).then_inc(mix_in, 16)
            sp.dma_start(WG[:], w_gate).then_inc(mix_in, 16)
            sp.dma_start(W1[:], w1.rearrange("e d h -> d e h")).then_inc(w1_in, 16)
            sp.dma_start(W3[:], w3.rearrange("e d h -> d e h")).then_inc(w3_in, 16)
            sp.dma_start(W2[:], w2.rearrange("e (m p) d -> p e m d", p=P)).then_inc(w2_in, 16)
            with sp.Fori(0, NG) as g:
                sp.wait_ge(e_pool.sem, e_pool.value(g, "out"))
                for n in range(GT):
                    to = out_tok[:, :, bass.ds(g * GT + n, 1), :].rearrange("s b o c -> s b (o c)")
                    sp.dma_start(to, OUT[:, n, :]).then_inc(stored, 16)
            sp.wait_ge(stored, 16 * NT)

        @block.gpsimd
        def _(pool):
            pool.memset(zero[:], 0.0).then_inc(pool_const.sem, pool_const.step("zero"))
            pool.wait_ge(pool_const.sem, pool_const.value(0, "zero"))
            pool.affine_select(out=ident[:], in_=zero[:], compare_op=ALU.not_equal, fill=1.0, base=0,
                                               pattern=[[-1, P]], channel_multiplier=1) \
                .then_inc(pool_const.sem, pool_const.step("ident"))
            for e in range(E):
                pool.memset(IOTA[:, e:e + 1], float(e))
            pool.memset(Q[:, N - B:], 1.0)
            pool.memset(NHALF[:], -0.5).then_inc(pool_const.sem, pool_const.step("rest"))
            pool.wait_ge(pool_const.sem, pool_const.value(0, "rest"))

            def deviations(q):
                pool.wait_ge(ln_dve.sem, ln_dve.value(q, "eps"))
                pool.tensor_tensor(RS[:, 0, :], VE[:, 0, :], NHALF[:], ALU.pow) \
                    .then_inc(ln_pool.sem, ln_pool.step("rs"))

            def deviations2(q):
                pool.wait_ge(ln2_dve.sem, ln2_dve.value(q, "eps"))
                pool.tensor_tensor(RS[:, 1, :], VE[:, 1, :], NHALF[:], ALU.pow) \
                    .then_inc(ln2_pool.sem, ln2_pool.step("rs"))

            def differences(q):
                c0, c1 = difference_cols(q)
                pool.wait_ge(ln_act.sem, ln_act.value(q, "k"))
                pool.tensor_tensor(YS[:, c0:c1], K[:, c0:c1], K[:, c0 + B:c1 + B], ALU.subtract) \
                    .then_inc(dk_pool.sem, dk_pool.step("dk"))
                pool.wait_ge(dk_pool.sem, dk_pool.value(q, "dk"))
                pool.tensor_scalar(YS[:, c0:c1], YS[:, c0:c1], -2.0 * K_SAFE, 2.0 * K_SAFE, ALU.max, ALU.min) \
                    .then_inc(dk_pool.sem, dk_pool.step("clip"))

            deviations(0)
            for q in range(NQ):
                deviations2(q)
                if q + 1 < NQ:
                    deviations(q + 1)
                if q > 0:
                    differences(q - 1)
            pool.wait_ge(kmax_dve.sem, kmax_dve.value(0, "max"))
            pool.partition_all_reduce(KMA[:], KMM[:], P, RMAX).then_inc(kmax_all, 1)
            differences(NQ - 1)

            def y_part(g, h):
                k = g * 2 + h
                v = tile3(V[:, cols(k, HALF_N)])
                if not (first(g) and h == 0):
                    pool.wait_ge(y_dve.sem, y_dve.value(k - 1, "y"))
                pool.wait_ge(ln_act.sem, ln_act.value(0 if first(g) else NQ - 1, "v"))
                pool.wait_ge(y_dve.sem, y_dve.value(k, "e2"))
                pool.tensor_tensor(F2V[:, h], F2[:, h], v, ALU.mult).then_inc(y_pool.sem, y_pool.step("f2v"))
                pool.tensor_tensor(E2V[:, h], E2[:, h], v, ALU.mult).then_inc(y_pool.sem, y_pool.step("e2v"))
                pool.wait_ge(y_dve.sem, y_dve.value(k, "eb"))
                pool.tensor_tensor(DEN[:, h], EB[:, h], E2[:, h], ALU.add).then_inc(y_pool.sem, y_pool.step("den"))

            def y_numerator(g, h):
                k = g * 2 + h
                pool.wait_ge(y_dve.sem, y_dve.value(k, ("aa", B - 1)))
                pool.tensor_tensor(EAA[:, h], E1[:, h], AA[:, h, 0:HS, :], ALU.mult) \
                    .then_inc(y_pool.sem, y_pool.step("ea"))
                pool.wait_ge(y_pool.sem, y_pool.value(k, "ea"))
                pool.tensor_tensor(NUM[:, h], EAA[:, h], E2V[:, h], ALU.add).then_inc(y_pool.sem, y_pool.step("num"))

            def hidden_half(g, e):
                if e >= 2:
                    pool.wait_ge(p_pe.sem, p_pe.value(g, e - 2))
                elif not first(g):
                    pool.wait_ge(p_pe.sem, p_pe.value(g - 1, E - 2 + e))
                pool.wait_ge(s_act.sem, s_act.value(g, ("silu", e)))
                pool.tensor_tensor(HT[:, e % 2, 1, :], SL[:, e % 2, GN:], H3V[:, e % 2, :], ALU.mult) \
                    .then_inc(m_second.sem, m_second.step(e))

            def a_ln2(g):
                pool.wait_ge(a_dve.sem, a_dve.value(g, "eps"))
                pool.tensor_tensor(RS[:, 0, 0:GT], VE[:, 0, 0:GT], NHALF[:, 0:GT], ALU.pow) \
                    .then_inc(a_pool.sem, a_pool.step("rs"))

            def a_residual(g):
                pool.wait_ge(g_dve.sem, g_dve.value(g, "xa"))
                pool.tensor_tensor(XG[:], XA[:], gate_rows(0), ALU.mult).then_inc(g_pool.sem, g_pool.step("xg"))
                pool.wait_ge(g_pool.sem, g_pool.value(g, "xg"))
                pool.tensor_tensor(X[:, ranks(g), :], XG[:], X[:, ranks(g), :], ALU.add) \
                    .then_inc(g_pool.sem, g_pool.step("xr"))

            def a_ln3(g):
                pool.wait_ge(g_dve.sem, g_dve.value(g, "eps3"))
                pool.tensor_tensor(RS[:, 1, 0:GT], VE[:, 1, 0:GT], NHALF[:, 0:GT], ALU.pow) \
                    .then_inc(g_pool.sem, g_pool.step("rs3"))

            def accumulate(g, e):
                pool.wait_ge(w_act.sem, w_act.value(g, (e, GT - 1)))
                if e == 1:
                    if not first(g):
                        pool.wait_ge(e_pool.sem, e_pool.value(g - 1, "og"))
                    pool.tensor_tensor(ACC[:], YW[:, 0], YW[:, 1], ALU.add).then_inc(e_pool.sem, e_pool.step("a1"))
                else:
                    pool.wait_ge(e_pool.sem, e_pool.value(g, f"a{e - 1}"))
                    pool.tensor_tensor(ACC[:], ACC[:], YW[:, e % 2], ALU.add) \
                        .then_inc(e_pool.sem, e_pool.step(f"a{e}"))

            def finish(g):
                pool.wait_ge(e_pool.sem, e_pool.value(g, f"a{E - 1}"))
                pool.tensor_tensor(OG[:], ACC[:], gate_rows(1), ALU.mult).then_inc(e_pool.sem, e_pool.step("og"))
                pool.wait_ge(e_pool.sem, e_pool.value(g, "og"))
                if not first(g):
                    pool.wait_ge(stored, g * (16 * GT))
                pool.tensor_tensor(OUT[:], OG[:], X[:, ranks(g), :], ALU.add).then_inc(e_pool.sem, e_pool.step("out"))

            def gate_rows(k):
                return GAB[:, k:k + 1, :].broadcast_to((P, GT, C))

            def turn(t):
                rec, att, gate, late = groups(t)
                for slot in range(SLOTS):
                    g, e = expert(t, slot // 2)
                    if slot % 2 == 0 and g is not None and rec is not None:
                        hidden_half(g, e)
                    if slot == 0 and att is not None:
                        if first(att):
                            y_part(att, 0)
                            y_numerator(att, 0)
                        y_part(att, 1)
                    if slot == 5 and att is not None:
                        a_ln2(att)
                    if slot == 9 and rec is not None:
                        y_part(rec, 0)
                    if slot == 12 and rec is not None:
                        y_numerator(rec, 0)
                    if slot % 2 == 1 and g is not None and e > 0:
                        accumulate(g, e)
                    if slot == 2 and att is not None:
                        y_numerator(att, 1)
                    if slot == 2 * LATE and late is not None:
                        finish(late)
                    if slot == 12 and att is not None:
                        a_residual(att)
                    if slot == 15 and att is not None:
                        a_ln3(att)

            for t in range(1, FIRST_FULL):
                turn(t)
            with pool.Fori(FIRST_FULL, NG) as t:
                turn(t)
            for t in range(NG, TURNS):
                turn(t)

        @block.scalar
        def _(act):
            act.dma_start(CB[:], c).then_inc(c_in, 16)
            act.dma_start(WMOD[:, 0:2 * C], wmod[:, 0:2 * C]).then_inc(wmod_first, 16)

            act.wait_ge(pool_const.sem, pool_const.value(0, "zero"))
            act.activation(CSW[:], zero[0:B, 0:1], ACT.Silu).then_inc(warm, 1)
            act.wait_ge(c_in, 16)
            act.activation(CS[:], CB[:], ACT.Silu).then_inc(mod_act.sem, mod_act.step("silu"))
            act.wait_ge(mod_pe.sem, mod_pe.value(0, "ct"))
            ct = pB[:, 0:B].rearrange("p (o b) -> p o b", o=1).broadcast_to((P, TS, B))
            act.copy(tile3(CT[:]), ct).then_inc(mod_act.sem, mod_act.step("ct"))
            act.wait_ge(vec_in, 16 * 7)
            act.activation(HSh[:, 0:B], zero[:, 0:B], ACT.Identity, bias=sh_v).then_inc(shift_set, 1)
            act.activation(UE[:, 0:1], u_v, ACT.Exp).then_inc(u_act.sem, u_act.step("u"))
            act.activation(UE[:, 1:2], u_v, ACT.Exp, scale=-1.0).then_inc(u_act.sem, u_act.step("iu"))

            def first_stage(q):
                act.wait_ge(ln_pe.sem, ln_pe.value(q, "t"))
                act.activation(HSh[:, bass.ds(q * QN + B, QN)], pA[:], ACT.Identity, bias=b1_v,
                                           scale=g1_v).then_inc(ln_act.sem, ln_act.step("hs"))
                act.wait_ge(ln_pe.sem, ln_pe.value(q, "k"))
                act.copy(K[:, cols(q, QN)], pH1[0][:]).then_inc(ln_act.sem, ln_act.step("k"))
                if q == 0:
                    act.wait_ge(dk_dve.sem, dk_dve.value(0, "clip"))
                    act.activation(Q[:, 0:GN + B], YS[:, 0:GN + B], ACT.Exp, bias=w_v) \
                        .then_inc(q_act.sem, q_act.step("first"))
                act.activation(H3T[:, cols(q, QN)], pH1[0][:], ACT.Abs).then_inc(ln_act.sem, ln_act.step("abs_k"))
                act.wait_ge(ln_pe.sem, ln_pe.value(q, "v"))
                act.copy(V[:, cols(q, QN)], pH3[0][:]).then_inc(ln_act.sem, ln_act.step("v"))
                act.wait_ge(ln_pe.sem, ln_pe.value(q, "r"))
                act.activation(SR[:, cols(q, QN)], pH1[1][:], ACT.Tanh, scale=0.5) \
                    .then_inc(ln_act.sem, ln_act.step("r"))

            def exponentials(q):
                c0, c1 = difference_cols(q)
                act.wait_ge(dk_pool.sem, dk_pool.value(q, "clip"))
                act.activation(Q[:, c0:c1], YS[:, c0:c1], ACT.Exp, bias=w_v).then_inc(q_act.sem, q_act.step(("q", q)))

            for q in range(NQ):
                first_stage(q)
                if q > 0:
                    exponentials(q - 1)
            exponentials(NQ - 1)

            act.wait_ge(kmax_dve.sem, kmax_dve.value(0, "flag"))
            outside = act.value_load(FLAG[0:1, 0:1])
            with act.If(outside > 0):
                with act.Fori(0, T) as t:
                    act.wait_ge(slow_dve, t * 17 + 7)
                    act.activation(sE[:], sD[:], ACT.Exp).then_inc(slow_act, 1)
                    act.wait_ge(slow_dve, t * 17 + 16)
                    act.activation(sL[:], sBB[:], ACT.Ln).then_inc(slow_act, 1)

            def a_hs2(g):
                if not first(g):
                    act.wait_ge(a_pe.sem, a_pe.value(g - 1, "kk1"))
                    act.copy(HS2[:, 0:B], HS2[:, GN:GN + B]).then_inc(a_act.sem, a_act.step("carry"))
                    act.wait_ge(a_act.sem, a_act.value(g, "carry"))
                else:
                    act.activation(HS2[:, 0:B], zero[:, 0:B], ACT.Identity, bias=sh_v) \
                        .then_inc(a_act.sem, a_act.step("carry"))
                act.wait_ge(a_pe.sem, a_pe.value(g, "t_x2"))
                act.activation(HS2[:, B:B + GN], pA[:, 0:GN], ACT.Identity, bias=b2_v, scale=g2_v) \
                    .then_inc(a_act.sem, a_act.step("hs2"))

            def a_mix(g, i):
                if i == 0:
                    if not first(g):
                        act.wait_ge(g_dve.sem, g_dve.value(g - 1, "t1"))
                    act.wait_ge(a_pe.sem, a_pe.value(g, "rr"))
                    act.activation(RRT[:], pA[:, 0:GN], ACT.Tanh, scale=0.5).then_inc(a_act.sem, a_act.step("rr"))
                half = slice(i * FM * GN // 2, (i + 1) * FM * GN // 2)
                act.wait_ge(a_pe.sem, a_pe.value(g, f"kk{i}"))
                act.activation(KR[:, half], (pB, pC)[i][:], ACT.Relu).then_inc(a_act.sem, a_act.step(f"re{i}"))
                act.wait_ge(a_act.sem, a_act.value(g, f"re{i}"))
                kq = KQ[:, i * FM // 2:(i + 1) * FM // 2, :].rearrange("p m n -> p (m n)")
                act.activation(kq, KR[:, half], ACT.Square).then_inc(a_act.sem, a_act.step(f"sq{i}"))

            def a_h3(g):
                act.wait_ge(g_pe.sem, g_pe.value(g, "t_h3"))
                act.copy(H3S[:], pB[:, 0:GN]).then_inc(g_act.sem, g_act.step("h3s"))
                act.copy(H3T[:, cols(g)], pB[:, 0:GN]).then_inc(g_act.sem, g_act.step("h3t"))

            def a_gate(g):
                act.wait_ge(g_dve.sem, g_dve.value(g, "df"))
                act.activation(TH[:], DF[:], ACT.Tanh, scale=0.5).then_inc(g_act.sem, g_act.step("th"))

            def silu(g, e):
                if e >= 2:
                    act.wait_ge(m_first.sem, m_first.value(g, e - 2))
                    act.wait_ge(*second_half(g, e - 2))
                elif not first(g):
                    act.wait_ge(m_first.sem, m_first.value(g - 1, E - 2 + e))
                    act.wait_ge(*second_half(g - 1, E - 2 + e))
                act.wait_ge(h_pe.sem, h_pe.value(g, e))
                act.copy(H3V[:, e % 2, :], pH3[e % 2][:, GN:]).then_inc(s_act.sem, s_act.step(("h3", e)))
                act.activation(SL[:, e % 2], pH1[e % 2][:], ACT.Silu).then_inc(s_act.sem, s_act.step(("silu", e)))

            def weigh(g, e):
                if e >= 2:
                    act.wait_ge(e_pool.sem, e_pool.value(g, f"a{max(e - 2, 1)}"))
                elif not first(g):
                    act.wait_ge(e_pool.sem, e_pool.value(g - 1, f"a{E - 2 + e}"))
                act.wait_ge(p_pe.sem, p_pe.value(g, e))
                if e == 0:
                    act.wait_ge(we_dve.sem, we_dve.value(g, "we"))
                for n in range(GT):
                    act.activation(YW[:, e % 2, n], pY[:, n * C:(n + 1) * C], ACT.Copy, scale=WE[:, n, e:e + 1]) \
                        .then_inc(w_act.sem, w_act.step((e, n)))

            def turn(t):
                _, att, gate, late = groups(t)
                for slot in range(SLOTS):
                    if slot == 3 and gate is not None:
                        a_h3(gate)
                    if slot == 6 and gate is not None:
                        a_gate(gate)
                    g, e = expert(t, slot // 2) if slot % 2 else ahead(t, slot // 2)
                    if g is not None:
                        if slot % 2:
                            weigh(g, e)
                        else:
                            silu(g, e)
                    if slot == 6 and att is not None:
                        a_hs2(att)
                    if slot == 8 and att is not None:
                        a_mix(att, 0)
                    if slot == 9 and att is not None:
                        a_mix(att, 1)

            for t in range(1, FIRST_FULL):
                turn(t)
            with act.Fori(FIRST_FULL, NG) as t:
                turn(t)
            for t in range(NG, TURNS):
                turn(t)

        @block.vector
        def _(dve):
            def wait_apart(semaphore, value):
                dve.wait_ge(semaphore, value)
                if not isinstance(value, int):
                    dve.sem_inc(passed, 1)

            def modulation():
                dve.wait_ge(mod_pe.sem, mod_pe.value(0, "first"))
                dve.tensor_scalar(MOD[:, 1, :], pH3[1][:, C:2 * C], 1.0, None, ALU.add) \
                    .then_inc(mod_dve.sem, mod_dve.step("sa"))
                dve.tensor_copy(MOD[:, 0, :], pH3[1][:, 0:C]).then_inc(mod_dve.sem, mod_dve.step("ca"))
                dve.wait_ge(mod_dve.sem, mod_dve.value(0, "ca"))

            def rest_of_modulation():
                dve.wait_ge(mod_pe.sem, mod_pe.value(0, "rest"))
                dve.tensor_copy(MOD[:].rearrange("p k c -> p (k c)")[:, 2 * C:], pY[:]) \
                    .then_inc(mod_dve.sem, mod_dve.step("rest"))
                dve.wait_ge(mod_dve.sem, mod_dve.value(0, "rest"))
                dve.tensor_scalar(MOD[:, 4, :], MOD[:, 4, :], 1.0, None, ALU.add) \
                    .then_inc(mod_dve.sem, mod_dve.step("cb"))
                gates = MOD[:].rearrange("p (i k) c -> p i k c", i=2)[:, :, 2, :]
                dve.tensor_scalar(GSG[:], gates, 0.0, 2.0, ALU.is_ge, ALU.mult) \
                    .then_inc(mod_dve.sem, mod_dve.step("sign"))
                dve.scalar_tensor_tensor(GAB[:], gates, -1.0, gates, ALU.mult, ALU.max) \
                    .then_inc(mod_dve.sem, mod_dve.step("abs"))
                dve.wait_ge(mod_dve.sem, mod_dve.value(0, "abs"))
                dve.tensor_scalar(GAB[:], GAB[:], MIN_GATE, None, ALU.max).then_inc(mod_dve.sem, mod_dve.step("size"))
                dve.wait_ge(mod_dve.sem, mod_dve.value(0, "size"))
                dve.scalar_tensor_tensor(GAB[:], GSG[:], -1.0, GAB[:], ALU.add, ALU.mult) \
                    .then_inc(mod_dve.sem, mod_dve.step("gate"))

            def part_stats(q, k, src, counter):
                for n in range(QT):
                    if k == 1:
                        dve.wait_ge(ln_dve.sem, ln_dve.value(q, ("h", n)))
                    dve.bn_stats(STAT[:, k, n, :], src(n)).then_inc(counter.sem, counter.step(("st", n)))
                    yield
                for n in range(QT):
                    dve.wait_ge(counter.sem, counter.value(q, ("st", n)))
                    dve.bn_aggr(MV[:, k, n, :], STAT[:, k, n, :]).then_inc(counter.sem, counter.step(("ag", n)))
                    yield
                dve.wait_ge(counter.sem, counter.value(q, ("ag", QT - 1)))
                dve.tensor_scalar(VE[:, k, :], MV[:, k, :, 1], LN_EPS, None, ALU.add) \
                    .then_inc(counter.sem, counter.step("eps"))
                yield

            def stats(q):
                yield from part_stats(q, 0, lambda n: X[:, q * QT + n, :], ln_dve)

            def modulated(q):
                dve.wait_ge(ln_dve.sem, ln_dve.value(q, "eps"))
                for n in range(QT):
                    dve.scalar_tensor_tensor(XN[:, n, :], X[:, q * QT + n, :], MV[:, 0, n, 0:1], MOD[:, 1, :],
                                             ALU.subtract, ALU.mult).then_inc(ln_dve.sem, ln_dve.step(("scaled", n)))
                    yield
                dve.wait_ge(ln_pool.sem, ln_pool.value(q, "rs"))
                for n in range(QT):
                    dve.wait_ge(ln_dve.sem, ln_dve.value(q, ("scaled", n)))
                    dve.scalar_tensor_tensor(H[:, q * QT + n, :], XN[:, n, :], RS[:, 0, n:n + 1], MOD[:, 0, :],
                                             ALU.mult, ALU.add).then_inc(ln_dve.sem, ln_dve.step(("h", n)))
                    yield
                yield from part_stats(q, 1, lambda n: H[:, q * QT + n, :], ln2_dve)

            def normed(q):
                dve.wait_ge(ln2_pool.sem, ln2_pool.value(q, "rs"))
                if not first(q):
                    dve.wait_ge(ln_pe.sem, ln_pe.value(q - 1, "t"))
                for n in range(QT):
                    dve.tensor_scalar(HN[:, n, :], H[:, q * QT + n, :], MV[:, 1, n, 0:1], RS[:, 1, n:n + 1],
                                      ALU.subtract, ALU.mult).then_inc(ln2_dve.sem, ln2_dve.step(("n", n)))
                    yield

            def first_difference():
                dve.wait_ge(ln_act.sem, ln_act.value(0, "k"))
                dve.tensor_tensor(YS[:, 0:GN + B], K[:, 0:GN + B], K[:, B:GN + 2 * B], ALU.subtract) \
                    .then_inc(dk_dve.sem, dk_dve.step("dk"))
                dve.wait_ge(dk_dve.sem, dk_dve.value(0, "dk"))
                dve.tensor_scalar(YS[:, 0:GN + B], YS[:, 0:GN + B], -2.0 * K_SAFE, 2.0 * K_SAFE, ALU.max, ALU.min) \
                    .then_inc(dk_dve.sem, dk_dve.step("clip"))

            def largest_k(q):
                dve.wait_ge(ln_act.sem, ln_act.value(q, "abs_k"))
                dve.tensor_reduce(KM[:, q:q + 1], H3T[:, q * QN:(q + 1) * QN], AX_X, ALU.max) \
                    .then_inc(kmax_dve.sem, kmax_dve.step(("km", q)))
                yield

            def range_check():
                dve.scalar_tensor_tensor(VA[:], VEC[:, 0:2], -1.0, VEC[:, 0:2], ALU.mult, ALU.max) \
                    .then_inc(kmax_dve.sem, kmax_dve.step("wu"))
                yield
                dve.wait_ge(kmax_dve.sem, kmax_dve.value(0, "wu"))
                dve.tensor_scalar(KM[:, NQ:NQ + 2], VA[:], K_SAFE / W_SAFE, None, ALU.mult) \
                    .then_inc(kmax_dve.sem, kmax_dve.step("um"))
                yield
                dve.wait_ge(kmax_dve.sem, kmax_dve.value(0, "um"))
                dve.tensor_reduce(KMM[:], KM[:], AX_X, ALU.max).then_inc(kmax_dve.sem, kmax_dve.step("max"))
                yield

            def choose_path():
                dve.wait_ge(kmax_all, 1)
                dve.tensor_scalar(FLAG[:], KMA[:], K_SAFE, None, ALU.is_gt) \
                    .then_inc(kmax_dve.sem, kmax_dve.step("flag"))
                dve.wait_ge(kmax_dve.sem, kmax_dve.value(0, "flag"))
                outside = dve.value_load(FLAG[0:1, 0:1])
                with dve.If(outside > 0):
                    dve.wait_ge(ln_act.sem, ln_act.value(NQ - 1, "v"))
                    dve.wait_ge(q_act.sem, q_act.value(0, ("q", NQ - 1)))
                    general_path()

            def rest_of_first_stage():
                dve.wait_ge(x_rest, 16 * (NT - QT))
                yield from stats(1)
                for q in range(1, NQ):
                    yield from modulated(q)
                    if q + 1 < NQ:
                        yield from stats(q + 1)
                    yield from largest_k(q - 1)
                    yield from normed(q)

            dve.memset(REC[:, 0, 0, :, :], 0.0).then_inc(wkv_start.sem, wkv_start.step("z"))
            dve.memset(AA[:, 1, HS, :], 0.0).then_inc(wkv_start.sem, wkv_start.step("aa"))
            dve.wait_ge(wkv_start.sem, wkv_start.value(0, "z"))
            dve.memset(REC[:, 0, 0, RG, :], 1.0).then_inc(wkv_start.sem, wkv_start.step("g"))
            dve.memset(REC[:, 0, 0, RBB, :], 1.0).then_inc(wkv_start.sem, wkv_start.step("bb"))
            dve.memset(REC[:, 0, 0, RINV, :], 1e30).then_inc(wkv_start.sem, wkv_start.step("inv"))

            def wkv_steps(g, half, s0, s1, side):
                for s in range(s0, s1):
                    if s > 0 or first(g):
                        was, now = REC[:, half, s], REC[:, half, s + 1]
                    else:
                        was, now = REC[:, 1 - half, GS], REC[:, half, 1]
                    if s > 0:
                        dve.wait_ge(wkv.sem, wkv.value(g, ("g", s - 1)))
                    elif first(g):
                        dve.wait_ge(wkv_start.sem, wkv_start.value(0, "q"))
                    else:
                        dve.wait_ge(wkv.sem, wkv.value(g - 1, ("g", GS - 1)))
                    u2 = was[:, RU:RU + 1, :].broadcast_to((P, 2, B))
                    dve.scalar_tensor_tensor(now[:, RR_:RBB + 1, :], u2, 1.0, was[:, RQ:RG + 1, :],
                                             ALU.add, ALU.mult).then_inc(wkv.sem, wkv.step(("rb", s)))
                    if s == 0:
                        dve.wait_ge(q_act.sem, q_act.value(0, "first" if first(g) else ("q", last_part(g))))
                        dve.tensor_copy(REC[:, half, 1:, RQ, :], tile3(Q[:, bass.ds(g * GN + B, GN)])) \
                            .then_inc(wkv.sem, wkv.step("q"))
                    else:
                        next(side, None)
                    dve.wait_ge(wkv.sem, wkv.value(g, ("rb", s)))
                    dve.reciprocal(now[:, RINV, :], now[:, RR_, :]).then_inc(wkv.sem, wkv.step(("inv", s)))
                    dve.scalar_tensor_tensor(now[:, RU, :], now[:, RR_, :], R_CAP, now[:, RBB, :],
                                             ALU.min, ALU.mult).then_inc(wkv.sem, wkv.step(("u", s)))
                    if s == 0:
                        last = REC[:, 0 if first(g) else 1 - half, 0 if first(g) else GS, RG:]
                        dve.tensor_copy(REC[:, half, 0, RG:], last).then_inc(wkv.sem, wkv.step("carry"))
                    else:
                        next(side, None)
                    dve.wait_ge(wkv.sem, wkv.value(g, ("inv", s)))
                    dve.tensor_scalar(now[:, RG, :], now[:, RINV, :], 1.0 / R_CAP, 1.0,
                                      ALU.max, ALU.min).then_inc(wkv.sem, wkv.step(("g", s)))
                    next(side, None)

            def y_records(g, half, h):
                k = g * 2 + h
                here = slice(h * HS, (h + 1) * HS)
                before, r_inv = REC[:, half, here, RR_, :], REC[:, half, here, RINV, :]
                if first(g) and h == 0:
                    dve.wait_ge(u_act.sem, u_act.value(0, "iu"))
                else:
                    dve.wait_ge(y_pool.sem, y_pool.value(k - 1, "num"))
                dve.wait_ge(wkv.sem, wkv.value(g, ("g", (h + 1) * HS - 2)))
                dve.tensor_scalar(F1[:, h], before, 1.0, None, ALU.min).then_inc(y_dve.sem, y_dve.step("f1"))
                yield
                dve.tensor_scalar(F2[:, h], r_inv, 1.0, None, ALU.min).then_inc(y_dve.sem, y_dve.step("f2"))
                yield
                dve.tensor_scalar(E1[:, h], before, UE[:, 1:2], 1.0, ALU.mult, ALU.min) \
                    .then_inc(y_dve.sem, y_dve.step("e1"))
                yield
                dve.tensor_scalar(E2[:, h], r_inv, UE[:, 0:1], 1.0, ALU.mult, ALU.min) \
                    .then_inc(y_dve.sem, y_dve.step("e2"))
                yield
                dve.wait_ge(y_dve.sem, y_dve.value(k, "e1"))
                dve.tensor_tensor(EB[:, h], E1[:, h], REC[:, half, here, RBB, :], ALU.mult) \
                    .then_inc(y_dve.sem, y_dve.step("eb"))
                yield
                if first(g) and h == 0:
                    dve.wait_ge(wkv_start.sem, wkv_start.value(0, "aa"))
                else:
                    dve.wait_ge(y_dve.sem, y_dve.value(k - 1, ("aa", B - 1)))
                dve.tensor_copy(AA[:, h, 0, :], AA[:, 1 - h, HS, :]).then_inc(y_dve.sem, y_dve.step("carry"))
                yield

            def y_scan(g, h):
                k = g * 2 + h
                dve.wait_ge(y_dve.sem, y_dve.value(k, "carry"))
                dve.wait_ge(y_pool.sem, y_pool.value(k, "f2v"))
                for b in range(B):
                    dve.tensor_tensor_scan(AA[:, h, 1:, b], F1[:, h, :, b], F2V[:, h, :, b], AA[:, h, 0, b:b + 1],
                                           ALU.mult, ALU.add).then_inc(y_dve.sem, y_dve.step(("aa", b)))
                    if b % 2:
                        yield

            def y_reciprocal(g, h):
                dve.wait_ge(y_pool.sem, y_pool.value(g * 2 + h, "den"))
                piece = HS // RP
                for i in range(RP):
                    part = slice(i * piece, (i + 1) * piece)
                    dve.reciprocal(RDEN[:, h, part, :], DEN[:, h, part, :]) \
                        .then_inc(y_dve.sem, y_dve.step(("rden", i)))
                    yield

            def y_att(g, h):
                k = g * 2 + h
                here = slice(h * HALF_N, (h + 1) * HALF_N)
                dve.wait_ge(y_dve.sem, y_dve.value(k, ("rden", RP - 1)))
                dve.wait_ge(y_pool.sem, y_pool.value(k, "num"))
                dve.tensor_tensor(tile3(YY[:, here]), NUM[:, h], RDEN[:, h], ALU.mult) \
                    .then_inc(y_dve.sem, y_dve.step("y"))
                yield
                if first(g):
                    dve.wait_ge(ln_act.sem, ln_act.value(0, "r"))
                elif h == 0:
                    dve.wait_ge(ln_act.sem, ln_act.value(NQ - 1, "r"))
                    dve.wait_ge(a_pe.sem, a_pe.value(g - 1, "t_att"))
                dve.wait_ge(y_dve.sem, y_dve.value(k, "y"))
                dve.scalar_tensor_tensor(ATT[:, here], SR[:, cols(k, HALF_N)], 1.0, YY[:, here], ALU.add, ALU.mult) \
                    .then_inc(y_dve.sem, y_dve.step("att"))
                yield

            def norm(g, src, k, dve_steps, stat, aggr, eps):
                for n in range(GT):
                    dve.bn_stats(STAT[:, k, n, :], src(n)).then_inc(dve_steps.sem, dve_steps.step((stat, n)))
                    yield
                for n in range(GT):
                    wait_apart(dve_steps.sem, dve_steps.value(g, (stat, n)))
                    dve.bn_aggr(MV[:, k, n, :], STAT[:, k, n, :]).then_inc(dve_steps.sem, dve_steps.step((aggr, n)))
                    yield
                dve.wait_ge(dve_steps.sem, dve_steps.value(g, (aggr, GT - 1)))
                dve.tensor_scalar(VE[:, k, 0:GT], MV[:, k, 0:GT, 1], LN_EPS, None, ALU.add) \
                    .then_inc(dve_steps.sem, dve_steps.step(eps))
                yield

            def xr(g):
                return lambda n: X[:, bass.ds(g * GT + n, 1), :].rearrange("p o c -> p (o c)")

            def a_x1(g):
                if not first(g):
                    dve.wait_ge(g_dve.sem, g_dve.value(g - 1, "xa"))
                dve.wait_ge(a_pe.sem, a_pe.value(g, "t_att"))
                pa = pA[:, 0:GN].rearrange("p (n c) -> p n c", c=C)
                dve.scalar_tensor_tensor(X1[:], pa, 0.5, H[:, ranks(g), :], ALU.mult, ALU.add) \
                    .then_inc(a_dve.sem, a_dve.step("x1"))
                yield
                wait_apart(a_dve.sem, a_dve.value(g, "x1"))
                yield from norm(g, lambda n: X1[:, n, :], 0, a_dve, "st", "ag", "eps")

            def a_x2(g):
                dve.wait_ge(a_pool.sem, a_pool.value(g, "rs"))
                for n in range(GT):
                    dve.tensor_scalar(X2N[:, n, :], X1[:, n, :], MV[:, 0, n, 0:1], RS[:, 0, n:n + 1],
                                                 ALU.subtract, ALU.mult).then_inc(a_dve.sem, a_dve.step(("n", n)))
                    yield

            def a_mixed(g):
                dve.wait_ge(a_pe.sem, a_pe.value(g, "kv"))
                dve.wait_ge(a_act.sem, a_act.value(g, "rr"))
                kv = pA[:, 0:GN].rearrange("p (n c) -> p n c", c=C)
                dve.scalar_tensor_tensor(T1[:], RRT[:].rearrange("p (n c) -> p n c", c=C), 1.0, kv,
                                                    ALU.add, ALU.mult).then_inc(g_dve.sem, g_dve.step("t1"))
                yield
                dve.wait_ge(g_dve.sem, g_dve.value(g, "t1"))
                if not first(g):
                    dve.wait_ge(g_pool.sem, g_pool.value(g - 1, "xg"))
                dve.scalar_tensor_tensor(XA[:], T1[:], 0.5, X1[:], ALU.mult, ALU.add) \
                    .then_inc(g_dve.sem, g_dve.step("xa"))
                yield

            def a_stats3(g):
                wait_apart(g_pool.sem, g_pool.value(g, "xr"))
                yield from norm(g, xr(g), 1, g_dve, "st3", "ag3", "eps3")

            def a_n3(g):
                dve.wait_ge(g_dve.sem, g_dve.value(g, "eps3"))
                for n in range(GT):
                    dve.scalar_tensor_tensor(N3[:, n, :], xr(g)(n), MV[:, 1, n, 0:1], MOD[:, 4, :],
                                             ALU.subtract, ALU.mult).then_inc(g_dve.sem, g_dve.step(("n3", n)))
                    yield

            def a_h3(g):
                dve.wait_ge(g_pool.sem, g_pool.value(g, "rs3"))
                dve.wait_ge(g_dve.sem, g_dve.value(g, ("n3", GT - 1)))
                if not first(g):
                    dve.wait_ge(g_pe.sem, g_pe.value(g - 1, "t_h3"))
                for n in range(GT):
                    dve.scalar_tensor_tensor(H3[:, n, :], N3[:, n, :], RS[:, 1, n:n + 1], MOD[:, 3, :],
                                             ALU.mult, ALU.add).then_inc(g_dve.sem, g_dve.step(("h3", n)))
                    yield

            def a_top2(g):
                dve.wait_ge(g_pe.sem, g_pe.value(g, "logits"))
                dve.tensor_copy(LG[:], pC[:, 0:GT * E].rearrange("p (n e) -> p n e", e=E)) \
                    .then_inc(g_dve.sem, g_dve.step("lg"))
                yield
                wait_apart(g_dve.sem, g_dve.value(g, "lg"))
                for n in range(GT):
                    dve.max(MX[:, n, :], LG[:, n, :]).then_inc(g_dve.sem, g_dve.step(("mx", n)))
                    yield
                wait_apart(g_dve.sem, g_dve.value(g, ("mx", GT - 1)))
                for n in range(GT):
                    dve.max_index(IX[:, n, :], MX[:, n, :], LG[:, n, :]).then_inc(g_dve.sem, g_dve.step(("ix", n)))
                    yield
                dve.tensor_tensor(DF[:], MX[:, :, 0], MX[:, :, 1], ALU.subtract).then_inc(g_dve.sem, g_dve.step("df"))
                yield
                dve.wait_ge(g_dve.sem, g_dve.value(g, ("ix", GT - 1)))
                dve.tensor_copy(IXF[:], IX[:, :, 0:2]).then_inc(g_dve.sem, g_dve.step("ixf"))
                yield

            def a_weights(g):
                dve.wait_ge(g_act.sem, g_act.value(g, "th"))
                dve.tensor_scalar(PR[:, :, 0], TH[:], 0.5, 0.5, ALU.mult, ALU.add) \
                    .then_inc(g_dve.sem, g_dve.step("p1"))
                yield
                dve.tensor_scalar(PR[:, :, 1], TH[:], -0.5, 0.5, ALU.mult, ALU.add) \
                    .then_inc(g_dve.sem, g_dve.step("p2"))
                yield
                dve.wait_ge(g_dve.sem, g_dve.value(g, "p2"))
                for n in range(GT):
                    for k in range(2):
                        dve.tensor_scalar(WA[:, k, n, :], IOTA[:], IXF[:, n, k:k + 1], PR[:, n, k:k + 1],
                                                     ALU.is_equal, ALU.mult) \
                            .then_inc(g_dve.sem, g_dve.step(("w", n, k)))
                        yield
                dve.wait_ge(g_dve.sem, g_dve.value(g, ("w", 1, 1)))
                dve.tensor_tensor(WT[:], WA[:, 0], WA[:, 1], ALU.add).then_inc(g_dve.sem, g_dve.step("wt"))
                yield

            def weights_in(g):
                if not first(g):
                    dve.wait_ge(w_act.sem, w_act.value(g - 1, (E - 1, GT - 1)))
                dve.wait_ge(g_dve.sem, g_dve.value(g, "wt"))
                dve.tensor_copy(WE[:], WT[:]).then_inc(we_dve.sem, we_dve.step("we"))
                yield

            def hidden_half(g, e, both):
                if e >= 2:
                    dve.wait_ge(p_pe.sem, p_pe.value(g, e - 2))
                elif not first(g):
                    dve.wait_ge(p_pe.sem, p_pe.value(g - 1, E - 2 + e))
                dve.wait_ge(s_act.sem, s_act.value(g, ("silu", e)))
                dve.tensor_tensor(HT[:, e % 2, 0, :], SL[:, e % 2, 0:GN], pH3[e % 2][:, 0:GN], ALU.mult) \
                    .then_inc(m_first.sem, m_first.step(e))
                yield
                if both:
                    dve.tensor_tensor(HT[:, e % 2, 1, :], SL[:, e % 2, GN:], H3V[:, e % 2, :], ALU.mult) \
                        .then_inc(m_last, 1)
                    yield

            def side_work(t, half, slot):
                rec, att, gate, _ = groups(t)
                if att is not None:
                    if first(att) and slot == 2:
                        yield from largest_k(NQ - 1)
                        yield from range_check()
                    if first(att) and slot == 3:
                        choose_path()
                    if first(att) and slot == 3:
                        for h in range(2):
                            yield from y_records(att, 1 - half, h)
                            yield from y_scan(att, h)
                            yield from y_reciprocal(att, h)
                            yield from y_att(att, h)
                    if not first(att):
                        if slot == 0:
                            yield from y_records(att, 1 - half, 1)
                        if slot == 2:
                            yield from y_scan(att, 1)
                            yield from y_reciprocal(att, 1)
                        if slot == 3:
                            yield from y_att(att, 1)
                    if slot == (9 if first(att) else 4):
                        yield from a_x1(att)
                    if slot == (11 if first(att) else 6):
                        yield from a_x2(att)
                    if slot == (15 if first(att) else 12):
                        yield from a_mixed(att)
                    if slot == (15 if first(att) else 15):
                        yield from a_stats3(att)
                if rec is not None:
                    if slot == 9:
                        yield from y_records(rec, half, 0)
                    if slot == 11:
                        yield from y_scan(rec, 0)
                    if slot == 13:
                        yield from y_reciprocal(rec, 0)
                    if slot == 14:
                        yield from y_att(rec, 0)
                if gate is not None:
                    if slot == 1:
                        yield from a_n3(gate)
                        yield from a_h3(gate)
                    if slot == 5:
                        yield from a_top2(gate)
                    if slot == 7:
                        yield from a_weights(gate)
                        yield from weights_in(gate)

            def turn(t, half):
                rec, _, _, _ = groups(t)
                side = iter(())
                for slot in range(SLOTS):
                    g, e = expert(t, slot // 2)
                    urgent = hidden_half(g, e, rec is None) if slot % 2 == 0 and g is not None else ()
                    side = chain(urgent, side, side_work(t, half, slot))
                    if rec is not None:
                        wkv_steps(rec, half, slot * GS // SLOTS, (slot + 1) * GS // SLOTS, side)
                    else:
                        for _ in side:
                            pass
                for _ in side:
                    pass

            def general_path():
                count = [0]
                per = 17
                dve.memset(sPP[:], PP_START)
                dve.memset(sAA[:], 0.0)
                dve.memset(sBB[:], 1.0).then_inc(slow_copy, 1)
                dve.wait_ge(slow_copy, 1)
                dve.sem_clear(slow_copy)
                with dve.Fori(0, T) as t:
                    kt, vt = K[:, cols(t, B)], V[:, cols(t, B)]

                    def link(ins):
                        count[0] += 1
                        ins.then_inc(slow_dve, 1)
                        if count[0] == per:
                            wait_apart(slow_dve, t * per + count[0])
                        else:
                            dve.wait_ge(slow_dve, t * per + count[0])

                    link(dve.tensor_tensor(sM[:], sPP[:], kt, ALU.max))
                    link(dve.scalar_tensor_tensor(sP[:], kt, u_v, sPP[:], ALU.add, ALU.max))
                    link(dve.tensor_tensor(sD[:, 0], sPP[:], sP[:], ALU.subtract))
                    link(dve.scalar_tensor_tensor(sD[:, 1], kt, u_v, sP[:], ALU.add, ALU.subtract))
                    link(dve.tensor_tensor(sD[:, 2], sPP[:], sM[:], ALU.subtract))
                    link(dve.tensor_tensor(sD[:, 3], kt, sM[:], ALU.subtract))
                    link(dve.tensor_scalar(sT[:, 8], sM[:], w_v, None, ALU.add))
                    dve.wait_ge(slow_act, t * 2 + 1)
                    link(dve.tensor_tensor(sT[:, 0:2], sE[:, 0:4:2], sAA[:].rearrange("p (o b) -> p o b", o=1)
                                           .broadcast_to((P, 2, B)), ALU.mult))
                    link(dve.tensor_tensor(sT[:, 2:4], sE[:, 1:4:2], vt.rearrange("p (o b) -> p o b", o=1)
                                           .broadcast_to((P, 2, B)), ALU.mult))
                    link(dve.tensor_tensor(sT[:, 4:6], sE[:, 0:4:2], sBB[:].rearrange("p (o b) -> p o b", o=1)
                                           .broadcast_to((P, 2, B)), ALU.mult))
                    link(dve.tensor_tensor(sT[:, 0], sT[:, 0], sT[:, 2], ALU.add))
                    link(dve.tensor_tensor(sAA[:], sT[:, 1], sT[:, 3], ALU.add))
                    link(dve.tensor_tensor(sT[:, 6], sT[:, 4], sE[:, 1], ALU.add))
                    link(dve.reciprocal(sT[:, 7], sT[:, 6]))
                    link(dve.tensor_tensor(vt, sT[:, 0], sT[:, 7], ALU.mult))
                    link(dve.tensor_tensor(sBB[:], sT[:, 5], sE[:, 3], ALU.add))
                    dve.wait_ge(slow_act, t * 2 + 2)
                    link(dve.tensor_tensor(sPP[:], sT[:, 8], sL[:], ALU.add))
                    assert count[0] == per
                dve.memset(REC[:], NOTHING).then_inc(slow_copy, 1)
                dve.memset(Q[:], NOTHING).then_inc(slow_copy, 1)
                dve.memset(UE[:], 1.0).then_inc(slow_copy, 1)
                dve.wait_ge(slow_copy, 3)
                for field, value in ((RG, 1.0), (RBB, 1.0), (RINV, 1.0 / NOTHING)):
                    for half in range(2):
                        dve.memset(REC[:, half, :, field, :], value).then_inc(slow_copy, 1)
                dve.wait_ge(slow_copy, 9)

            dve.wait_ge(pool_const.sem, pool_const.value(0, "rest"))
            dve.wait_ge(x_first, 16 * QT)
            for _ in stats(0):
                pass
            modulation()
            for _ in chain(modulated(0), normed(0)):
                pass
            rest_of_modulation()
            first_difference()
            dve.wait_ge(q_act.sem, q_act.value(0, "first"))
            dve.wait_ge(wkv_start.sem, wkv_start.value(0, "inv"))
            dve.tensor_copy(REC[:, 0, 0, RQ, :], Q[:, 0:B]).then_inc(wkv_start.sem, wkv_start.step("q"))
            side = rest_of_first_stage()
            wkv_steps(0, 0, 0, GS, side)
            for _ in side:
                pass
            for t in range(1, FIRST_FULL):
                turn(t, t % 2)
            with dve.Fori(FIRST_FULL // 2, NG // 2) as pair:
                turn(pair * 2, 0)
                turn(pair * 2 + 1, 1)
            for t in range(NG, TURNS):
                turn(t, t % 2)

        @block.tensor
        def _(pe):
            pe.wait_ge(pool_const.sem, pool_const.value(0, "ident"))
            pe.wait_ge(mod_act.sem, mod_act.value(0, "silu"))
            pe.transpose(pB[:, 0:B], CS[:], ident[0:B, 0:B]).then_inc(mod_pe.sem, mod_pe.step("ct"))
            pe.wait_ge(mod_act.sem, mod_act.value(0, "ct"))
            pe.wait_ge(wmod_first, 16)
            pe.matmul(pH3[1][:, 0:2 * C], CT[:], WMOD[:, 0:2 * C], start=True, stop=True) \
                .then_inc(mod_pe.sem, mod_pe.step("first"))
            pe.wait_ge(wmod_rest, 16)
            pe.matmul(pY[:], CT[:], WMOD[:, 2 * C:], start=True, stop=True).then_inc(mod_pe.sem, mod_pe.step("rest"))
            pe.wait_ge(wkvr_in, 48)
            pe.wait_ge(shift_set, 1)

            def first_stage(q):
                if not first(q):
                    pe.wait_ge(ln_act.sem, ln_act.value(q - 1, "r"))
                for n in range(QT):
                    pe.wait_ge(ln2_dve.sem, ln2_dve.value(q, ("n", n)))
                    ins = pe.transpose(pA[:, n * P:(n + 1) * P], HN[:, n, :], ident[:])
                ins.then_inc(ln_pe.sem, ln_pe.step("t"))
                pe.wait_ge(ln_act.sem, ln_act.value(q, "hs"))
                for w, p, name in ((WK, pH1[0], "k"), (WV, pH3[0], "v"), (WR, pH1[1], "r")):
                    pe.matmul(p[:], w[:], HSh[:, cols(q, QN)], start=True, stop=True) \
                        .then_inc(ln_pe.sem, ln_pe.step(name))

            first_stage(0)
            with pe.Fori(1, NQ) as q:
                first_stage(q)
            for s in (w1_in, w3_in, w2_in):
                pe.wait_ge(s, 16)
            pe.wait_ge(mix_in, 16 * 4)
            pe.wait_ge(mod_dve.sem, mod_dve.value(0, "rest"))
            pe.wait_ge(ln_act.sem, ln_act.value(NQ - 1, "r"))

            def to_tokens(src, dst):
                for n in range(GT):
                    ins = pe.transpose(dst[:, n * P:(n + 1) * P], src(n), ident[:])
                return ins

            def a_att(g):
                if not first(g):
                    pe.wait_ge(g_dve.sem, g_dve.value(g - 1, "t1"))
                pe.wait_ge(y_dve.sem, y_dve.value(g * 2 + 1, "att"))
                to_tokens(lambda n: ATT[:, n * P:(n + 1) * P], pA).then_inc(a_pe.sem, a_pe.step("t_att"))

            def a_x2(g):
                pe.wait_ge(a_dve.sem, a_dve.value(g, ("n", GT - 1)))
                to_tokens(lambda n: X2N[:, n, :], pA).then_inc(a_pe.sem, a_pe.step("t_x2"))

            def a_mix(g):
                pe.wait_ge(a_act.sem, a_act.value(g, "hs2"))
                for n in range(GT):
                    ins = pe.matmul(pA[:, n * C:(n + 1) * C], HS2[:, n * P:(n + 1) * P], WCR[:], start=True, stop=True)
                ins.then_inc(a_pe.sem, a_pe.step("rr"))
                if not first(g):
                    pe.wait_ge(g_dve.sem, g_dve.value(g - 1, "lg"))
                a_half(0)

            def a_half(i):
                for m in range(FM // 2):
                    f = i * FM // 2 + m
                    ins = pe.matmul((pB, pC)[i][:, m * GN:(m + 1) * GN], WCK[:, f * P:(f + 1) * P], HS2[:, 0:GN],
                                    start=True, stop=True)
                ins.then_inc(a_pe.sem, a_pe.step(f"kk{i}"))

            def a_kv(g):
                pe.wait_ge(a_act.sem, a_act.value(g, "rr"))
                for n in range(GT):
                    for f in range(FM):
                        if n == 0 and f in (0, FM // 2):
                            pe.wait_ge(a_act.sem, a_act.value(g, "sq0" if f == 0 else "sq1"))
                        ins = pe.matmul(pA[:, n * C:(n + 1) * C], KQ[:, f, n * P:(n + 1) * P], WCV[:, f, :],
                                        start=(f == 0), stop=(f == FM - 1))
                ins.then_inc(a_pe.sem, a_pe.step("kv"))

            def a_h3(g):
                pe.wait_ge(g_dve.sem, g_dve.value(g, ("h3", GT - 1)))
                to_tokens(lambda n: H3[:, n, :], pB).then_inc(g_pe.sem, g_pe.step("t_h3"))

            def a_logits(g):
                pe.wait_ge(g_act.sem, g_act.value(g, "h3s"))
                for n in range(GT):
                    ins = pe.matmul(pC[:, n * E:(n + 1) * E], H3S[:, n * P:(n + 1) * P], WG[:], start=True, stop=True)
                ins.then_inc(g_pe.sem, g_pe.step("logits"))

            def hidden(g, e):
                if e == 0:
                    pe.wait_ge(g_act.sem, g_act.value(g, "h3t"))
                if e >= 2:
                    pe.wait_ge(m_first.sem, m_first.value(g, e - 2))
                    pe.wait_ge(*second_half(g, e - 2))
                elif not first(g):
                    pe.wait_ge(m_first.sem, m_first.value(g - 1, E - 2 + e))
                    pe.wait_ge(*second_half(g - 1, E - 2 + e))
                for w, p in ((W1, pH1[e % 2]), (W3, pH3[e % 2])):
                    for m in range(HM):
                        ins = pe.matmul(p[:, m * GN:(m + 1) * GN], w[:, e, m * P:(m + 1) * P], H3T[:, cols(g)],
                                        start=True, stop=True)
                ins.then_inc(h_pe.sem, h_pe.step(e))

            def project(g, e):
                pe.wait_ge(m_first.sem, m_first.value(g, e))
                pe.wait_ge(*second_half(g, e))
                if e >= 1:
                    pe.wait_ge(w_act.sem, w_act.value(g, (e - 1, GT - 1)))
                elif not first(g):
                    pe.wait_ge(w_act.sem, w_act.value(g - 1, (E - 1, GT - 1)))
                for n in range(GT):
                    for m in range(HM):
                        ins = pe.matmul(pY[:, n * C:(n + 1) * C], HT[:, e % 2, m, n * P:(n + 1) * P], W2[:, e, m, :],
                                        start=(m == 0), stop=(m == HM - 1))
                ins.then_inc(p_pe.sem, p_pe.step(e))

            def turn(t):
                _, att, gate, _ = groups(t)
                for slot in range(SLOTS):
                    if slot == 4 and gate is not None:
                        a_logits(gate)
                    g, e = expert(t, slot // 2) if slot % 2 else ahead(t, slot // 2)
                    if g is not None:
                        if slot % 2:
                            project(g, e)
                        else:
                            hidden(g, e)
                    if slot == 2 and gate is not None:
                        a_h3(gate)
                    if slot == 3 and att is not None:
                        a_att(att)
                    if slot == 6 and att is not None:
                        a_x2(att)
                    if slot == 7 and att is not None:
                        a_mix(att)
                    if slot == 8 and att is not None:
                        a_half(1)
                    if slot == 10 and att is not None:
                        a_kv(att)

            for t in range(1, FIRST_FULL):
                turn(t)
            with pe.Fori(FIRST_FULL, NG) as t:
                turn(t)
            for t in range(NG, TURNS):
                turn(t)


_INS = ['L0_attn_x', 'L0_attn_time_decay', 'L0_attn_time_first', 'L0_attn_time_shift', 'L0_attn_Wk', 'L0_attn_Wv',
        'L0_attn_Wr', 'L0_attn_Wck', 'L0_attn_Wcv', 'L0_attn_Wcr', 'L0_attn_ln1_g', 'L0_attn_ln1_b', 'L0_attn_ln2_g',
        'L0_attn_ln2_b', 'L0_ffn_w_gate', 'L0_ffn_w1', 'L0_ffn_w3', 'L0_ffn_w2', 'L0_c', 'L0_wmod']
_OUTS = [((8, 256, 128), 'float32')]


def kernel(**inputs):
    import numpy as _np
    import concourse.bacc as _bacc
    from concourse import mybir as _mybir
    from concourse.bass_utils import run_bass_kernel_spmd as _run

    nc = _bacc.Bacc("TRN2", target_bir_lowering=False, num_devices=1)
    arrays, args = {}, []
    for name in _INS:
        a = _np.ascontiguousarray(inputs[name])
        arrays[f"in_{name}_dram"] = a
        args.append(nc.dram_tensor(f"in_{name}_dram", a.shape, _mybir.dt.from_np(a.dtype), kind="ExternalInput").ap())
    for i, (shape, dtype) in enumerate(_OUTS):
        dt = _mybir.dt.from_np(_np.dtype(dtype))
        args.append(nc.dram_tensor(f"out_{i}_dram", shape, dt, kind="ExternalOutput").ap())
    adaln_rwkv_moe(nc, *args)
    r = _run(nc, [arrays], core_ids=[0])
    got = tuple(r.results[0][f"out_{i}_dram"] for i in range(len(_OUTS)))
    return got[0]
```
